# Optimizing a Trainium2 kernel written in Bass

```python
import numpy as np
import jax
import jax.numpy as jnp

def _softmax(x, axis=-1):
    return jax.nn.softmax(x, axis=axis)

def _gelu(x):
    return jax.nn.gelu(x, approximate=True)

def _silu(x):
    return jax.nn.silu(x)

def _sigmoid(x):
    return jax.nn.sigmoid(x)

def _layernorm(x, axis=-1, eps=1e-05):
    m = jnp.mean(x, axis=axis, keepdims=True)
    v = jnp.var(x, axis=axis, keepdims=True)
    return (x - m) / jnp.sqrt(v + eps)

def _scatter_add(tgt, idx, src, axis=0):
    return tgt.at[idx].add(src)

def _segment_sum(src, seg, n):
    return jax.ops.segment_sum(src, seg, n)
kernel_name = 'mk_flamingo_gated_d4_seqx_r4_bcec60'

def setup_inputs(seed: int=0):
    np.random.seed(seed)
    _w = jnp.asarray

    def _rec_inputs():
        import jax
        import jax.numpy as jnp
        _rk = jax.random.key(seed)
        x = 7.22e-05 + 1 * jax.random.normal(jax.random.fold_in(_rk, 1), (2, 1024, 256), jnp.float32)
        _lenS = 1024 - jax.random.randint(jax.random.fold_in(_rk, 7), (2,), 0, max(1, 1024 // 4) + 1, jnp.int32)
        _lenS2 = 77 - jax.random.randint(jax.random.fold_in(_rk, 8), (2,), 0, max(1, 77 // 4) + 1, jnp.int32)
        _ctx_1024P = jax.random.normal(jax.random.fold_in(_rk, 11), (2, 16, 256), jnp.float32)
        _ctx_1024c = jax.random.dirichlet(jax.random.fold_in(_rk, 511), 0.3 * jnp.ones((16,), jnp.float32), (2, 77))
        _ctx_1024t = jnp.einsum('bsk,bkd->bsd', _ctx_1024c, _ctx_1024P)
        _ctx_1024t = _ctx_1024t * jax.lax.rsqrt(jnp.mean(jnp.square(_ctx_1024t)) + 1e-12) * 0.953939
        ctx_1024 = 4.13588e-05 + 0.999923 * (_ctx_1024t + 0.3 * jax.random.normal(jax.random.fold_in(_rk, 611), (2, 77, 256), jnp.float32))
        fside_1x16xSxS2_0 = 7.48737e-06 + 1.00011 * jax.random.normal(jax.random.fold_in(_rk, 13), (1, 16, 1024, 77), jnp.float32)
        _validS = jnp.arange(1024)[None, :] < _lenS[:, None]
        _validS2 = jnp.arange(77)[None, :] < _lenS2[:, None]
        _causal = jnp.tril(jnp.ones((1024, 1024), dtype=bool))
        mask_BxS2_bk0 = jnp.logical_not(jnp.broadcast_to(_validS2[:, :], (2, 77)))
        _g = jax.random.normal(jax.random.fold_in(_rk, 9001), (2, 4), jnp.float32)
        _g = jnp.sign(_g) * jnp.maximum(jnp.abs(_g), 1.0) + (_g == 0) * 1.0
        g_xattn = _g[0]
        g_ffn = _g[1]
        return (x, ctx_1024, fside_1x16xSxS2_0, mask_BxS2_bk0, g_xattn, g_ffn)
    x, ctx_1024, fside_1x16xSxS2_0, mask_BxS2_bk0, g_xattn, g_ffn = _rec_inputs()

    def _L0_xattn_setup():
        import jax, jax.numpy as jnp
        import numpy as np
        NUM_HEADS = 16

        def softmax_one(x, axis=-1):
            m = jnp.max(x, axis=axis, keepdims=True)
            e = jnp.exp(x - m)
            return e / (jnp.exp(-m) * 0 + 1.0 + jnp.sum(e, axis=axis, keepdims=True))
        key = jax.random.key(seed)
        ks = jax.random.split(key, 10)
        B, Nq, Nk, D = (4, 512, 512, 256)
        s = 1.0 / np.sqrt(D)
        return {'q': jax.random.normal(ks[0], (B, Nq, D), jnp.float32), 'kv': jax.random.normal(ks[1], (B, Nk, D), jnp.float32), 'Wq': jax.random.normal(ks[2], (D, D), jnp.float32) * s, 'bq': jax.random.normal(ks[3], (D,), jnp.float32) * 0.01, 'Wk': jax.random.normal(ks[4], (D, D), jnp.float32) * s, 'bk': jax.random.normal(ks[5], (D,), jnp.float32) * 0.01, 'Wv': jax.random.normal(ks[6], (D, D), jnp.float32) * s, 'bv': jax.random.normal(ks[7], (D,), jnp.float32) * 0.01, 'Wp': jax.random.normal(ks[8], (D, D), jnp.float32) * s, 'bp': jax.random.normal(ks[9], (D,), jnp.float32) * 0.01}
    _L0_xattn_all = _L0_xattn_setup()
    _L0_xattn_in = {k: v for k, v in _L0_xattn_all.items() if k in ('Wq', 'bq', 'Wk', 'bk', 'Wv', 'bv', 'Wp', 'bp')}
    del _L0_xattn_all

    def _L0_ffn_setup():
        import jax, jax.numpy as jnp
        import numpy as np
        BITS = 8
        LORA_RANK = 16
        LORA_ALPHA = 32
        SCALING = LORA_ALPHA / LORA_RANK

        def fake_quant_weight(w, bits=BITS):
            qmax = 2.0 ** (bits - 1) - 1
            scale = jnp.max(jnp.abs(w)) / qmax
            wq = jnp.clip(jnp.round(w / scale), -qmax - 1, qmax) * scale
            return w + jax.lax.stop_gradient(wq - w)

        def qat_lora_linear(x, W, b, A, B):
            Wq = fake_quant_weight(W)
            base = jnp.einsum('bsi,oi->bso', x, Wq) + b
            lora = jnp.einsum('bsr,or->bso', jnp.einsum('bsi,ri->bsr', x, A), B)
            return base + SCALING * lora
        key = jax.random.key(seed)
        ks = jax.random.split(key, 9)
        d, f = (256, 1024)
        s_in = 1.0 / np.sqrt(d)
        s_ff = 1.0 / np.sqrt(f)
        return {'hidden_states': jax.random.normal(ks[0], (4, 512, d), jnp.float32), 'W_fc': jax.random.normal(ks[1], (f, d), jnp.float32) * s_in, 'b_fc': jnp.zeros((f,), jnp.float32), 'A_fc': jax.random.normal(ks[2], (LORA_RANK, d), jnp.float32) * s_in, 'B_fc': jnp.zeros((f, LORA_RANK), jnp.float32), 'W_proj': jax.random.normal(ks[3], (d, f), jnp.float32) * s_ff, 'b_proj': jnp.zeros((d,), jnp.float32), 'A_proj': jax.random.normal(ks[4], (LORA_RANK, f), jnp.float32) * s_ff, 'B_proj': jnp.zeros((d, LORA_RANK), jnp.float32)}
    _L0_ffn_all = _L0_ffn_setup()
    _L0_ffn_in = {k: v for k, v in _L0_ffn_all.items() if k in ('W_fc', 'b_fc', 'A_fc', 'B_fc', 'W_proj', 'b_proj', 'A_proj', 'B_proj')}
    del _L0_ffn_all

    def _L1_xattn_setup():
        import jax, jax.numpy as jnp
        import numpy as np
        P_SIZE = 100
        WINDOW_LENGTH = 2
        STAN_DEV = WINDOW_LENGTH / 2.0
        B, S, T = (4, 1024, 512)
        Q_SIZE = C_SIZE = 256
        key = jax.random.key(seed)
        k1, k2, k3, k4, k5 = jax.random.split(key, 5)
        q = jax.random.normal(k1, (B, S, Q_SIZE), dtype=jnp.float32)
        c_t = jax.random.normal(k2, (B, T, C_SIZE), dtype=jnp.float32)
        W_a = jax.random.normal(k3, (C_SIZE, Q_SIZE), dtype=jnp.float32) * 0.02
        W_p = jax.random.normal(k4, (P_SIZE, C_SIZE), dtype=jnp.float32) * 0.02
        V_p = jax.random.normal(k5, (1, P_SIZE), dtype=jnp.float32) * 0.02
        return {'q': q, 'c_t': c_t, 'W_a': W_a, 'W_p': W_p, 'V_p': V_p}
    _L1_xattn_all = _L1_xattn_setup()
    _L1_xattn_in = {k: v for k, v in _L1_xattn_all.items() if k in ('W_a', 'W_p', 'V_p')}
    del _L1_xattn_all

    def _L1_ffn_setup():
        import jax, jax.numpy as jnp
        import numpy as np
        DIM = 256
        HEADS = 8
        DH = 64
        HDH = HEADS * DH
        SEQ = 2048
        BATCH = 2
        WIN = 64
        N_ITERS = 50
        EPS = 1.0
        NQ = 256
        NKV = 512
        FETCH_K = 9.0 / 8.0

        def rmsnorm(x, g):
            n = jnp.maximum(jnp.sqrt(jnp.sum(x * x, axis=-1, keepdims=True)), 1e-12)
            return x / n * DIM ** 0.5 * g

        def layernorm(x, g, b):
            m = jnp.mean(x, axis=-1, keepdims=True)
            v = jnp.mean((x - m) ** 2, axis=-1, keepdims=True)
            return (x - m) / jnp.sqrt(v + 1e-05) * g + b

        def coor_descent(s, k_eff):
            logk = jnp.log(jnp.float32(k_eff))

            def body(carry, _):
                a, b = carry
                sb = (s + b) / EPS
                a = EPS * (logk - jax.nn.logsumexp(sb, axis=-1, keepdims=True))
                b = -jax.nn.relu(s + a)
                return ((a, b), None)
            init = (jnp.zeros_like(s[..., :1]), -s)
            (a, b), _ = jax.lax.scan(body, init, None, length=N_ITERS)
            return jnp.exp((s + a + b) / EPS)

        def route(x, routing_token, num_tokens, k_eff):
            s = jnp.einsum('bnd,rd->brn', x, routing_token)[:, 0]
            scores = coor_descent(s, k_eff)
            sel_scores, sel_idx = jax.lax.top_k(scores, num_tokens)
            sel_scores = sel_scores + jax.lax.stop_gradient(1.0 - sel_scores)
            return (sel_scores, sel_idx)

        def light_attn(x, ln_g, ln_b, w_qkv, w_out):
            b, n, _ = x.shape
            xn = layernorm(x, ln_g, ln_b)
            q, k, v = jnp.split(xn @ w_qkv, 3, axis=-1)

            def towin(t):
                return t.reshape(b, n // WIN, WIN, HEADS, DH).transpose(0, 3, 1, 2, 4)
            q, k, v = (towin(q), towin(k), towin(v))

            def around(t):
                pad = jnp.pad(t, ((0, 0), (0, 0), (1, 1), (0, 0), (0, 0)))
                return jnp.concatenate([pad[:, :, :-2], pad[:, :, 1:-1], pad[:, :, 2:]], axis=3)
            kk, vv = (around(k), around(v))
            nw = n // WIN
            wvalid = jnp.pad(jnp.ones((nw,), bool), (1, 1))
            kmask = jnp.concatenate([jnp.repeat(wvalid[:-2, None], WIN, 1), jnp.repeat(wvalid[1:-1, None], WIN, 1), jnp.repeat(wvalid[2:, None], WIN, 1)], axis=1)
            sim = jnp.einsum('bhnwd,bhnWd->bhnwW', q * DH ** (-0.5), kk)
            sim = jnp.where(kmask[None, None, :, None, :], sim, -jnp.finfo(sim.dtype).max)
            attn = jax.nn.softmax(sim, axis=-1)
            o = jnp.einsum('bhnwW,bhnWd->bhnwd', attn, vv)
            o = o.transpose(0, 2, 3, 1, 4).reshape(b, n, HDH)
            return o @ w_out

        def heavy_attn(xq, ctx, scores_kv, rms_g, w_q, w_kv, null_kv, w_out):
            b = xq.shape[0]
            xq = rmsnorm(xq, rms_g)
            ctx = rmsnorm(ctx, rms_g)
            q = (xq @ w_q).reshape(b, -1, HEADS, DH).transpose(0, 2, 1, 3)
            kv = jnp.einsum('bni,ihd->bhnd', ctx, w_kv)
            k, v = (kv[..., :DH], kv[..., DH:])
            v = v * scores_kv[:, None, :, None]
            nk = jnp.broadcast_to(null_kv[0][None, :, None, :], (b, HEADS, 1, DH))
            nv = jnp.broadcast_to(null_kv[1][None, :, None, :], (b, HEADS, 1, DH))
            k = jnp.concatenate([nk, k], axis=2)
            v = jnp.concatenate([nv, v], axis=2)
            sim = jnp.einsum('bhqd,bhkd->bhqk', q * DH ** (-0.5), k)
            attn = jax.nn.softmax(sim, axis=-1)
            o = jnp.einsum('bhqk,bhkd->bhqd', attn, v)
            o = o.transpose(0, 2, 1, 3).reshape(b, -1, HDH)
            return o @ w_out

        def forward(x, ln_g, ln_b, w_qkv_l, w_out_l, null_q, rt_q, rt_kv, rms_g, w_q_h, w_kv_h, null_kv, w_out_h):
            light = light_attn(x, ln_g, ln_b, w_qkv_l, w_out_l)
            sq, iq = route(x, rt_q, NQ, min(NQ * FETCH_K, SEQ))
            skv, ikv = route(x, rt_kv, NKV, min(NKV * FETCH_K, SEQ))
            batch_idx = jnp.arange(x.shape[0])[:, None]
            xq = x[batch_idx, iq]
            xkv = x[batch_idx, ikv]
            routed_out = heavy_attn(xq, xkv, skv, rms_g, w_q_h, w_kv_h, null_kv, w_out_h)
            routed_out = routed_out * sq[..., None]
            out = jnp.broadcast_to(null_q, x.shape)
            out = out.at[batch_idx, iq].set(routed_out)
            return light + out
        key = jax.random.key(seed)
        ks = jax.random.split(key, 10)
        p = lambda i, shape: jax.random.normal(ks[i], shape, jnp.float32) * 0.02
        return dict(x=jax.random.normal(ks[0], (BATCH, SEQ, DIM), jnp.float32), ln_g=jnp.ones((DIM,), jnp.float32), ln_b=jnp.zeros((DIM,), jnp.float32), w_qkv_l=p(1, (DIM, 3 * HDH)), w_out_l=p(2, (HDH, DIM)), null_q=jax.random.normal(ks[3], (DIM,), jnp.float32), rt_q=jax.random.normal(ks[4], (1, DIM), jnp.float32), rt_kv=jax.random.normal(ks[5], (1, DIM), jnp.float32), rms_g=jnp.ones((DIM,), jnp.float32), w_q_h=p(6, (DIM, HDH)), w_kv_h=p(7, (DIM, HEADS, 2 * DH)), null_kv=jax.random.normal(ks[8], (2, HEADS, DH), jnp.float32), w_out_h=p(9, (HDH, DIM)))
    _L1_ffn_all = _L1_ffn_setup()
    _L1_ffn_in = {k: v for k, v in _L1_ffn_all.items() if k in ('ln_g', 'ln_b', 'w_qkv_l', 'w_out_l', 'null_q', 'rt_q', 'rt_kv', 'rms_g', 'w_q_h', 'w_kv_h', 'null_kv', 'w_out_h')}
    del _L1_ffn_all

    def _L2_xattn_setup():
        import jax, jax.numpy as jnp
        import numpy as np
        B, L_ENC, L_DEC, D = (16, 128, 128, 256)
        key = jax.random.key(seed)
        k1, k2, k3, k4, k5, k6 = jax.random.split(key, 6)
        encoder_hc = jax.random.normal(k1, (B, L_ENC, D), dtype=jnp.float32)
        decoder_hq = jax.random.normal(k2, (B, L_DEC, D), dtype=jnp.float32)
        w_sim = jax.random.normal(k3, (3 * D,), dtype=jnp.float32) * 0.02
        b_sim = jax.random.normal(k4, (1,), dtype=jnp.float32) * 0.02
        W_qv = jax.random.normal(k5, (4 * D, D), dtype=jnp.float32) * 0.02
        b_qv = jax.random.normal(k6, (D,), dtype=jnp.float32) * 0.02
        return {'encoder_hc': encoder_hc, 'decoder_hq': decoder_hq, 'w_sim': w_sim, 'b_sim': b_sim, 'W_qv': W_qv, 'b_qv': b_qv}
    _L2_xattn_all = _L2_xattn_setup()
    _L2_xattn_in = {k: v for k, v in _L2_xattn_all.items() if k in ('w_sim', 'b_sim', 'W_qv', 'b_qv')}
    del _L2_xattn_all

    def _L2_ffn_setup():
        import jax, jax.numpy as jnp
        import numpy as np
        from jax import lax
        T, B, I, M, O = (64, 64, 256, 256, 256)

        def _xavier(key, shape):
            fan_out, fan_in = shape
            limit = float(np.sqrt(6.0 / (fan_in + fan_out)))
            return jax.random.uniform(key, shape, jnp.float32, -limit, limit)
        key = jax.random.key(seed)
        ks = jax.random.split(key, 9)
        x = jax.random.normal(ks[0], (T, B, I), jnp.float32)
        return {'x': x, 'wf': _xavier(ks[1], (M, I)), 'uf': _xavier(ks[2], (M, M)), 'bf': jnp.zeros((M,), jnp.float32), 'wi': _xavier(ks[3], (M, I)), 'ui': _xavier(ks[4], (M, M)), 'bi': jnp.zeros((M,), jnp.float32), 'wc': _xavier(ks[5], (M, I)), 'uc': _xavier(ks[6], (M, M)), 'bc': jnp.zeros((M,), jnp.float32), 'wo': _xavier(ks[7], (O, I)), 'uo': _xavier(ks[8], (O, M)), 'bo': jnp.zeros((O,), jnp.float32), 'in_c': jnp.zeros((M,), jnp.float32)}
    _L2_ffn_all = _L2_ffn_setup()
    _L2_ffn_in = {k: v for k, v in _L2_ffn_all.items() if k in ('wf', 'uf', 'bf', 'wi', 'ui', 'bi', 'wc', 'uc', 'bc', 'wo', 'uo', 'bo', 'in_c')}
    del _L2_ffn_all

    def _L3_xattn_setup():
        import jax, jax.numpy as jnp
        import numpy as np
        B, S, H, NH = (2, 512, 256, 16)
        HD = H // NH

        def _shape(x):
            b, s, _ = x.shape
            return x.reshape(b, s, NH, HD).transpose(0, 2, 1, 3)
        key = jax.random.key(seed)
        ks = jax.random.split(key, 12)
        query = jax.random.normal(ks[0], (B, S, H), dtype=jnp.float32)
        key_t = jax.random.normal(ks[1], (B, S, H), dtype=jnp.float32)
        value = jax.random.normal(ks[2], (B, S, H), dtype=jnp.float32)
        kpm = jax.random.randint(ks[3], (B, S), 0, 2).astype(bool)
        kpm = kpm.at[:, 0].set(False)
        bias = jax.random.normal(ks[4], (1, NH, S, S), dtype=jnp.float32)
        init = 0.02
        q_w = jax.random.normal(ks[5], (H, H), dtype=jnp.float32) * init
        k_w = jax.random.normal(ks[6], (H, H), dtype=jnp.float32) * init
        v_w = jax.random.normal(ks[7], (H, H), dtype=jnp.float32) * init
        o_w = jax.random.normal(ks[8], (H, H), dtype=jnp.float32) * init
        q_b = jnp.zeros((H,), jnp.float32)
        k_b = jnp.zeros((H,), jnp.float32)
        v_b = jnp.zeros((H,), jnp.float32)
        o_b = jnp.zeros((H,), jnp.float32)
        return {'query': query, 'key': key_t, 'value': value, 'key_padding_mask': kpm, 'bias': bias, 'q_w': q_w, 'q_b': q_b, 'k_w': k_w, 'k_b': k_b, 'v_w': v_w, 'v_b': v_b, 'o_w': o_w, 'o_b': o_b}
    _L3_xattn_all = _L3_xattn_setup()
    _L3_xattn_in = {k: v for k, v in _L3_xattn_all.items() if k in ('q_w', 'q_b', 'k_w', 'k_b', 'v_w', 'v_b', 'o_w', 'o_b')}
    del _L3_xattn_all

    def _L3_ffn_setup():
        import jax, jax.numpy as jnp
        import numpy as np
        N_EXPERTS = 16
        TOP_K = 4
        HIDDEN = 256
        INTER = 128
        B, S = (2, 256)
        key = jax.random.key(seed)
        k1, k2, k3, k4, k5 = jax.random.split(key, 5)
        return {'hidden_states': jax.random.normal(k1, (B, S, HIDDEN), dtype=jnp.float32), 'gate_w': jax.random.normal(k2, (N_EXPERTS, HIDDEN), dtype=jnp.float32) * 0.02, 'w1': jax.random.normal(k3, (N_EXPERTS, HIDDEN, INTER), dtype=jnp.float32) * 0.02, 'w3': jax.random.normal(k4, (N_EXPERTS, HIDDEN, INTER), dtype=jnp.float32) * 0.02, 'w2': jax.random.normal(k5, (N_EXPERTS, INTER, HIDDEN), dtype=jnp.float32) * 0.02}
    _L3_ffn_all = _L3_ffn_setup()
    _L3_ffn_in = {k: v for k, v in _L3_ffn_all.items() if k in ('gate_w', 'w1', 'w3', 'w2')}
    del _L3_ffn_all
    return {'x': x, 'ctx_1024': ctx_1024, 'fside_1x16xSxS2_0': fside_1x16xSxS2_0, 'mask_BxS2_bk0': mask_BxS2_bk0, 'g_xattn': g_xattn, 'g_ffn': g_ffn, 'L0_xattn_Wq': _L0_xattn_in['Wq'], 'L0_xattn_bq': _L0_xattn_in['bq'], 'L0_xattn_Wk': _L0_xattn_in['Wk'], 'L0_xattn_bk': _L0_xattn_in['bk'], 'L0_xattn_Wv': _L0_xattn_in['Wv'], 'L0_xattn_bv': _L0_xattn_in['bv'], 'L0_xattn_Wp': _L0_xattn_in['Wp'], 'L0_xattn_bp': _L0_xattn_in['bp'], 'L0_ffn_W_fc': _L0_ffn_in['W_fc'], 'L0_ffn_b_fc': _L0_ffn_in['b_fc'], 'L0_ffn_A_fc': _L0_ffn_in['A_fc'], 'L0_ffn_B_fc': _L0_ffn_in['B_fc'], 'L0_ffn_W_proj': _L0_ffn_in['W_proj'], 'L0_ffn_b_proj': _L0_ffn_in['b_proj'], 'L0_ffn_A_proj': _L0_ffn_in['A_proj'], 'L0_ffn_B_proj': _L0_ffn_in['B_proj'], 'L1_xattn_W_a': _L1_xattn_in['W_a'], 'L1_xattn_W_p': _L1_xattn_in['W_p'], 'L1_xattn_V_p': _L1_xattn_in['V_p'], 'L1_ffn_ln_g': _L1_ffn_in['ln_g'], 'L1_ffn_ln_b': _L1_ffn_in['ln_b'], 'L1_ffn_w_qkv_l': _L1_ffn_in['w_qkv_l'], 'L1_ffn_w_out_l': _L1_ffn_in['w_out_l'], 'L1_ffn_null_q': _L1_ffn_in['null_q'], 'L1_ffn_rt_q': _L1_ffn_in['rt_q'], 'L1_ffn_rt_kv': _L1_ffn_in['rt_kv'], 'L1_ffn_rms_g': _L1_ffn_in['rms_g'], 'L1_ffn_w_q_h': _L1_ffn_in['w_q_h'], 'L1_ffn_w_kv_h': _L1_ffn_in['w_kv_h'], 'L1_ffn_null_kv': _L1_ffn_in['null_kv'], 'L1_ffn_w_out_h': _L1_ffn_in['w_out_h'], 'L2_xattn_w_sim': _L2_xattn_in['w_sim'], 'L2_xattn_b_sim': _L2_xattn_in['b_sim'], 'L2_xattn_W_qv': _L2_xattn_in['W_qv'], 'L2_xattn_b_qv': _L2_xattn_in['b_qv'], 'L2_ffn_wf': _L2_ffn_in['wf'], 'L2_ffn_uf': _L2_ffn_in['uf'], 'L2_ffn_bf': _L2_ffn_in['bf'], 'L2_ffn_wi': _L2_ffn_in['wi'], 'L2_ffn_ui': _L2_ffn_in['ui'], 'L2_ffn_bi': _L2_ffn_in['bi'], 'L2_ffn_wc': _L2_ffn_in['wc'], 'L2_ffn_uc': _L2_ffn_in['uc'], 'L2_ffn_bc': _L2_ffn_in['bc'], 'L2_ffn_wo': _L2_ffn_in['wo'], 'L2_ffn_uo': _L2_ffn_in['uo'], 'L2_ffn_bo': _L2_ffn_in['bo'], 'L2_ffn_in_c': _L2_ffn_in['in_c'], 'L3_xattn_q_w': _L3_xattn_in['q_w'], 'L3_xattn_q_b': _L3_xattn_in['q_b'], 'L3_xattn_k_w': _L3_xattn_in['k_w'], 'L3_xattn_k_b': _L3_xattn_in['k_b'], 'L3_xattn_v_w': _L3_xattn_in['v_w'], 'L3_xattn_v_b': _L3_xattn_in['v_b'], 'L3_xattn_o_w': _L3_xattn_in['o_w'], 'L3_xattn_o_b': _L3_xattn_in['o_b'], 'L3_ffn_gate_w': _L3_ffn_in['gate_w'], 'L3_ffn_w1': _L3_ffn_in['w1'], 'L3_ffn_w3': _L3_ffn_in['w3'], 'L3_ffn_w2': _L3_ffn_in['w2']}

def reference(x, ctx_1024, fside_1x16xSxS2_0, mask_BxS2_bk0, g_xattn, g_ffn, L0_xattn_Wq, L0_xattn_bq, L0_xattn_Wk, L0_xattn_bk, L0_xattn_Wv, L0_xattn_bv, L0_xattn_Wp, L0_xattn_bp, L0_ffn_W_fc, L0_ffn_b_fc, L0_ffn_A_fc, L0_ffn_B_fc, L0_ffn_W_proj, L0_ffn_b_proj, L0_ffn_A_proj, L0_ffn_B_proj, L1_xattn_W_a, L1_xattn_W_p, L1_xattn_V_p, L1_ffn_ln_g, L1_ffn_ln_b, L1_ffn_w_qkv_l, L1_ffn_w_out_l, L1_ffn_null_q, L1_ffn_rt_q, L1_ffn_rt_kv, L1_ffn_rms_g, L1_ffn_w_q_h, L1_ffn_w_kv_h, L1_ffn_null_kv, L1_ffn_w_out_h, L2_xattn_w_sim, L2_xattn_b_sim, L2_xattn_W_qv, L2_xattn_b_qv, L2_ffn_wf, L2_ffn_uf, L2_ffn_bf, L2_ffn_wi, L2_ffn_ui, L2_ffn_bi, L2_ffn_wc, L2_ffn_uc, L2_ffn_bc, L2_ffn_wo, L2_ffn_uo, L2_ffn_bo, L2_ffn_in_c, L3_xattn_q_w, L3_xattn_q_b, L3_xattn_k_w, L3_xattn_k_b, L3_xattn_v_w, L3_xattn_v_b, L3_xattn_o_w, L3_xattn_o_b, L3_ffn_gate_w, L3_ffn_w1, L3_ffn_w3, L3_ffn_w2):
    import jax
    import jax.numpy as jnp

    def _L0_xattn_ref(q, kv, Wq, bq, Wk, bk, Wv, bv, Wp, bp):
        import jax, jax.numpy as jnp
        import numpy as np
        NUM_HEADS = 16

        def softmax_one(x, axis=-1):
            m = jnp.max(x, axis=axis, keepdims=True)
            e = jnp.exp(x - m)
            return e / (jnp.exp(-m) * 0 + 1.0 + jnp.sum(e, axis=axis, keepdims=True))
        B, Nq, D = q.shape
        Nk = kv.shape[1]
        H = NUM_HEADS
        hd = D // H
        scale = hd ** (-0.5)
        qh = (q @ Wq.T + bq).reshape(B, Nq, H, hd).transpose(0, 2, 1, 3)
        kh = (kv @ Wk.T + bk).reshape(B, Nk, H, hd).transpose(0, 2, 1, 3)
        vh = (kv @ Wv.T + bv).reshape(B, Nk, H, hd).transpose(0, 2, 1, 3)
        attn = jnp.einsum('bhqd,bhkd->bhqk', qh * scale, kh)
        attn = softmax_one(attn, axis=-1)
        x = jnp.einsum('bhqk,bhkd->bhqd', attn, vh)
        x = x.transpose(0, 2, 1, 3).reshape(B, Nq, D)
        return x @ Wp.T + bp

    def _L0_ffn_ref(hidden_states, W_fc, b_fc, A_fc, B_fc, W_proj, b_proj, A_proj, B_proj):
        import jax, jax.numpy as jnp
        import numpy as np
        BITS = 8
        LORA_RANK = 16
        LORA_ALPHA = 32
        SCALING = LORA_ALPHA / LORA_RANK

        def fake_quant_weight(w, bits=BITS):
            qmax = 2.0 ** (bits - 1) - 1
            scale = jnp.max(jnp.abs(w)) / qmax
            wq = jnp.clip(jnp.round(w / scale), -qmax - 1, qmax) * scale
            return w + jax.lax.stop_gradient(wq - w)

        def qat_lora_linear(x, W, b, A, B):
            Wq = fake_quant_weight(W)
            base = jnp.einsum('bsi,oi->bso', x, Wq) + b
            lora = jnp.einsum('bsr,or->bso', jnp.einsum('bsi,ri->bsr', x, A), B)
            return base + SCALING * lora
        h = qat_lora_linear(hidden_states, W_fc, b_fc, A_fc, B_fc)
        h = jax.nn.gelu(h, approximate=False)
        h = qat_lora_linear(h, W_proj, b_proj, A_proj, B_proj)
        return h

    def _L1_xattn_ref(q, c_t, W_a, W_p, V_p):
        import jax, jax.numpy as jnp
        import numpy as np
        P_SIZE = 100
        WINDOW_LENGTH = 2
        STAN_DEV = WINDOW_LENGTH / 2.0
        B, S, T = (4, 1024, 512)
        Q_SIZE = C_SIZE = 256
        Bq, Sq, _ = q.shape
        hid = jnp.tanh(jnp.einsum('btc,pc->btp', c_t, W_p))
        p_t = Sq * jax.nn.sigmoid(jnp.einsum('btp,op->bto', hid, V_p))
        win_low = p_t.astype(jnp.int32) - WINDOW_LENGTH
        window = win_low + jnp.arange(2 * WINDOW_LENGTH, dtype=jnp.int32)
        window = jnp.clip(window, 0, Sq - 1)
        qw = jnp.take_along_axis(q[:, None, :, :], window[:, :, :, None], axis=2)
        scores = jnp.einsum('btwq,cq,btc->btw', qw, W_a, c_t)
        s_pos = window.astype(jnp.float32)
        gauss = jnp.exp(-jnp.square(s_pos - p_t) / (2.0 * STAN_DEV ** 2))
        a_t = jax.nn.softmax(scores, axis=-1) * gauss
        s_t = jnp.einsum('btw,btwq->btq', a_t, qw)
        return s_t

    def _L1_ffn_ref(x, ln_g, ln_b, w_qkv_l, w_out_l, null_q, rt_q, rt_kv, rms_g, w_q_h, w_kv_h, null_kv, w_out_h):
        import jax, jax.numpy as jnp
        import numpy as np
        DIM = 256
        HEADS = 8
        DH = 64
        HDH = HEADS * DH
        SEQ = 2048
        BATCH = 2
        WIN = 64
        N_ITERS = 50
        EPS = 1.0
        NQ = 256
        NKV = 512
        FETCH_K = 9.0 / 8.0

        def rmsnorm(x, g):
            n = jnp.maximum(jnp.sqrt(jnp.sum(x * x, axis=-1, keepdims=True)), 1e-12)
            return x / n * DIM ** 0.5 * g

        def layernorm(x, g, b):
            m = jnp.mean(x, axis=-1, keepdims=True)
            v = jnp.mean((x - m) ** 2, axis=-1, keepdims=True)
            return (x - m) / jnp.sqrt(v + 1e-05) * g + b

        def coor_descent(s, k_eff):
            logk = jnp.log(jnp.float32(k_eff))

            def body(carry, _):
                a, b = carry
                sb = (s + b) / EPS
                a = EPS * (logk - jax.nn.logsumexp(sb, axis=-1, keepdims=True))
                b = -jax.nn.relu(s + a)
                return ((a, b), None)
            init = (jnp.zeros_like(s[..., :1]), -s)
            (a, b), _ = jax.lax.scan(body, init, None, length=N_ITERS)
            return jnp.exp((s + a + b) / EPS)

        def route(x, routing_token, num_tokens, k_eff):
            s = jnp.einsum('bnd,rd->brn', x, routing_token)[:, 0]
            scores = coor_descent(s, k_eff)
            sel_scores, sel_idx = jax.lax.top_k(scores, num_tokens)
            sel_scores = sel_scores + jax.lax.stop_gradient(1.0 - sel_scores)
            return (sel_scores, sel_idx)

        def light_attn(x, ln_g, ln_b, w_qkv, w_out):
            b, n, _ = x.shape
            xn = layernorm(x, ln_g, ln_b)
            q, k, v = jnp.split(xn @ w_qkv, 3, axis=-1)

            def towin(t):
                return t.reshape(b, n // WIN, WIN, HEADS, DH).transpose(0, 3, 1, 2, 4)
            q, k, v = (towin(q), towin(k), towin(v))

            def around(t):
                pad = jnp.pad(t, ((0, 0), (0, 0), (1, 1), (0, 0), (0, 0)))
                return jnp.concatenate([pad[:, :, :-2], pad[:, :, 1:-1], pad[:, :, 2:]], axis=3)
            kk, vv = (around(k), around(v))
            nw = n // WIN
            wvalid = jnp.pad(jnp.ones((nw,), bool), (1, 1))
            kmask = jnp.concatenate([jnp.repeat(wvalid[:-2, None], WIN, 1), jnp.repeat(wvalid[1:-1, None], WIN, 1), jnp.repeat(wvalid[2:, None], WIN, 1)], axis=1)
            sim = jnp.einsum('bhnwd,bhnWd->bhnwW', q * DH ** (-0.5), kk)
            sim = jnp.where(kmask[None, None, :, None, :], sim, -jnp.finfo(sim.dtype).max)
            attn = jax.nn.softmax(sim, axis=-1)
            o = jnp.einsum('bhnwW,bhnWd->bhnwd', attn, vv)
            o = o.transpose(0, 2, 3, 1, 4).reshape(b, n, HDH)
            return o @ w_out

        def heavy_attn(xq, ctx, scores_kv, rms_g, w_q, w_kv, null_kv, w_out):
            b = xq.shape[0]
            xq = rmsnorm(xq, rms_g)
            ctx = rmsnorm(ctx, rms_g)
            q = (xq @ w_q).reshape(b, -1, HEADS, DH).transpose(0, 2, 1, 3)
            kv = jnp.einsum('bni,ihd->bhnd', ctx, w_kv)
            k, v = (kv[..., :DH], kv[..., DH:])
            v = v * scores_kv[:, None, :, None]
            nk = jnp.broadcast_to(null_kv[0][None, :, None, :], (b, HEADS, 1, DH))
            nv = jnp.broadcast_to(null_kv[1][None, :, None, :], (b, HEADS, 1, DH))
            k = jnp.concatenate([nk, k], axis=2)
            v = jnp.concatenate([nv, v], axis=2)
            sim = jnp.einsum('bhqd,bhkd->bhqk', q * DH ** (-0.5), k)
            attn = jax.nn.softmax(sim, axis=-1)
            o = jnp.einsum('bhqk,bhkd->bhqd', attn, v)
            o = o.transpose(0, 2, 1, 3).reshape(b, -1, HDH)
            return o @ w_out

        def forward(x, ln_g, ln_b, w_qkv_l, w_out_l, null_q, rt_q, rt_kv, rms_g, w_q_h, w_kv_h, null_kv, w_out_h):
            light = light_attn(x, ln_g, ln_b, w_qkv_l, w_out_l)
            sq, iq = route(x, rt_q, NQ, min(NQ * FETCH_K, SEQ))
            skv, ikv = route(x, rt_kv, NKV, min(NKV * FETCH_K, SEQ))
            batch_idx = jnp.arange(x.shape[0])[:, None]
            xq = x[batch_idx, iq]
            xkv = x[batch_idx, ikv]
            routed_out = heavy_attn(xq, xkv, skv, rms_g, w_q_h, w_kv_h, null_kv, w_out_h)
            routed_out = routed_out * sq[..., None]
            out = jnp.broadcast_to(null_q, x.shape)
            out = out.at[batch_idx, iq].set(routed_out)
            return light + out
        return forward(x, ln_g, ln_b, w_qkv_l, w_out_l, null_q, rt_q, rt_kv, rms_g, w_q_h, w_kv_h, null_kv, w_out_h)

    def _L2_xattn_ref(encoder_hc, decoder_hq, w_sim, b_sim, W_qv, b_qv):
        import jax, jax.numpy as jnp
        import numpy as np
        B, L_ENC, L_DEC, D = (16, 128, 128, 256)
        d = encoder_hc.shape[-1]
        w1, w2, w3 = (w_sim[:d], w_sim[d:2 * d], w_sim[2 * d:])
        Sim = (encoder_hc @ w1)[:, :, None] + (decoder_hq @ w2)[:, None, :] + jnp.einsum('bid,bjd->bij', encoder_hc * w3, decoder_hq) + b_sim[0]
        A = jax.nn.softmax(Sim, axis=2)
        hq_hat = jnp.einsum('bij,bjd->bid', A, decoder_hq)
        Batt = jax.nn.softmax(jnp.max(Sim, axis=2), axis=1)
        hc_bar = jnp.einsum('bi,bid->bd', Batt, encoder_hc)[:, None, :]
        hc_hat = jnp.broadcast_to(hc_bar, encoder_hc.shape)
        feats = jnp.concatenate([encoder_hc, hq_hat, encoder_hc * hq_hat, encoder_hc * hc_hat], axis=-1)
        hcq = feats @ W_qv + b_qv
        return hcq

    def _L2_ffn_ref(x, wf, uf, bf, wi, ui, bi, wc, uc, bc, wo, uo, bo, in_c):
        import jax, jax.numpy as jnp
        import numpy as np
        from jax import lax
        T, B, I, M, O = (64, 64, 256, 256, 256)

        def _xavier(key, shape):
            fan_out, fan_in = shape
            limit = float(np.sqrt(6.0 / (fan_in + fan_out)))
            return jax.random.uniform(key, shape, jnp.float32, -limit, limit)
        batch = x.shape[1]
        c0 = jnp.broadcast_to(in_c, (batch, in_c.shape[0]))

        def step(c, xt):
            ft = jax.nn.sigmoid(xt @ wf.T + c @ uf.T + bf)
            it = jax.nn.sigmoid(xt @ wi.T + c @ ui.T + bi)
            gt = jnp.tanh(xt @ wc.T + c @ uc.T + bc)
            c = ft * c + it * gt
            return (c, None)
        c_final, _ = lax.scan(step, c0, x)
        h = jnp.tanh(jnp.einsum('tbi,oi->tbo', x, wo) + c_final @ uo.T + bo)
        return h

    def _L3_xattn_ref(query, key, value, key_padding_mask, bias, q_w, q_b, k_w, k_b, v_w, v_b, o_w, o_b):
        import jax, jax.numpy as jnp
        import numpy as np
        B, S, H, NH = (2, 512, 256, 16)
        HD = H // NH

        def _shape(x):
            b, s, _ = x.shape
            return x.reshape(b, s, NH, HD).transpose(0, 2, 1, 3)
        scale = HD ** (-0.5)
        q = _shape(query @ q_w.T + q_b)
        k = _shape(key @ k_w.T + k_b)
        v = _shape(value @ v_w.T + v_b)
        attn = jnp.einsum('bhqd,bhkd->bhqk', q, k) * scale + bias
        mask = key_padding_mask[:, None, None, :]
        attn = jnp.where(mask, -jnp.inf, attn)
        probs = jax.nn.softmax(attn, axis=-1)
        probs = jnp.where(mask, 0.0, probs)
        denom = jnp.maximum(probs.sum(axis=-1, keepdims=True), 1e-06)
        probs = probs / denom
        ctx = jnp.einsum('bhqk,bhkd->bhqd', probs, v)
        ctx = ctx.transpose(0, 2, 1, 3).reshape(query.shape[0], query.shape[1], H)
        return ctx @ o_w.T + o_b

    def _L3_ffn_ref(hidden_states, gate_w, w1, w3, w2):
        import jax, jax.numpy as jnp
        import numpy as np
        N_EXPERTS = 16
        TOP_K = 4
        HIDDEN = 256
        INTER = 128
        B, S = (2, 256)
        'DeepseekV3 MoE adapter forward: router -> sparse scores -> expert GLU MLP -> combine.'
        b, s, h = hidden_states.shape
        x = hidden_states.reshape(-1, h)
        logits = jnp.einsum('th,eh->te', x, gate_w)
        probs = jax.nn.softmax(logits, axis=-1)
        topk_w, topk_idx = jax.lax.top_k(probs, TOP_K)
        topk_w = topk_w / jnp.sum(topk_w, axis=-1, keepdims=True)
        one_hot = (topk_idx[..., None] == jnp.arange(N_EXPERTS)).astype(topk_w.dtype)
        scores = jnp.einsum('tk,tke->te', topk_w, one_hot)
        g = jnp.einsum('th,ehi->tei', x, w1)
        u = jnp.einsum('th,ehi->tei', x, w3)
        act = jax.nn.silu(g) * u
        expert_out = jnp.einsum('tei,eih->teh', act, w2)
        out = jnp.einsum('teh,te->th', expert_out, scores)
        return out.reshape(b, s, h)
    x = x + jnp.tanh(g_xattn[0]) * _L0_xattn_ref(_layernorm(x, axis=-1), ctx_1024, L0_xattn_Wq, L0_xattn_bq, L0_xattn_Wk, L0_xattn_bk, L0_xattn_Wv, L0_xattn_bv, L0_xattn_Wp, L0_xattn_bp)
    x = x + jnp.tanh(g_ffn[0]) * _L0_ffn_ref(_layernorm(x, axis=-1), L0_ffn_W_fc, L0_ffn_b_fc, L0_ffn_A_fc, L0_ffn_B_fc, L0_ffn_W_proj, L0_ffn_b_proj, L0_ffn_A_proj, L0_ffn_B_proj)
    x = x + jnp.tanh(g_xattn[1]) * _L1_xattn_ref(ctx_1024, _layernorm(x, axis=-1), L1_xattn_W_a, L1_xattn_W_p, L1_xattn_V_p)
    x = x + jnp.tanh(g_ffn[1]) * _L1_ffn_ref(_layernorm(x, axis=-1), L1_ffn_ln_g, L1_ffn_ln_b, L1_ffn_w_qkv_l, L1_ffn_w_out_l, L1_ffn_null_q, L1_ffn_rt_q, L1_ffn_rt_kv, L1_ffn_rms_g, L1_ffn_w_q_h, L1_ffn_w_kv_h, L1_ffn_null_kv, L1_ffn_w_out_h)
    x = x + jnp.tanh(g_xattn[2]) * _L2_xattn_ref(_layernorm(x, axis=-1), ctx_1024, L2_xattn_w_sim, L2_xattn_b_sim, L2_xattn_W_qv, L2_xattn_b_qv)
    x = x + jnp.tanh(g_ffn[2]) * _L2_ffn_ref(_layernorm(x, axis=-1), L2_ffn_wf, L2_ffn_uf, L2_ffn_bf, L2_ffn_wi, L2_ffn_ui, L2_ffn_bi, L2_ffn_wc, L2_ffn_uc, L2_ffn_bc, L2_ffn_wo, L2_ffn_uo, L2_ffn_bo, L2_ffn_in_c)
    x = x + jnp.tanh(g_xattn[3]) * _L3_xattn_ref(_layernorm(x, axis=-1), ctx_1024, ctx_1024, mask_BxS2_bk0, fside_1x16xSxS2_0, L3_xattn_q_w, L3_xattn_q_b, L3_xattn_k_w, L3_xattn_k_b, L3_xattn_v_w, L3_xattn_v_b, L3_xattn_o_w, L3_xattn_o_b)
    x = x + jnp.tanh(g_ffn[3]) * _L3_ffn_ref(_layernorm(x, axis=-1), L3_ffn_gate_w, L3_ffn_w1, L3_ffn_w3, L3_ffn_w2)
    return x

_drawn_inputs = setup_inputs


def setup_inputs(seed=0):
    import zlib

    import numpy as np

    out = dict(_drawn_inputs(seed))
    spreads = {'L0_ffn_b_fc': (0.0, 0.1),
     'L0_ffn_B_fc': (0.0, 0.1),
     'L0_ffn_b_proj': (0.0, 0.1),
     'L0_ffn_B_proj': (0.0, 0.1),
     'L1_ffn_ln_g': (1.0, 0.6),
     'L1_ffn_ln_b': (0.0, 0.8),
     'L1_ffn_rms_g': (1.0, 0.6),
     'L2_ffn_bf': (0.0, 0.8),
     'L2_ffn_bi': (0.0, 0.8),
     'L2_ffn_bc': (0.0, 0.491),
     'L2_ffn_bo': (0.0, 0.281),
     'L2_ffn_in_c': (0.0, 0.565),
     'L3_xattn_q_b': (0.0, 0.8),
     'L3_xattn_k_b': (0.0, 2.0),
     'L3_xattn_v_b': (0.0, 0.601),
     'L3_xattn_o_b': (0.0, 0.1)}
    factors = {'fside_1x16xSxS2_0': 8.0,
     'g_ffn': 26.504,
     'L0_xattn_bq': 3.241,
     'L0_xattn_bk': 64.0,
     'L0_xattn_bv': 3.071,
     'L1_ffn_rt_kv': 8.0,
     'L1_ffn_w_q_h': 8.0,
     'L1_ffn_w_kv_h': 3.164,
     'L1_ffn_null_kv': 8.0,
     'L1_ffn_w_out_h': 3.053,
     'L2_xattn_w_sim': 2.683,
     'L2_xattn_b_qv': 5.995,
     'L2_ffn_wf': 2.715,
     'L2_ffn_uf': 7.751,
     'L2_ffn_ui': 4.044,
     'L3_xattn_q_w': 8.0,
     'L3_xattn_k_w': 8.0,
     'L3_ffn_gate_w': 8.0,
     'L3_ffn_w1': 8.0,
     'L3_ffn_w3': 8.0,
     'L3_ffn_w2': 8.0}
    for name, (base, spread) in spreads.items():
        noise = np.random.default_rng([zlib.crc32(name.encode()), seed]).standard_normal(out[name].shape)
        drawn = base * np.exp(spread * noise) if base else spread * noise
        out[name] = jnp.asarray(drawn.astype(out[name].dtype))
    for name, factor in factors.items():
        out[name] = (out[name] * factor).astype(out[name].dtype)
    return out
```

```python
from contextlib import ExitStack

import numpy as np

import concourse.bass as bass
from concourse import mybir

F32 = mybir.dt.float32
BF16 = mybir.dt.bfloat16
U8 = mybir.dt.uint8
ALU = mybir.AluOpType
ACT = mybir.ActivationFunctionType
AX = mybir.AxisListType

P = 128
B, S, D = 2, 1024, 256
NT = B * S // P
HT = S // P
DC = D // P
SC = 77
H16, HD16 = 16, 16
HPC = P // HD16
F0 = 1024
FC = F0 // P
RANK = 16
WIN, PSZ = 4, 100
H8, DH = 8, 64
HDH = H8 * DH
WINDOW = 64
HC = HDH // P
NQ, NKV = 256, 512
FETCH, SEQ_CAP = 9.0 / 8.0, 2048
NE, TOP, INTER = 16, 4, 128
EPS = 1e-5
NEG = -1e30
MAGIC = 12582912.0

PACKS = {
    "const": [("ident", P), ("headmask", HPC), ("ones", P), ("before", P), ("slots", NKV)],
    "A": [("wq", DC * D), ("wk", DC * D), ("wv", DC * D), ("wp", DC * D), ("bq", DC), ("bk", DC)],
    "B": [("fc", DC * F0), ("proj", FC * D), ("bfc", FC)],
    "lora": [("afc", D), ("bfcT", F0), ("aproj", F0), ("bprojT", D)],
    "C": [("wp", DC * PSZ), ("wa", DC * D), ("vp", 1), ("iota", SC), ("woff", WIN)],
    "D": [("wqkv", DC * 3 * HDH), ("wout", HC * D), ("wqh", DC * HDH), ("wkh", DC * HDH), ("wvh", DC * HDH),
          ("wouth", HC * D), ("lng", DC), ("lnb", DC), ("rmsg", DC), ("nk", HC * H8)],
    "E": [("wqv", 4 * DC * D), ("w1", DC), ("w2", DC), ("w3", DC)],
    "F": [(n, DC * D) for n in ("wf", "wi", "wc", "wo", "uf", "ui", "uc", "uo")] + [("bias", 3 * DC), ("c0", DC)],
    "G": [("wq", DC * D), ("wk", DC * D), ("wv", DC * D), ("wp", DC * D), ("bq", DC), ("bk", DC)],
    "H": [("gate", DC * NE)],
}
ROWS = {"A": [("bv", D), ("bp", D)], "B": [("bproj", D)], "D": [("rtq", D), ("rtkv", D), ("nullq", D), ("nv", HDH)],
        "E": [("bqv", D), ("bsim", 1)], "F": [("bo", D)], "G": [("bv", D), ("bp", D)]}
LOADS = {"A": 32, "B": 48, "C": 16, "D": 64, "E": 32, "F": 32, "G": 32, "H": 80}


def columns(pack):
    at, out = 0, {}
    for name, n in pack:
        out[name] = (at, at + n)
        at += n
    return out, at


class Chain:

    def __init__(self, eng, sem):
        self.eng, self.sem, self.base, self.k, self.i, self.per = eng, sem, 0, 0, None, 0

    def link(self, ins):
        ins.then_inc(self.sem, 1)
        self.k += 1
        if self.i is None:
            self.eng.wait_ge(self.sem, self.base + self.k)
        else:
            self.eng.wait_ge(self.sem, self.i * self.per + (self.base + self.k))

    def begin(self, i, per):
        self.base += self.k
        self.i, self.per, self.k = i, per, 0

    def end(self, trips):
        assert self.k == self.per, (self.k, self.per)
        self.base, self.i, self.k = self.base + trips * self.per, None, 0


def nth(i, per, k):
    return i * per + (k + 1)


TOTALS = {
    "xn_ready": {"A": 16, "B": 16, "C": 16, "D": 16, "E": 16, "F": 16, "G": 16, "H": 16},
    "xT_ps": {"A": 8, "B": 8, "C": 8, "D": 16, "E": 8, "F": 8, "G": 8, "H": 8},
    "xT_ready": {"A": 8, "B": 8, "C": 8, "D": 16, "E": 8, "F": 8, "G": 8, "H": 8},
    "x_new": {"A": 16, "B": 16, "C": 16, "D": 16, "E": 16, "F": 16, "G": 16, "H": 16},
    "y_ps": {"A": 16, "B": 16, "C": 16, "D": 16, "E": 16, "F": 8, "G": 16, "H": 16},
    "var": {"A": 1, "B": 1, "C": 1, "Dx": 1, "Dh": 1, "E": 1, "F": 1, "G": 1, "H": 1},
    "std": {"A": 1, "B": 1, "C": 1, "Dx": 1, "Dh": 1, "E": 1, "F": 1, "G": 1, "H": 1},
    "q_ps": {"A": 8, "D": 16, "G": 8},
    "q_ready": {"A": 8, "D": 16, "G": 8},
    "s_ps": {"A": 32, "C": 8, "D": 32, "E": 16, "G": 32},
    "p_ready": {"A": 32, "D": 32, "E": 16, "G": 32},
    "pT_ps": {"A": 32, "D": 32, "G": 32},
    "pT_ready": {"A": 32, "D": 32, "G": 32},
    "o_ps": {"A": 32, "D": 32, "G": 32},
    "on_ready": {"A": 32, "D": 32, "G": 32},
    "oT_ps": {"A": 16, "D": 32, "G": 16},
    "oT_ready": {"A": 16, "D": 32, "G": 16},
    "a_ready": {"C": 8, "E": 8},
    "aT_ps": {"C": 8, "E": 8},
    "aT_ready": {"C": 8, "E": 8},
    "kv_ps": {"A": 1, "G": 1},
    "kv_ready": {"A": 1, "G": 1},
    "sub_ready": {"A": 32, "G": 32},
}


def done(layer, name):
    total = 0
    for each, count in TOTALS[name].items():
        if each == layer:
            return total
        total += count


def build(nc, ins, out, stop):
    ctx = ExitStack()
    with ctx:
        def sb(name, shape, dt=F32):
            return ctx.enter_context(nc.sbuf_tensor(name, shape, dt))

        sems = {}

        def sem(name):
            if name not in sems:
                sems[name] = ctx.enter_context(nc.semaphore(name))
            return sems[name]

        x = sb("x", [P, NT, D])
        hall = sb("hall", [P, NT, D])
        work = sb("work", [P, 9216])
        stats = sb("stats", [P, NT, 6])
        mean = sb("mean", [P, NT, 1])
        rstd = sb("rstd", [P, NT, 1])
        small = sb("small", [P, 512])
        gates = sb("gates", [P, 8])
        ctxT = sb("ctxT", [P, DC, B * SC])
        ctxN = sb("ctxN", [SC, B, D])
        maskR = sb("maskR", [B, HT, 2 * P], BF16)
        maskL = sb("maskL", [B, P], BF16)
        route = sb("route", [P, 640])
        mask8 = sb("mask8", [SC, B], U8)
        maskrow8 = sb("maskrow8", [1, B, SC], U8)
        big = sb("big", [P, 12288])
        dpack = sb("dpack", [P, columns(PACKS["D"])[1]])
        place, at_big, at_d = {"D": dpack}, 0, 0
        for name in ("A", "B", "lora"):
            n = columns(PACKS[name])[1]
            place[name] = big[0:RANK if name == "lora" else P, at_big:at_big + n]
            at_big += n
        for name in ("G", "H"):
            n = columns(PACKS[name])[1]
            place[name] = dpack[:, at_d:at_d + n]
            at_d += n
        bias_sb = dpack[:, at_d:at_d + 2 * H16 * SC].rearrange("p (j n) -> p j n", j=2)
        at_d += 2 * H16 * SC
        esel = dpack[0:NE, at_d:at_d + NE * P].rearrange("p (e n) -> p e n", e=NE)
        packs, pk = {}, {}
        for name, pack in PACKS.items():
            cols, n = columns(pack)
            packs[name] = place[name] if name in place else sb(f"pack_{name}", [P, n])
            pk[name] = {k: packs[name][:, a:b] for k, (a, b) in cols.items()}
        rows, rw = {}, {}
        for name, pack in ROWS.items():
            cols, n = columns(pack)
            rows[name] = sb(f"rows_{name}", [P, n])
            rw[name] = {k: rows[name][:, a:b] for k, (a, b) in cols.items()}
        ps = ctx.enter_context(nc.psum_tensor("ps", [P, 8, 512], F32))
        ident = pk["const"]["ident"]
        ones = pk["const"]["ones"]

        def carve(specs, base=work, at=0):
            views = {}
            for name, dims in specs:
                n = int(np.prod(dims))
                assert at + n <= base.shape[1], name
                v = base[:, at:at + n]
                at += n
                if len(dims) == 2:
                    v = v.rearrange("p (a b) -> p a b", a=dims[0])
                elif len(dims) == 3:
                    v = v.rearrange("p (a b c) -> p a b c", a=dims[0], b=dims[1])
                elif len(dims) == 4:
                    v = v.rearrange("p (a b c d) -> p a b c d", a=dims[0], b=dims[1], c=dims[2])
                views[name] = v
            return views

        score_rows = nc.dram_tensor("score_rows", (2 * B * HT, P), F32, kind="Internal").ap()
        hflat = hall[:, :, :].rearrange("p t d -> p (t d)")
        KV = carve([("kbd", (DC, B, HPC * SC)), ("vaug", (B, H16, HD16 + 1)), ("kmask", (512,))], hflat)
        keep = small[0:SC, 0:B]
        maskrow = sb("maskrow", [1, B, SC], BF16)
        onesb = sb("onesb", [1, P], BF16)

        block = ctx.enter_context(nc.Block())

        UNITS = [(b, c) for b in range(B) for c in range(DC)]
        NU = len(UNITS)
        A = carve([("xn", (B, D)), ("xnT", (DC, B * P)), ("qT", (DC, B * P)), ("sub", (2, HPC * SC)),
                   ("p", (2, HPC * SC)), ("pT", (2, HPC * P)), ("on", (2, P)), ("oT", (B, D)), ("tmp", (B, D)),
                   ("mx", (2, HPC)), ("den", (2, HPC)), ("em", (NU, HPC)), ("rden", (2, HPC))])
        S_BANK = [0, 2]
        XT_BANK, Q_BANK, PT_BANK = 4, 5, 6
        O_REG = ps[:, 4, 0:HPC * (HD16 + 1)]
        OT_REG, Y_REG = ps[:, 5, 0:D], ps[:, 5, D:2 * D]

        def s_psum(u):
            return ps[:, S_BANK[u % 2]:S_BANK[u % 2] + 2, 0:4 * SC].rearrange("p k (h s) -> p k h s", h=4)

        def quad(ap):
            return ap.rearrange("p (k h s) -> p k h s", k=2, h=4)

        def load_bias(sp):
            def load(n, j):
                sp.dma_start(bias_sb[:, j, :].rearrange("p (h s) -> p h s", h=H16),
                             ins["fside"][:, :, bass.ds(n * P, P), :].rearrange("o h p s -> p (o h) s")
                             ).then_inc(sem(f"G_bias_in{j}"), 16)

            load(0, 0)
            load(1, 1)
            with sp.Fori(1, HT // 2) as i:
                for j in range(2):
                    sp.wait_ge(sem("G_bias_free"), i * 2 + (j - 1))
                    load(i * 2 + j, j)

        def heads16_pe(pe, L):
            w = pk[L]
            s = lambda n: sem(n if n in TOTALS else f"{L}_{n}")
            pe.wait_ge(sem("const_in"), 96)
            pe.wait_ge(sem(f"{L}_in"), LOADS[L])
            for c in range(DC):
                for ci in range(DC):
                    mm = nc.tensor.matmul(ps[:, c, 0:B * SC], w["wk"][:, ci * D + c * P:ci * D + (c + 1) * P],
                                          ctxT[:, ci, :], start=ci == 0, stop=ci == DC - 1)
            for b in range(B):
                for ci in range(DC):
                    mm = nc.tensor.matmul(ps[0:SC, 2 + b, 0:D], ctxT[:, ci, b * SC:(b + 1) * SC],
                                          w["wv"][:, ci * D:(ci + 1) * D], start=ci == 0, stop=ci == DC - 1)
            mm.then_inc(s("kv_ps"), 1)
            pe.wait_ge(s("kv_ready"), 1 + done(L, "kv_ready"))

            with pe.Fori(0, HT) as i:
                for b in range(B):
                    pe.wait_ge(s("xn_ready"), nth(i, B, b) + done(L, "xn_ready"))
                    for c in range(DC):
                        mm = nc.tensor.transpose(ps[:, XT_BANK, c * D + b * P:c * D + (b + 1) * P],
                                                 A["xn"][:, b, c * P:(c + 1) * P], ident)
                mm.then_inc(s("xT_ps"), 1)
                pe.wait_ge(s("xT_ready"), nth(i, 1, 0) + done(L, "xT_ready"))
                for co in range(DC):
                    for ci in range(DC):
                        mm = nc.tensor.matmul(ps[:, Q_BANK, co * D:(co + 1) * D],
                                              w["wq"][:, ci * D + co * P:ci * D + (co + 1) * P],
                                              A["xnT"][:, ci, :], start=ci == 0, stop=ci == DC - 1)
                mm.then_inc(s("q_ps"), 1)

                def scores(u):
                    b, c = UNITS[u]
                    if u == 0:
                        pe.wait_ge(s("q_ready"), nth(i, 1, 0) + done(L, "q_ready"))
                    if u >= 2:
                        pe.wait_ge(s("sub_ready"), nth(i, NU, u - 2) + done(L, "sub_ready"))
                    for k in range(2):
                        o = ps[:, S_BANK[u % 2] + k, 0:4 * SC]
                        mm = nc.tensor.matmul(o, A["qT"][:, c, b * P:(b + 1) * P],
                                              KV["kbd"][:, c, b, k * 4 * SC:(k + 1) * 4 * SC], start=True, stop=L == "A")
                        if L == "G":
                            for h in range(4):
                                mm = nc.tensor.matmul(ps[:, S_BANK[u % 2] + k, h * SC:(h + 1) * SC], onesb[:, :],
                                                      maskrow[:, b, :], start=False, stop=h == 3)
                    mm.then_inc(s("s_ps"), 1)

                def turn_p(u):
                    pe.wait_ge(s("p_ready"), nth(i, NU, u) + done(L, "p_ready"))
                    if u >= 1:
                        pe.wait_ge(s("pT_ready"), nth(i, NU, u - 1) + done(L, "pT_ready"))
                    for h in range(HPC):
                        mm = nc.tensor.transpose(ps[0:SC, PT_BANK + h // 4, h % 4 * P:(h % 4 + 1) * P],
                                                 A["p"][:, u % 2, h * SC:(h + 1) * SC], ident)
                    mm.then_inc(s("pT_ps"), 1)

                def weigh_v(u):
                    b, c = UNITS[u]
                    pe.wait_ge(s("pT_ready"), nth(i, NU, u) + done(L, "pT_ready"))
                    if u >= 1:
                        pe.wait_ge(s("on_ready"), nth(i, NU, u - 1) + done(L, "on_ready"))
                    for h in range(HPC):
                        mm = nc.tensor.matmul(O_REG[:, h * 17:h * 17 + 17],
                                              A["pT"][0:SC, u % 2, h * P:(h + 1) * P],
                                              KV["vaug"][0:SC, b, c * HPC + h, :], start=True, stop=True)
                    mm.then_inc(s("o_ps"), 1)

                def turn_o(b):
                    pe.wait_ge(s("on_ready"), nth(i, NU, 2 * b + 1) + done(L, "on_ready"))
                    if b == 1:
                        pe.wait_ge(s("x_new"), nth(i, B, 0) + done(L, "x_new"))
                    for c in range(DC):
                        mm = nc.tensor.transpose(OT_REG[:, c * P:(c + 1) * P], A["on"][:, (2 * b + c) % 2, :], ident)
                    mm.then_inc(s("oT_ps"), 1)

                def project(b):
                    pe.wait_ge(s("oT_ready"), nth(i, B, b) + done(L, "oT_ready"))
                    for c in range(DC):
                        mm = nc.tensor.matmul(Y_REG, A["oT"][:, b, c * P:(c + 1) * P], w["wp"][:, c * D:(c + 1) * D],
                                              start=c == 0, stop=c == DC - 1)
                    mm.then_inc(s("y_ps"), 1)

                scores(0)
                scores(1)
                turn_p(0)
                scores(2)
                weigh_v(0)
                turn_p(1)
                scores(3)
                weigh_v(1)
                turn_p(2)
                turn_o(0)
                weigh_v(2)
                turn_p(3)
                project(0)
                weigh_v(3)
                turn_o(1)
                project(1)

        def heads16_act(act, L):
            s = lambda n: sem(n if n in TOTALS else f"{L}_{n}")
            with act.Fori(0, HT) as i:
                act.wait_ge(s("xT_ps"), nth(i, 1, 0) + done(L, "xT_ps"))
                nc.scalar.copy(A["xnT"], ps[:, XT_BANK, :].rearrange("p (c n) -> p c n", c=DC)).then_inc(s("xT_ready"), 1)

                def exps(u):
                    act.wait_ge(s("sub_ready"), nth(i, NU, u) + done(L, "sub_ready"))
                    if u >= 2:
                        act.wait_ge(s("pT_ps"), nth(i, NU, u - 2) + done(L, "pT_ps"))
                    if L == "A":
                        nc.scalar.activation(A["em"][:, u, :], A["mx"][:, u % 2, :], ACT.Exp,
                                             scale=-1.0).then_inc(s("em_ready"), 1)
                    nc.scalar.activation(A["p"][:, u % 2, :], A["sub"][:, u % 2, :], ACT.Exp).then_inc(s("p_ready"), 1)

                def take_pT(u):
                    act.wait_ge(s("pT_ps"), nth(i, NU, u) + done(L, "pT_ps"))
                    if u >= 2:
                        act.wait_ge(s("o_ps"), nth(i, NU, u - 2) + done(L, "o_ps"))
                    nc.scalar.copy(A["pT"][0:SC, u % 2, :].rearrange("p (k n) -> p k n", k=2),
                                   ps[0:SC, PT_BANK:PT_BANK + 2, :]).then_inc(s("pT_ready"), 1)

                def take_oT(b):
                    act.wait_ge(s("oT_ps"), nth(i, B, b) + done(L, "oT_ps"))
                    nc.scalar.copy(A["oT"][:, b, :], OT_REG).then_inc(s("oT_ready"), 1)

                exps(0)
                exps(1)
                take_pT(0)
                exps(2)
                take_pT(1)
                exps(3)
                take_pT(2)
                take_oT(0)
                take_pT(3)
                take_oT(1)

        def finish(t, y, bias, gate, tmp, done):
            if bias is not None:
                chain_dve.link(nc.vector.tensor_tensor(tmp, y, bias, ALU.add))
                y = tmp
            chain_dve.link(nc.vector.scalar_tensor_tensor(out=x[:, t, :], in0=y, scalar=gates[:, gate:gate + 1], in1=x[:, t, :],
                                         op0=ALU.mult, op1=ALU.add))
            nc.vector.bn_stats(stats[:, t, :], x[:, t, :]).then_inc(done, 1)

        def heads16_dve(dve, L):
            link = chain_dve.link
            w = pk[L]
            s = lambda n: sem(n if n in TOTALS else f"{L}_{n}")
            ve = nc.vector
            dve.wait_ge(sem("const_in"), 96)
            dve.wait_ge(sem(f"{L}_in"), LOADS[L])
            dve.wait_ge(s("kv_ps"), 1 + done(L, "kv_ps"))
            hm = pk["const"]["headmask"]
            for c in range(DC):
                for b in range(B):
                    link(ve.scalar_tensor_tensor(
                        out=KV["kbd"][:, c, b, :].rearrange("p (h s) -> p h s", h=HPC),
                        in0=ps[:, c, b * SC:(b + 1) * SC].rearrange("p (o s) -> p o s", o=1).to_broadcast([P, HPC, SC]),
                        scalar=w["bk"][:, c:c + 1], in1=hm.rearrange("p (h o) -> p h o", o=1).to_broadcast([P, HPC, SC]),
                        op0=ALU.add, op1=ALU.mult))
            if L == "G":
                link(ve.tensor_copy(keep, mask8[:, :]))
                link(ve.tensor_scalar(keep, keep, -1.0, 1.0, ALU.mult, ALU.add))
                link(ve.tensor_copy(small[0:1, 8:8 + B * SC], maskrow8[:, :, :].rearrange("p b s -> p (b s)")))
                link(ve.tensor_scalar(maskrow[:, :, :].rearrange("p b s -> p (b s)"), small[0:1, 8:8 + B * SC], NEG, None, ALU.mult))
                link(ve.memset(onesb[:, :], 1.0))
            link(ve.memset(KV["vaug"][0:SC], 1.0))
            for b in range(B):
                link(ve.tensor_tensor(KV["vaug"][0:SC, b, :, 0:HD16],
                                      ps[0:SC, 2 + b, 0:D].rearrange("p (h e) -> p h e", h=H16),
                                      rw[L]["bv"][0:SC, :].rearrange("p (h e) -> p h e", h=H16), ALU.add))
                if L == "G":
                    link(ve.tensor_scalar(KV["vaug"][0:SC, b], KV["vaug"][0:SC, b], keep[:, b:b + 1], None, ALU.mult))
            link(ve.memset(small[:, 511:512], 0.0))
            dve.sem_inc(s("kv_ready"), 1)

            def body(i, j=None):
                n = i if j is None else i * 2 + j
                for b in range(B):
                    t = n + b * HT
                    ve.tensor_scalar(A["xn"][:, b, :], x[:, t, :], mean[:, t, :], rstd[:, t, :],
                                     ALU.subtract, ALU.mult).then_inc(s("xn_ready"), 1)
                dve.wait_ge(s("q_ps"), nth(n, 1, 0) + done(L, "q_ps"))
                for c in range(DC):
                    q = ve.tensor_scalar(A["qT"][:, c, :], ps[:, Q_BANK, c * D:(c + 1) * D], w["bq"][:, c:c + 1],
                                         HD16 ** -0.5, ALU.add, ALU.mult)
                    if c == 0:
                        link(q)
                    else:
                        q.then_inc(s("q_ready"), 1)

                def shift(u):
                    b, c = UNITS[u]
                    m = A["mx"][:, u % 2, :]
                    dve.wait_ge(s("s_ps"), nth(n, NU, u) + done(L, "s_ps"))
                    if u >= 2:
                        dve.wait_ge(s("p_ready"), nth(n, NU, u - 2) + done(L, "p_ready"))
                    src = s_psum(u)
                    if L == "G":
                        if u == 0:
                            dve.wait_ge(sem(f"G_bias_in{j}"), nth(i, 1, 0) * 16)
                        ins_ = ve.tensor_tensor(quad(A["sub"][:, u % 2, :]), src,
                                                quad(bias_sb[:, j, c * HPC * SC:(c + 1) * HPC * SC]), ALU.add)
                        if u == NU - 1:
                            ins_.then_inc(s("bias_free"), 1)
                            dve.wait_ge(s("bias_free"), nth(n, 1, 0))
                        else:
                            link(ins_)
                        src = quad(A["sub"][:, u % 2, :])
                    link(ve.tensor_reduce(m.rearrange("p (k h) -> p k h", k=2), src, AX.X, ALU.max))
                    ve.tensor_tensor(quad(A["sub"][:, u % 2, :]), src,
                                     m.rearrange("p (k h o) -> p k h o", k=2, o=1).to_broadcast([P, 2, 4, SC]),
                                     ALU.subtract).then_inc(s("sub_ready"), 1)

                def normalise(u):
                    o = O_REG.rearrange("p (h e) -> p h e", h=HPC)
                    den = A["den"][:, u % 2, :]
                    dve.wait_ge(s("o_ps"), nth(n, NU, u) + done(L, "o_ps"))
                    if L == "A":
                        dve.wait_ge(s("em_ready"), nth(n, NU, u))
                        link(ve.tensor_scalar(A["em"][:, u, :], A["em"][:, u, :], 0.0, 1.0, ALU.mult, ALU.add))
                        link(ve.tensor_tensor(den, A["em"][:, u, :], o[:, :, HD16], ALU.add))
                    else:
                        link(ve.tensor_scalar(den, o[:, :, HD16], 1e-6, None, ALU.max))
                    link(ve.reciprocal(A["rden"][:, u % 2, :], den))
                    if u >= 2:
                        dve.wait_ge(s("oT_ps"), nth(n, B, u // 2 - 1) + done(L, "oT_ps"))
                    ve.tensor_tensor(A["on"][:, u % 2, :].rearrange("p (h e) -> p h e", h=HPC), o[:, :, 0:HD16],
                                     A["rden"][:, u % 2, :].rearrange("p (h o) -> p h o", o=1).to_broadcast([P, HPC, HD16]),
                                     ALU.mult).then_inc(s("on_ready"), 1)

                def update(b):
                    dve.wait_ge(s("y_ps"), nth(n, B, b) + done(L, "y_ps"))
                    finish(n + b * HT, Y_REG, rw[L]["bp"], {"A": 0, "G": 3}[L], A["tmp"][:, b, :], s("x_new"))

                shift(0)
                shift(1)
                shift(2)
                normalise(0)
                shift(3)
                normalise(1)
                normalise(2)
                update(0)
                normalise(3)
                update(1)

            if L == "A":
                per = 1 + 4 * 1 + 4 * 3 + 2 * 2
                with dve.Fori(0, HT) as i:
                    chain_dve.begin(i, per)
                    body(i)
                chain_dve.end(HT)
            else:
                per = 2 * (1 + 3 * 2 + 1 + 4 * 2 + 2 * 2)
                with dve.Fori(0, HT // 2) as i:
                    chain_dve.begin(i, per)
                    for j in range(2):
                        body(i, j)
                chain_dve.end(HT // 2)

        def norm_dve(dve, L):
            link, ve = chain_dve.link, nc.vector
            m0, m1, v0, v1 = (stats[:, :, k] for k in (1, 4, 2, 5))
            half, t1 = small[:, 256:256 + NT], small[:, 272:272 + NT]
            link(ve.tensor_tensor(t1, m0, m1, ALU.add))
            link(ve.tensor_scalar(mean[:, :, 0], t1, 0.5, None, ALU.mult))
            link(ve.tensor_tensor(half, m0, m1, ALU.subtract))
            link(ve.scalar_tensor_tensor(out=half, in0=half, scalar=0.25, in1=half, op0=ALU.mult, op1=ALU.mult))
            link(ve.tensor_tensor(t1, v0, v1, ALU.add))
            link(ve.scalar_tensor_tensor(out=t1, in0=t1, scalar=1.0 / D, in1=half, op0=ALU.mult, op1=ALU.add))
            ve.tensor_scalar(rstd[:, :, 0], t1, EPS, None, ALU.add).then_inc(sem("var"), 1)
            dve.wait_ge(sem("std"), 1 + done(L, "std"))
            link(ve.reciprocal(rstd[:, :, 0], rstd[:, :, 0]))

        def norm_act(act, L):
            act.wait_ge(sem("var"), 1 + done(L, "var"))
            nc.scalar.activation(rstd[:, :, 0], rstd[:, :, 0], ACT.Sqrt).then_inc(sem("std"), 1)

        BW = carve([("xn", (B, D)), ("xnT", (DC, B * P)), ("hT", (FC, B * P)), ("tmp", (B, D)), ("q", (DC * F0,))])

        def ffn_setup_dve(dve):
            link, ve = chain_dve.link, nc.vector
            dve.wait_ge(sem("B_in"), LOADS["B"])
            for k, name in enumerate(("fc", "proj")):
                w = pk["B"][name]
                mxp, scale = small[:, 300 + k:301 + k], small[:, 302 + k:303 + k]
                ve.tensor_reduce(mxp, w, AX.X, ALU.max, apply_absolute_value=True).then_inc(sem("B_absmax"), 1)
            for k, name in enumerate(("fc", "proj")):
                w = pk["B"][name]
                mxa, scale = small[:, 304 + k:305 + k], small[:, 302 + k:303 + k]
                rs = small[:, 306 + k:307 + k]
                dve.wait_ge(sem("B_allmax"), k + 1)
                link(ve.tensor_scalar(scale, mxa, 1.0 / 127.0, None, ALU.mult))
                link(ve.reciprocal(rs, scale))
                q = BW["q"]
                link(ve.tensor_scalar(q, w, rs, MAGIC, ALU.mult, ALU.add))
                link(ve.tensor_scalar(q, q, MAGIC, 127.0, ALU.subtract, ALU.min))
                link(ve.tensor_scalar(q, q, -128.0, scale, ALU.max, ALU.mult))
                link(ve.tensor_tensor(q, q, w, ALU.subtract))
                link(ve.tensor_tensor(w, w, q, ALU.add))
                dve.wait_ge(sem("B_lora"), 1)
                src = ps[:, 4 * k:4 * k + 4, :].rearrange("p k n -> p (k n)")
                link(ve.scalar_tensor_tensor(out=w, in0=src, scalar=2.0, in1=w, op0=ALU.mult, op1=ALU.add))
            dve.sem_inc(sem("B_weights"), 1)

        def ffn_setup_pool(pool):
            for k in range(2):
                pool.wait_ge(sem("B_absmax"), k + 1)
                nc.gpsimd.partition_all_reduce(small[:, 304 + k:305 + k], small[:, 300 + k:301 + k], P,
                                               bass.bass_isa.ReduceOp.max).then_inc(sem("B_allmax"), 1)

        def ffn_pe(pe):
            w, lo = pk["B"], pk["lora"]
            pe.wait_ge(sem("B_in"), LOADS["B"])
            pe.wait_ge(sem("x_new"), NT + done("A", "x_new"))
            for c in range(DC):
                for n in range(F0 // 512):
                    nc.tensor.matmul(ps[:, c * 2 + n, :], lo["afc"][:, c * P:(c + 1) * P],
                                     lo["bfcT"][:, n * 512:(n + 1) * 512], start=True, stop=True)
            for f in range(FC):
                mm = nc.tensor.matmul(ps[:, 4 + f // 2, f % 2 * D:(f % 2 + 1) * D], lo["aproj"][:, f * P:(f + 1) * P],
                                      lo["bprojT"], start=True, stop=True)
            mm.then_inc(sem("B_lora"), 1)
            pe.wait_ge(sem("B_weights"), 1)
            with pe.Fori(0, HT) as i:
                for b in range(B):
                    pe.wait_ge(sem("xn_ready"), nth(i, B, b) + done("B", "xn_ready"))
                    for c in range(DC):
                        mm = nc.tensor.transpose(ps[:, 0, c * D + b * P:c * D + (b + 1) * P],
                                                 BW["xn"][:, b, c * P:(c + 1) * P], ident)
                mm.then_inc(sem("xT_ps"), 1)
                pe.wait_ge(sem("xT_ready"), nth(i, 1, 0) + done("B", "xT_ready"))
                for f in range(FC):
                    for c in range(DC):
                        mm = nc.tensor.matmul(ps[:, 1 + f // 2, f % 2 * D:(f % 2 + 1) * D],
                                              w["fc"][:, c * F0 + f * P:c * F0 + (f + 1) * P], BW["xnT"][:, c, :],
                                              start=c == 0, stop=c == DC - 1)
                    if f % 2:
                        mm.then_inc(sem("B_h_ps"), 1)
                for b in range(B):
                    for f in range(FC):
                        if b == 0:
                            pe.wait_ge(sem("B_h_ready"), nth(i, FC, f))
                        mm = nc.tensor.matmul(ps[:, 5 + b, 0:D], BW["hT"][:, f, b * P:(b + 1) * P],
                                              w["proj"][:, f * D:(f + 1) * D], start=f == 0, stop=f == FC - 1)
                    mm.then_inc(sem("y_ps"), 1)

        def ffn_act(act):
            with act.Fori(0, HT) as i:
                act.wait_ge(sem("xT_ps"), nth(i, 1, 0) + done("B", "xT_ps"))
                nc.scalar.copy(BW["xnT"], ps[:, 0, :].rearrange("p (c n) -> p c n", c=DC)).then_inc(sem("xT_ready"), 1)
                for f in range(FC):
                    act.wait_ge(sem("B_h_ps"), nth(i, FC // 2, f // 2))
                    nc.scalar.activation(BW["hT"][:, f, :], ps[:, 1 + f // 2, f % 2 * D:(f % 2 + 1) * D], ACT.Gelu,
                                         bias=pk["B"]["bfc"][:, f:f + 1]).then_inc(sem("B_h_ready"), 1)

        def ffn_dve(dve):
            with dve.Fori(0, HT) as i:
                chain_dve.begin(i, 4)
                for b in range(B):
                    t = i + b * HT
                    nc.vector.tensor_scalar(BW["xn"][:, b, :], x[:, t, :], mean[:, t, :], rstd[:, t, :],
                                            ALU.subtract, ALU.mult).then_inc(sem("xn_ready"), 1)
                for b in range(B):
                    dve.wait_ge(sem("y_ps"), nth(i, B, b) + done("B", "y_ps"))
                    finish(i + b * HT, ps[:, 5 + b, 0:D], rw["B"]["bproj"], 4, BW["tmp"][:, b, :], sem("x_new"))
            chain_dve.end(HT)

        CW = carve([("xn", (B, D)), ("xnT", (DC, B * P)), ("hidT", (B * P,)), ("RT", (DC, B * P)), ("hot", (B, WIN, SC)),
                    ("prod", (B, WIN, SC)), ("a", (B, SC)), ("aT", (B * P,)), ("pos", (6, B)), ("w4", (6, B, WIN))])

        def local_pe(pe):
            w = pk["C"]
            pe.wait_ge(sem("C_in"), LOADS["C"])
            with pe.Fori(0, HT) as i:
                for b in range(B):
                    pe.wait_ge(sem("xn_ready"), nth(i, B, b) + done("C", "xn_ready"))
                    for c in range(DC):
                        mm = nc.tensor.transpose(ps[:, 0, c * D + b * P:c * D + (b + 1) * P],
                                                 CW["xn"][:, b, c * P:(c + 1) * P], ident)
                mm.then_inc(sem("xT_ps"), 1)
                pe.wait_ge(sem("xT_ready"), nth(i, 1, 0) + done("C", "xT_ready"))
                for c in range(DC):
                    mm = nc.tensor.matmul(ps[0:PSZ, 1, 0:B * P], w["wp"][:, c * PSZ:(c + 1) * PSZ], CW["xnT"][:, c, :],
                                          start=c == 0, stop=c == DC - 1)
                mm.then_inc(sem("C_hid_ps"), 1)
                for co in range(DC):
                    for ci in range(DC):
                        mm = nc.tensor.matmul(ps[:, 2, co * D:(co + 1) * D],
                                              w["wa"][:, ci * D + co * P:ci * D + (co + 1) * P], CW["xnT"][:, ci, :],
                                              start=ci == 0, stop=ci == DC - 1)
                mm.then_inc(sem("C_R_ps"), 1)
                pe.wait_ge(sem("C_hid_ready"), nth(i, 1, 0))
                for b in range(B):
                    mm = nc.tensor.matmul(ps[:, 4, b:b + 1], CW["hidT"][0:PSZ, b * P:(b + 1) * P], w["vp"][0:PSZ, :],
                                          start=True, stop=True)
                mm.then_inc(sem("C_z_ps"), 1)
                pe.wait_ge(sem("C_R_ready"), nth(i, 1, 0))
                for b in range(B):
                    for c in range(DC):
                        mm = nc.tensor.matmul(ps[:, 3, b * SC:(b + 1) * SC], CW["RT"][:, c, b * P:(b + 1) * P],
                                              ctxT[:, c, b * SC:(b + 1) * SC], start=c == 0, stop=c == DC - 1)
                mm.then_inc(sem("s_ps"), 1)
                pe.wait_ge(sem("a_ready"), nth(i, 1, 0) + done("C", "a_ready"))
                for b in range(B):
                    mm = nc.tensor.transpose(ps[0:SC, 5, b * P:(b + 1) * P], CW["a"][:, b, :], ident)
                mm.then_inc(sem("aT_ps"), 1)
                pe.wait_ge(sem("aT_ready"), nth(i, 1, 0) + done("C", "aT_ready"))
                for b in range(B):
                    nc.tensor.matmul(ps[:, 6 + b, 0:D], CW["aT"][0:SC, b * P:(b + 1) * P], ctxN[:, b, :],
                                     start=True, stop=True).then_inc(sem("y_ps"), 1)

        def local_act(act):
            pos, w4 = CW["pos"], CW["w4"]
            with act.Fori(0, HT) as i:
                act.wait_ge(sem("xT_ps"), nth(i, 1, 0) + done("C", "xT_ps"))
                nc.scalar.copy(CW["xnT"], ps[:, 0, :].rearrange("p (c n) -> p c n", c=DC)).then_inc(sem("xT_ready"), 1)
                act.wait_ge(sem("C_hid_ps"), nth(i, 1, 0))
                nc.scalar.activation(CW["hidT"][0:PSZ, :], ps[0:PSZ, 1, 0:B * P], ACT.Tanh).then_inc(sem("C_hid_ready"), 1)
                act.wait_ge(sem("C_R_ps"), nth(i, 1, 0))
                nc.scalar.copy(CW["RT"], ps[:, 2, :].rearrange("p (c n) -> p c n", c=DC)).then_inc(sem("C_R_ready"), 1)
                act.wait_ge(sem("C_z_ps"), nth(i, 1, 0))
                nc.scalar.activation(pos[:, 0, :], ps[:, 4, 0:B], ACT.Exp, scale=-1.0).then_inc(sem("C_ez_ready"), 1)
                act.wait_ge(sem("C_d2_ready"), nth(i, 1, 0))
                nc.scalar.activation(w4[:, 2], w4[:, 1], ACT.Exp, scale=-0.5).then_inc(sem("C_gauss_ready"), 1)
                act.wait_ge(sem("C_sc_ready"), nth(i, 1, 0))
                nc.scalar.activation(w4[:, 4], w4[:, 3], ACT.Exp).then_inc(sem("C_e_ready"), 1)
                act.wait_ge(sem("aT_ps"), nth(i, 1, 0) + done("C", "aT_ps"))
                nc.scalar.copy(CW["aT"][0:SC, :], ps[0:SC, 5, 0:B * P]).then_inc(sem("aT_ready"), 1)

        def local_dve(dve):
            link, ve = chain_dve.link, nc.vector
            pos, w4 = CW["pos"], CW["w4"]
            hot, prod = CW["hot"], CW["prod"]
            iota = pk["C"]["iota"].rearrange("p (o s) -> p o s", o=1)
            woff = pk["C"]["woff"].rearrange("p (o w) -> p o w", o=1)

            def per_tok(v):
                return v.rearrange("p (b o) -> p b o", o=1).to_broadcast([P, B, WIN])

            def over_s(v):
                return v.rearrange("p b (w o) -> p (b w) o", o=1).to_broadcast([P, B * WIN, SC])

            flat = lambda v: v.rearrange("p b w s -> p (b w) s")
            dve.wait_ge(sem("C_in"), LOADS["C"])
            with dve.Fori(0, HT) as i:
                chain_dve.begin(i, 20 + 2)
                for b in range(B):
                    t = i + b * HT
                    ve.tensor_scalar(CW["xn"][:, b, :], x[:, t, :], mean[:, t, :], rstd[:, t, :],
                                     ALU.subtract, ALU.mult).then_inc(sem("xn_ready"), 1)
                dve.wait_ge(sem("C_ez_ready"), nth(i, 1, 0))
                link(ve.tensor_scalar(pos[:, 0, :], pos[:, 0, :], 1.0, None, ALU.add))
                link(ve.reciprocal(pos[:, 0, :], pos[:, 0, :]))
                link(ve.tensor_scalar(pos[:, 1, :], pos[:, 0, :], float(SC), None, ALU.mult))
                link(ve.tensor_scalar(pos[:, 2, :], pos[:, 1, :], MAGIC, None, ALU.add))
                link(ve.tensor_scalar(pos[:, 2, :], pos[:, 2, :], MAGIC, None, ALU.subtract))
                link(ve.tensor_tensor(pos[:, 3, :], pos[:, 2, :], pos[:, 1, :], ALU.is_gt))
                link(ve.tensor_tensor(pos[:, 2, :], pos[:, 2, :], pos[:, 3, :], ALU.subtract))
                link(ve.tensor_tensor(w4[:, 0], per_tok(pos[:, 2, :]), woff.to_broadcast([P, B, WIN]), ALU.add))
                link(ve.tensor_scalar(w4[:, 0], w4[:, 0], 0.0, float(SC - 1), ALU.max, ALU.min))
                link(ve.tensor_tensor(w4[:, 1], w4[:, 0], per_tok(pos[:, 1, :]), ALU.subtract))
                ve.tensor_tensor(w4[:, 1], w4[:, 1], w4[:, 1], ALU.mult).then_inc(sem("C_d2_ready"), 1)
                link(ve.tensor_tensor(flat(hot), iota.to_broadcast([P, B * WIN, SC]), over_s(w4[:, 0]), ALU.is_equal))
                dve.wait_ge(sem("s_ps"), nth(i, 1, 0) + done("C", "s_ps"))
                for b in range(B):
                    s_b = ps[:, 3, b * SC:(b + 1) * SC].rearrange("p (o s) -> p o s", o=1)
                    link(ve.tensor_tensor(prod[:, b], hot[:, b], s_b.to_broadcast([P, WIN, SC]), ALU.mult))
                link(ve.tensor_reduce(w4[:, 3].rearrange("p b w -> p (b w)"), flat(prod), AX.X, ALU.add))
                link(ve.tensor_reduce(pos[:, 4, :], w4[:, 3], AX.X, ALU.max))
                ve.tensor_tensor(w4[:, 3], w4[:, 3], per_tok(pos[:, 4, :]), ALU.subtract).then_inc(sem("C_sc_ready"), 1)
                dve.wait_ge(sem("C_e_ready"), nth(i, 1, 0))
                link(ve.tensor_reduce(pos[:, 5, :], w4[:, 4], AX.X, ALU.add))
                link(ve.reciprocal(pos[:, 5, :], pos[:, 5, :]))
                dve.wait_ge(sem("C_gauss_ready"), nth(i, 1, 0))
                link(ve.tensor_tensor(w4[:, 5], w4[:, 4], w4[:, 2], ALU.mult))
                link(ve.tensor_tensor(w4[:, 5], w4[:, 5], per_tok(pos[:, 5, :]), ALU.mult))
                link(ve.tensor_tensor(flat(prod), flat(hot), over_s(w4[:, 5]), ALU.mult))
                ve.tensor_reduce(CW["a"], prod.rearrange("p b w s -> p b s w"), AX.X, ALU.add).then_inc(sem("a_ready"), 1)
                for b in range(B):
                    dve.wait_ge(sem("y_ps"), nth(i, B, b) + done("C", "y_ps"))
                    finish(i + b * HT, ps[:, 6 + b, 0:D], None, 1, None, sem("x_new"))
            chain_dve.end(HT)

        EW = carve([("xn", (B, D)), ("xnT", (DC, B * P)), ("hqT", (DC, B * P)), ("ehT", (DC, B * P)), ("p", (B, SC)),
                    ("aT", (B * P,)), ("RT", (DC, B * SC)), ("simrow", (B * SC,)), ("sim", (NT, SC)), ("mx", (NT, 1)),
                    ("wgt", (NT,)), ("m", (2, B)), ("hc", (DC, B)), ("sum", (2, B, 1)), ("w14", (B, DC, D)), ("tmp", (B, D))])

        def sim_pe(pe):
            w = pk["E"]
            pe.wait_ge(sem("E_in"), LOADS["E"])
            pe.wait_ge(sem("E_setup"), 1)
            for c in range(DC):
                mm = nc.tensor.matmul(ps[0:1, 7, 0:B * SC], w["w2"][:, c:c + 1], ctxT[:, c, :], start=c == 0, stop=c == DC - 1)
            mm.then_inc(sem("E_row_ps"), 1)
            pe.wait_ge(sem("E_row_ready"), 1)
            with pe.Fori(0, HT) as i:
                for b in range(B):
                    pe.wait_ge(sem("xn_ready"), nth(i, B, b) + done("E", "xn_ready"))
                    for c in range(DC):
                        mm = nc.tensor.transpose(ps[:, 0, c * D + b * P:c * D + (b + 1) * P],
                                                 EW["xn"][:, b, c * P:(c + 1) * P], ident)
                mm.then_inc(sem("xT_ps"), 1)
                pe.wait_ge(sem("xT_ready"), nth(i, 1, 0) + done("E", "xT_ready"))
                for b in range(B):
                    for c in range(DC):
                        nc.tensor.matmul(ps[:, 1 + b, 0:SC], EW["xnT"][:, c, b * P:(b + 1) * P],
                                         EW["RT"][:, c, b * SC:(b + 1) * SC], start=c == 0, stop=False)
                    nc.tensor.matmul(ps[:, 1 + b, 0:SC], ones[0:1, :], EW["simrow"][0:1, b * SC:(b + 1) * SC],
                                     start=False, stop=True).then_inc(sem("s_ps"), 1)
            pe.wait_ge(sem("E_wgt_ready"), 1)
            pe.wait_ge(sem("E_h_kept"), NT)
            for b in range(B):
                for c in range(DC):
                    for t in range(HT):
                        nc.tensor.matmul(ps[:, 3, c * B + b:c * B + b + 1], hall[:, b * HT + t, c * P:(c + 1) * P],
                                         EW["wgt"][:, b * HT + t:b * HT + t + 1], start=t == 0, stop=t == HT - 1)
                for t in range(HT):
                    mm = nc.tensor.matmul(ps[:, 4, b:b + 1], ones, EW["wgt"][:, b * HT + t:b * HT + t + 1],
                                          start=t == 0, stop=t == HT - 1)
            mm.then_inc(sem("E_hc_ps"), 1)
            pe.wait_ge(sem("E_w14_ready"), 1)
            with pe.Fori(0, HT) as i:
                for b in range(B):
                    pe.wait_ge(sem("E_h_back"), nth(i, B, b))
                    for c in range(DC):
                        mm = nc.tensor.transpose(ps[:, 0, c * D + b * P:c * D + (b + 1) * P],
                                                 EW["xn"][:, b, c * P:(c + 1) * P], ident)
                mm.then_inc(sem("E_xT2_ps"), 1)
                pe.wait_ge(sem("a_ready"), nth(i, 1, 0) + done("E", "a_ready"))
                for b in range(B):
                    mm = nc.tensor.transpose(ps[0:SC, 1, b * P:(b + 1) * P], EW["p"][:, b, :], ident)
                mm.then_inc(sem("aT_ps"), 1)
                pe.wait_ge(sem("aT_ready"), nth(i, 1, 0) + done("E", "aT_ready"))
                for c in range(DC):
                    for b in range(B):
                        mm = nc.tensor.matmul(ps[:, 2, c * D + b * P:c * D + (b + 1) * P], ctxN[:, b, c * P:(c + 1) * P],
                                              EW["aT"][0:SC, b * P:(b + 1) * P], start=True, stop=True)
                mm.then_inc(sem("E_hq_ps"), 1)
                pe.wait_ge(sem("E_xT2_ready"), nth(i, 1, 0))
                for b in range(B):
                    for c in range(DC):
                        nc.tensor.matmul(ps[:, 5 + b, 0:D], EW["xnT"][:, c, b * P:(b + 1) * P], EW["w14"][:, b, c, :],
                                         start=c == 0, stop=False)
                pe.wait_ge(sem("E_hq_ready"), nth(i, 1, 0))
                for b in range(B):
                    for c in range(DC):
                        nc.tensor.matmul(ps[:, 5 + b, 0:D], EW["hqT"][:, c, b * P:(b + 1) * P],
                                         w["wqv"][:, (DC + c) * D:(DC + c + 1) * D], start=False, stop=False)
                pe.wait_ge(sem("E_eh_ready"), nth(i, 1, 0))
                for b in range(B):
                    for c in range(DC):
                        mm = nc.tensor.matmul(ps[:, 5 + b, 0:D], EW["ehT"][:, c, b * P:(b + 1) * P],
                                              w["wqv"][:, (2 * DC + c) * D:(2 * DC + c + 1) * D],
                                              start=False, stop=c == DC - 1)
                    mm.then_inc(sem("y_ps"), 1)

        def sim_pool(pool):
            with pool.Fori(0, HT) as i:
                for b in range(B):
                    pool.wait_ge(sem("xn_ready"), nth(i, B, b) + done("E", "xn_ready"))
                    nc.gpsimd.tensor_copy(hall[:, i + b * HT, :], EW["xn"][:, b, :]).then_inc(sem("E_h_kept"), 1)
            pool.wait_ge(sem("E_m_ready"), 1)
            nc.gpsimd.partition_all_reduce(EW["m"][:, 1, :], EW["m"][:, 0, :], P,
                                           bass.bass_isa.ReduceOp.max).then_inc(sem("E_mall_ready"), 1)
            pool.wait_ge(sem("E_h_kept"), NT)
            pool.wait_ge(sem("E_hc_ps"), 1)
            for i in (0,):
                for b in range(B):
                    nc.gpsimd.tensor_copy(EW["xn"][:, b, :], hall[:, i + b * HT, :]).then_inc(sem("E_h_back"), 1)
            with pool.Fori(1, HT) as i:
                for b in range(B):
                    pool.wait_ge(sem("E_xT2_ps"), i)
                    nc.gpsimd.tensor_copy(EW["xn"][:, b, :], hall[:, i + b * HT, :]).then_inc(sem("E_h_back"), 1)

        def sim_act(act):
            with act.Fori(0, HT) as i:
                act.wait_ge(sem("xT_ps"), nth(i, 1, 0) + done("E", "xT_ps"))
                nc.scalar.copy(EW["xnT"], ps[:, 0, :].rearrange("p (c n) -> p c n", c=DC)).then_inc(sem("xT_ready"), 1)
            act.wait_ge(sem("E_wsub_ready"), 1)
            nc.scalar.activation(EW["wgt"], EW["wgt"], ACT.Exp).then_inc(sem("E_wgt_ready"), 1)
            act.wait_ge(sem("E_sim_ready"), NT)
            with act.Fori(0, HT) as i:
                for b in range(B):
                    t = i + b * HT
                    if b == 0:
                        act.wait_ge(sem("E_p_free"), nth(i, 1, 0))
                    nc.scalar.activation(EW["p"][:, b, :], EW["sim"][:, t, :], ACT.Exp,
                                         accum_out=EW["sum"][:, 0, b, :]).then_inc(sem("p_ready"), 1)
                act.wait_ge(sem("E_xT2_ps"), nth(i, 1, 0))
                nc.scalar.copy(EW["xnT"], ps[:, 0, :].rearrange("p (c n) -> p c n", c=DC)).then_inc(sem("E_xT2_ready"), 1)
                act.wait_ge(sem("aT_ps"), nth(i, 1, 0) + done("E", "aT_ps"))
                nc.scalar.copy(EW["aT"][0:SC, :], ps[0:SC, 1, 0:B * P]).then_inc(sem("aT_ready"), 1)
                act.wait_ge(sem("E_hq_ps"), nth(i, 1, 0))
                nc.scalar.copy(EW["hqT"], ps[:, 2, :].rearrange("p (c n) -> p c n", c=DC)).then_inc(sem("E_hq_ready"), 1)

        def sim_dve(dve):
            link, ve = chain_dve.link, nc.vector
            w = pk["E"]
            dve.wait_ge(sem("E_in"), LOADS["E"])
            for c in range(DC):
                link(ve.tensor_scalar(EW["RT"][:, c, :], ctxT[:, c, :], w["w3"][:, c:c + 1], w["w1"][:, c:c + 1],
                                      ALU.mult, ALU.add))
            dve.sem_inc(sem("E_setup"), 1)
            dve.wait_ge(sem("E_row_ps"), 1)
            ve.tensor_scalar(EW["simrow"][0:1, :], ps[0:1, 7, 0:B * SC], rw["E"]["bsim"][0:1, :], None,
                             ALU.add).then_inc(sem("E_row_ready"), 1)
            norm_dve(dve, "E")
            with dve.Fori(0, HT) as i:
                chain_dve.begin(i, 2)
                for b in range(B):
                    t = i + b * HT
                    ve.tensor_scalar(EW["xn"][:, b, :], x[:, t, :], mean[:, t, :], rstd[:, t, :],
                                     ALU.subtract, ALU.mult).then_inc(sem("xn_ready"), 1)
                for b in range(B):
                    t = i + b * HT
                    dve.wait_ge(sem("s_ps"), nth(i, B, b) + done("E", "s_ps"))
                    link(ve.tensor_reduce(EW["mx"][:, t, :], ps[:, 1 + b, 0:SC], AX.X, ALU.max))
                    ve.tensor_scalar(EW["sim"][:, t, :], ps[:, 1 + b, 0:SC], EW["mx"][:, t, :], None,
                                     ALU.subtract).then_inc(sem("E_sim_ready"), 1)
                dve.wait_ge(sem("E_h_kept"), nth(i, B, B - 1))
            chain_dve.end(HT)
            mx = EW["mx"].rearrange("p (b t) o -> p b (t o)", b=B)
            wgt = EW["wgt"].rearrange("p (b t) -> p b t", b=B)
            ve.tensor_reduce(EW["m"][:, 0, :], mx, AX.X, ALU.max).then_inc(sem("E_m_ready"), 1)
            dve.wait_ge(sem("E_mall_ready"), 1)
            ve.tensor_tensor(wgt, mx, EW["m"][:, 1, :].rearrange("p (b o) -> p b o", o=1).to_broadcast([P, B, HT]),
                             ALU.subtract).then_inc(sem("E_wsub_ready"), 1)
            dve.wait_ge(sem("E_hc_ps"), 1)
            link(ve.reciprocal(EW["m"][:, 0, :], ps[:, 4, 0:B]))
            link(ve.tensor_tensor(EW["hc"], ps[:, 3, 0:DC * B].rearrange("p (c b) -> p c b", c=DC),
                                  EW["m"][:, 0, :].rearrange("p (o b) -> p o b", o=1).to_broadcast([P, DC, B]), ALU.mult))
            for b in range(B):
                for c in range(DC):
                    link(ve.scalar_tensor_tensor(out=EW["w14"][:, b, c, :], in0=w["wqv"][:, (3 * DC + c) * D:(3 * DC + c + 1) * D],
                                                 scalar=EW["hc"][:, c, b:b + 1], in1=w["wqv"][:, c * D:(c + 1) * D],
                                                 op0=ALU.mult, op1=ALU.add))
            dve.sem_inc(sem("E_w14_ready"), 1)
            dve.sem_inc(sem("E_p_free"), 1)
            with dve.Fori(0, HT) as i:
                chain_dve.begin(i, 2 + 2 * 2)
                for b in range(B):
                    dve.wait_ge(sem("p_ready"), nth(i, B, b) + done("E", "p_ready"))
                    link(ve.reciprocal(EW["sum"][:, 1, b, :], EW["sum"][:, 0, b, :]))
                    a = ve.tensor_scalar(EW["p"][:, b, :], EW["p"][:, b, :], EW["sum"][:, 1, b, :], None, ALU.mult)
                    if b == B - 1:
                        a.then_inc(sem("a_ready"), 1)
                dve.wait_ge(sem("E_hq_ready"), nth(i, 1, 0))
                ve.tensor_tensor(EW["ehT"], EW["xnT"], EW["hqT"], ALU.mult).then_inc(sem("E_eh_ready"), 1)
                for b in range(B):
                    dve.wait_ge(sem("y_ps"), nth(i, B, b) + done("E", "y_ps"))
                    finish(i + b * HT, ps[:, 5 + b, 0:D], rw["E"]["bqv"], 2, EW["tmp"][:, b, :], sem("x_new"))
                dve.sem_inc(sem("E_p_free"), 1)
            chain_dve.end(HT)

        GW = carve([("xn", (B, D)), ("xnT", (DC, B * P)), ("f", (DC, P)), ("i", (DC, P)), ("g", (DC, P)), ("c1", (DC, P)),
                    ("c2", (DC, P)), ("y", (B, D)), ("bias", (2, 3 * DC)), ("c0", (DC,))])
        GATES = ("f", "i", "g")

        def rnn_pe(pe):
            w = pk["F"]
            pe.wait_ge(sem("F_in"), LOADS["F"])
            pe.wait_ge(sem("x_new"), NT + done("E", "x_new"))
            for g in range(3):
                for co in range(DC):
                    for ci in range(DC):
                        mm = nc.tensor.matmul(ps[:, 7, g * DC + co:g * DC + co + 1],
                                              w["u" + "fic"[g]][:, ci * D + co * P:ci * D + (co + 1) * P],
                                              w["c0"][:, ci:ci + 1], start=ci == 0, stop=ci == DC - 1)
            mm.then_inc(sem("F_u0_ps"), 1)
            with pe.Fori(0, HT) as i:
                for b in range(B):
                    pe.wait_ge(sem("xn_ready"), nth(i, B, b) + done("F", "xn_ready"))
                    for c in range(DC):
                        mm = nc.tensor.transpose(ps[:, 0, c * D + b * P:c * D + (b + 1) * P],
                                                 GW["xn"][:, b, c * P:(c + 1) * P], ident)
                mm.then_inc(sem("xT_ps"), 1)
                pe.wait_ge(sem("xT_ready"), nth(i, 1, 0) + done("F", "xT_ready"))
                for b in range(B):
                    if b == 1:
                        pe.wait_ge(sem("F_c1_ready"), nth(i, 1, 0))
                    for g in range(3):
                        for co in range(DC):
                            o = ps[:, 1 + 3 * b + g, co * P:(co + 1) * P]
                            for ci in range(DC):
                                mm = nc.tensor.matmul(o, w["w" + "fic"[g]][:, ci * D + co * P:ci * D + (co + 1) * P],
                                                      GW["xnT"][:, ci, b * P:(b + 1) * P], start=ci == 0,
                                                      stop=b == 0 and ci == DC - 1)
                            if b == 1:
                                for ci in range(DC):
                                    mm = nc.tensor.matmul(o, w["u" + "fic"[g]][:, ci * D + co * P:ci * D + (co + 1) * P],
                                                          GW["c1"][:, ci, :], start=False, stop=ci == DC - 1)
                        mm.then_inc(sem("F_z_ps"), 1)
                pe.wait_ge(sem("F_c2_ready"), nth(i, 1, 0))
                for b in range(B):
                    o = ps[:, 7, b * D:(b + 1) * D]
                    for ci in range(DC):
                        nc.tensor.matmul(o, GW["xnT"][:, ci, b * P:(b + 1) * P], w["wo"][:, ci * D:(ci + 1) * D],
                                         start=ci == 0, stop=False)
                    for ci in range(DC):
                        mm = nc.tensor.matmul(o, GW["c2"][:, ci, :], w["uo"][:, ci * D:(ci + 1) * D],
                                              start=False, stop=ci == DC - 1)
                mm.then_inc(sem("y_ps"), 1)

        def rnn_act(act):
            with act.Fori(0, HT) as i:
                act.wait_ge(sem("xT_ps"), nth(i, 1, 0) + done("F", "xT_ps"))
                nc.scalar.copy(GW["xnT"], ps[:, 0, :].rearrange("p (c n) -> p c n", c=DC)).then_inc(sem("xT_ready"), 1)
                for b in range(B):
                    for g in range(3):
                        act.wait_ge(sem("F_z_ps"), nth(i, B * 3, b * 3 + g))
                        for co in range(DC):
                            a = nc.scalar.activation(GW[GATES[g]][:, co, :], ps[:, 1 + 3 * b + g, co * P:(co + 1) * P],
                                                     ACT.Tanh, bias=GW["bias"][:, b, g * DC + co:g * DC + co + 1],
                                                     scale=0.5 if g < 2 else 1.0)
                        a.then_inc(sem("F_gate_ready"), 1)
                act.wait_ge(sem("F_ysum_ready"), nth(i, 1, 0))
                nc.scalar.activation(GW["y"], GW["y"], ACT.Tanh).then_inc(sem("F_h_ready"), 1)

        def rnn_dve(dve):
            link, ve = chain_dve.link, nc.vector
            w = pk["F"]
            dve.wait_ge(sem("F_in"), LOADS["F"])
            dve.wait_ge(sem("F_u0_ps"), 1)
            b0, b1 = GW["bias"][:, 0, :], GW["bias"][:, 1, :]
            link(ve.tensor_tensor(b0, ps[:, 7, 0:3 * DC], w["bias"], ALU.add))
            link(ve.tensor_scalar(GW["bias"][:, 0, 0:2 * DC], GW["bias"][:, 0, 0:2 * DC], 0.5, None, ALU.mult))
            link(ve.tensor_scalar(GW["bias"][:, 1, 0:2 * DC], w["bias"][:, 0:2 * DC], 0.5, None, ALU.mult))
            link(ve.tensor_copy(GW["bias"][:, 1, 2 * DC:3 * DC], w["bias"][:, 2 * DC:3 * DC]))
            norm_dve(dve, "F")
            with dve.Fori(0, HT) as i:
                chain_dve.begin(i, 3 + 3 + 2)
                for b in range(B):
                    t = i + b * HT
                    ve.tensor_scalar(GW["xn"][:, b, :], x[:, t, :], mean[:, t, :], rstd[:, t, :],
                                     ALU.subtract, ALU.mult).then_inc(sem("xn_ready"), 1)
                for b in range(B):
                    dve.wait_ge(sem("F_gate_ready"), nth(i, B * 3, b * 3 + 2))
                    fi = GW["f"].rearrange("p c n -> p (c n)"), GW["i"].rearrange("p c n -> p (c n)")
                    both = work[:, FI_AT:FI_AT + 4 * P]
                    link(ve.tensor_scalar(both, both, 0.5, 0.5, ALU.mult, ALU.add))
                    link(ve.tensor_tensor(GW["i"], GW["i"], GW["g"], ALU.mult))
                    if b == 0:
                        for c in range(DC):
                            last = ve.scalar_tensor_tensor(out=GW["c1"][:, c, :], in0=GW["f"][:, c, :], scalar=w["c0"][:, c:c + 1],
                                                           in1=GW["i"][:, c, :], op0=ALU.mult, op1=ALU.add)
                            if c < DC - 1:
                                link(last)
                        last.then_inc(sem("F_c1_ready"), 1)
                    else:
                        link(ve.tensor_tensor(GW["c2"], GW["f"], GW["c1"], ALU.mult))
                        ve.tensor_tensor(GW["c2"], GW["c2"], GW["i"], ALU.add).then_inc(sem("F_c2_ready"), 1)
                dve.wait_ge(sem("y_ps"), nth(i, 1, 0) + done("F", "y_ps"))
                ve.tensor_tensor(GW["y"], ps[:, 7, :].rearrange("p (b d) -> p b d", b=B),
                                 rw["F"]["bo"].rearrange("p (o d) -> p o d", o=1).to_broadcast([P, B, D]),
                                 ALU.add).then_inc(sem("F_ysum_ready"), 1)
                dve.wait_ge(sem("F_h_ready"), nth(i, 1, 0))
                for b in range(B):
                    finish(i + b * HT, GW["y"][:, b, :], None, 6, None, sem("x_new"))
            chain_dve.end(HT)

        FI_AT = B * D + DC * B * P

        NG = 2 * B
        RT = carve([("s", (NG, HT)), ("u", (NG, HT)), ("y", (NG, HT)), ("e", (NG, HT)), ("sc", (NG, HT)), ("n", (NG, HT)),
                    ("tie", (NG, HT)), ("sure", (NG, HT)), ("sel", (NG, HT)), ("pos", (NG, HT)), ("one", (NG, HT)),
                    ("a", (NG,)), ("m", (NG,)), ("um", (NG,)), ("ym", (NG,)), ("tot", (NG,)), ("ln", (NG,)), ("gm", (NG,)),
                    ("logk", (NG,)), ("k", (NG,)), ("gstar", (NG,)), ("pmax", (NG,)),
                    ("ssq", (NT, 1)), ("aux", (NT, 3)), ("unsel", (NT, 1)), ("rmsg", (DC,))], route)
        s_cols = RT["s"].rearrange("p g (t o) -> p (g t) o", o=1)
        pos_cols = RT["pos"].rearrange("p g (t o) -> p (g t) o", o=1)
        flat32 = lambda v: v.rearrange("p g t -> p (g t)")

        def over_t(v):
            return v.rearrange("p (g o) -> p g o", o=1).to_broadcast([P, NG, HT])

        SPAN = S + P
        LB = carve([("xnT", (DC, SPAN)), ("kT", (HC, SPAN)), ("v", (HT + 1, HDH))], big)
        LW = carve([("xn", (2, D)), ("q", (H8, P)), ("p", (2, 4, 2 * P)), ("pT", (2, 8 * P)), ("on", (2, D)), ("oT", (2, D)),
                    ("nm", (2, 4)), ("sum", (2, 4, 1)), ("rs", (2, 4)), ("junk", (D,)), ("h", (2, D))])
        HB = carve([("selq", (HT, NQ)), ("selk", (HT, NKV)), ("xqT", (DC, NQ)), ("xkT", (DC, NKV)), ("kT", (HC, NKV)),
                    ("v", (NKV // P, HDH))], big)
        RB = carve([("row", (NG, S))], big)
        HWK = carve([("qT", (HC, NQ)), ("selT", (2, S)), ("xg", (2, D)), ("p", (2, NKV)), ("pT", (2, NKV)), ("o", (HDH,)),
                     ("oT", (HC, P)), ("nm", (H8,)), ("m", (H8,)), ("sum", (H8, 1)), ("pn", (H8,)), ("rs", (H8,)), ("sn", (H8,)),
                     ("routed", (2, D)), ("aux", (6, 3)), ("t", (2, D)), ("pv", (HDH,)), ("scT", (P,))])

        def light_dve(dve):
            link, ve = chain_dve.link, nc.vector
            w, r = pk["D"], rw["D"]
            dve.wait_ge(sem("D_in"), LOADS["D"])
            with dve.Fori(0, NT // 2) as i:
                chain_dve.begin(i, 2 * 4)
                for j in range(2):
                    t = i * 2 + j
                    ve.tensor_scalar(hall[:, t, :], x[:, t, :], mean[:, t, :], rstd[:, t, :],
                                     ALU.subtract, ALU.mult).then_inc(sem("D_h_ready"), 1)
                    dve.wait_ge(sem("D_h_ready"), nth(i, 2, j))
                    link(ve.bn_stats(stats[:, t, :], hall[:, t, :]))
                    for k, rt in enumerate(("rtq", "rtkv")):
                        link(ve.scalar_tensor_tensor(out=LW["junk"], in0=hall[:, t, :], scalar=1.0, in1=r[rt],
                                                     op0=ALU.mult, op1=ALU.mult,
                                                     accum_out=s_cols[:, t + k * NT, :]))
                    link(ve.scalar_tensor_tensor(out=LW["junk"], in0=hall[:, t, :], scalar=1.0, in1=hall[:, t, :],
                                                 op0=ALU.mult, op1=ALU.mult, accum_out=RT["ssq"][:, t, :]))
            chain_dve.end(NT // 2)
            link(ve.memset(LB["xnT"][:, :, 0:P // 2], 0.0))
            link(ve.memset(LB["xnT"][:, :, SPAN - P // 2:SPAN], 0.0))
            link(ve.memset(LW["q"], 0.0))
            dve.sem_inc(sem("D_zeros"), 1)
            norm_dve(dve, "Dh")
            with dve.Fori(0, B) as b:
                with dve.Fori(0, HT // 2) as i2:
                    for j in range(2):
                        n = b * HT + i2 * 2 + j
                        ve.tensor_scalar(LW["xn"][:, j, :], hall[:, n, :], mean[:, n, :], rstd[:, n, :],
                                         ALU.subtract, ALU.mult).then_inc(sem("xn_ready"), 1)
                    dve.wait_ge(sem("xT_ps"), b * HT + i2 * 2 + 2 + done("D", "xT_ps"))
                for j in range(HT + 1):
                    dve.wait_ge(sem("D_v_ps"), nth(b, HT + 1, j))
                    ve.tensor_copy(LB["v"][:, j, :], ps[:, 1 + j % 6, :]).then_inc(sem("D_v_ready"), 1)
                with dve.Fori(0, HT) as i:
                    n = b * HT + i

                    def row_max(u):
                        dve.wait_ge(sem("s_ps"), nth(n, 2, u) + done("D", "s_ps"))
                        ve.tensor_reduce(LW["nm"][:, u, :], ps[:, 1 + 2 * u:3 + 2 * u, :].rearrange("p k (h s) -> p (k h) s", h=2),
                                         AX.X, ALU.max, negate=True).then_inc(sem("D_nm_ready"), 1)

                    def take_pT(u):
                        dve.wait_ge(sem("pT_ps"), nth(n, 2, u) + done("D", "pT_ps"))
                        ve.tensor_copy(LW["pT"][:, u, :].rearrange("p (k n) -> p k n", k=2),
                                       ps[:, 5:7, :]).then_inc(sem("pT_ready"), 1)

                    def normalise(u):
                        dve.wait_ge(sem("o_ps"), nth(n, 2, u) + done("D", "o_ps"))
                        ve.reciprocal(LW["rs"][:, u, :], LW["sum"][:, u, :, 0]).then_inc(sem("D_rs"), 1)
                        dve.wait_ge(sem("D_rs"), nth(n, 2, u))
                        ve.tensor_tensor(LW["on"][:, u, :].rearrange("p (h e) -> p h e", h=4),
                                         ps[:, 7, 0:D].rearrange("p (h e) -> p h e", h=4),
                                         LW["rs"][:, u, :].rearrange("p (h o) -> p h o", o=1).to_broadcast([P, 4, DH]),
                                         ALU.mult).then_inc(sem("on_ready"), 1)

                    row_max(0)
                    row_max(1)
                    take_pT(0)
                    normalise(0)
                    take_pT(1)
                    normalise(1)
                    dve.wait_ge(sem("y_ps"), nth(n, 1, 0) + done("D", "y_ps"))
                    ve.scalar_tensor_tensor(out=x[:, n, :], in0=ps[:, 0, 0:D], scalar=gates[:, 5:6], in1=x[:, n, :],
                                            op0=ALU.mult, op1=ALU.add).then_inc(sem("D_x_light"), 1)

        def light_act(act):
            w = pk["D"]
            with act.Fori(0, B) as b:
                with act.Fori(0, HT // 2) as i2:
                    for j in range(2):
                        n = b * HT + i2 * 2 + j
                        if j == 0:
                            act.wait_ge(sem("D_zeros"), 1)
                        act.wait_ge(sem("xT_ps"), n + 1 + done("D", "xT_ps"))
                        for c in range(DC):
                            a = nc.scalar.activation(LB["xnT"][:, c, bass.ds(i2 * D + (j * P + P // 2), P)],
                                                     ps[:, j, c * P:(c + 1) * P], ACT.Identity,
                                                     scale=w["lng"][:, c:c + 1], bias=w["lnb"][:, c:c + 1])
                        a.then_inc(sem("xT_ready"), 1)
                for m in range(HC * 3):
                    act.wait_ge(sem("D_k_ps"), nth(b, HC * 3, m))
                    nc.scalar.copy(LB["kT"][:, m // 3, m % 3 * (SPAN // 3):(m % 3 + 1) * (SPAN // 3)],
                                   ps[:, 1 + m % 6, 0:SPAN // 3]).then_inc(sem("D_k_ready"), 1)
                with act.Fori(0, HT) as i:
                    n = b * HT + i
                    act.wait_ge(sem("q_ps"), nth(n, 1, 0) + done("D", "q_ps"))
                    for hh in range(2):
                        rows_ = slice(hh * DH, (hh + 1) * DH)
                        a = nc.scalar.activation(LW["q"][rows_].rearrange("p (c h) n -> p c h n", h=2)[:, :, hh, :],
                                                 ps[rows_, 0, :].rearrange("p (c n) -> p c n", c=HC), ACT.Copy,
                                                 scale=DH ** -0.5)
                    a.then_inc(sem("q_ready"), 1)

                    def exps(u):
                        act.wait_ge(sem("D_nm_ready"), nth(n, 2, u))
                        for h in range(4):
                            a = nc.scalar.activation(LW["p"][:, u, h, :], ps[:, 1 + 2 * u + h // 2, h % 2 * D:(h % 2 + 1) * D],
                                                     ACT.Exp, bias=LW["nm"][:, u, h:h + 1], accum_out=LW["sum"][:, u, h, :])
                        a.then_inc(sem("p_ready"), 1)

                    def take_oT(u):
                        act.wait_ge(sem("oT_ps"), nth(n, 2, u) + done("D", "oT_ps"))
                        nc.scalar.copy(LW["oT"][:, u, :], ps[:, 7, 0:D]).then_inc(sem("oT_ready"), 1)

                    exps(0)
                    exps(1)
                    take_oT(0)
                    take_oT(1)

        def light_pe(pe):
            w = pk["D"]
            pe.wait_ge(sem("D_in"), LOADS["D"])
            pe.wait_ge(sem("D_zeros"), 1)
            with pe.Fori(0, B) as b:
                with pe.Fori(0, HT // 2) as i2:
                    for j in range(2):
                        n = b * HT + i2 * 2 + j
                        pe.wait_ge(sem("xn_ready"), n + 1 + done("D", "xn_ready"))
                        for c in range(DC):
                            mm = nc.tensor.transpose(ps[:, j, c * P:(c + 1) * P], LW["xn"][:, j, c * P:(c + 1) * P], ident)
                        mm.then_inc(sem("xT_ps"), 1)
                    pe.wait_ge(sem("xT_ready"), b * HT + i2 * 2 + 2 + done("D", "xT_ready"))
                for m in range(HC * 3):
                    if m >= 6:
                        pe.wait_ge(sem("D_k_ready"), nth(b, HC * 3, m - 6))
                    at = m % 3 * (SPAN // 3)
                    for ci in range(DC):
                        mm = nc.tensor.matmul(ps[:, 1 + m % 6, 0:SPAN // 3],
                                              w["wqkv"][:, ci * 3 * HDH + HDH + m // 3 * P:ci * 3 * HDH + HDH + (m // 3 + 1) * P],
                                              LB["xnT"][:, ci, at:at + SPAN // 3], start=ci == 0, stop=ci == DC - 1)
                    mm.then_inc(sem("D_k_ps"), 1)
                for j in range(HT + 1):
                    if j < 6:
                        pe.wait_ge(sem("D_k_ready"), nth(b, HC * 3, 6 + j))
                    else:
                        pe.wait_ge(sem("D_v_ready"), nth(b, HT + 1, j - 6))
                    for ci in range(DC):
                        mm = nc.tensor.matmul(ps[:, 1 + j % 6, :], LB["xnT"][:, ci, j * P:(j + 1) * P],
                                              w["wqkv"][:, ci * 3 * HDH + 2 * HDH:(ci + 1) * 3 * HDH], start=ci == 0, stop=ci == DC - 1)
                    mm.then_inc(sem("D_v_ps"), 1)
                with pe.Fori(0, HT) as i:
                    n = b * HT + i
                    pe.wait_ge(sem("D_v_ready"), nth(b, HT + 1, HT))
                    for c in range(HC):
                        for ci in range(DC):
                            mm = nc.tensor.matmul(ps[:, 0, c * P:(c + 1) * P],
                                                  w["wqkv"][:, ci * 3 * HDH + c * P:ci * 3 * HDH + (c + 1) * P],
                                                  LB["xnT"][:, ci, bass.ds(i * P + P // 2, P)], start=ci == 0, stop=ci == DC - 1)
                    mm.then_inc(sem("q_ps"), 1)
                    pe.wait_ge(sem("q_ready"), nth(n, 1, 0) + done("D", "q_ready"))
                    for u in range(2):
                        for k in range(2):
                            bank = ps[:, 1 + 2 * u + k, :]
                            for h in range(2):
                                nc.tensor.matmul(bank[:, h * D:(h + 1) * D], maskL[:, :], maskR[:, i, :],
                                                 start=h == 0, stop=False, skip_group_check=True)
                            for h in range(2):
                                hd = 4 * u + 2 * k + h
                                mm = nc.tensor.matmul(bank[:, h * D:(h + 1) * D], LW["q"][:, hd, :],
                                                      LB["kT"][:, hd // 2, bass.ds(i * P, 2 * P)], start=False, stop=h == 1,
                                                      skip_group_check=True)
                        mm.then_inc(sem("s_ps"), 1)

                    def turn_p(u):
                        pe.wait_ge(sem("p_ready"), nth(n, 2, u) + done("D", "p_ready"))
                        if u == 1:
                            pe.wait_ge(sem("pT_ready"), nth(n, 2, 0) + done("D", "pT_ready"))
                        for h in range(4):
                            for k in range(2):
                                m = 2 * h + k
                                mm = nc.tensor.transpose(ps[:, 5 + m // 4, m % 4 * P:(m % 4 + 1) * P],
                                                         LW["p"][:, u, h, k * P:(k + 1) * P], ident)
                        mm.then_inc(sem("pT_ps"), 1)

                    def weigh_v(u):
                        pe.wait_ge(sem("pT_ready"), nth(n, 2, u) + done("D", "pT_ready"))
                        if u == 1:
                            pe.wait_ge(sem("oT_ready"), nth(n, 2, 0) + done("D", "oT_ready"))
                        for h in range(4):
                            hd = 4 * u + h
                            for k in range(2):
                                mm = nc.tensor.matmul(ps[:, 7, h * DH:(h + 1) * DH],
                                                      LW["pT"][:, u, (2 * h + k) * P:(2 * h + k + 1) * P],
                                                      LB["v"][:, i + k, hd * DH:(hd + 1) * DH], start=k == 0, stop=k == 1)
                        mm.then_inc(sem("o_ps"), 1)

                    def turn_o(u):
                        pe.wait_ge(sem("on_ready"), nth(n, 2, u) + done("D", "on_ready"))
                        for c in range(2):
                            mm = nc.tensor.transpose(ps[:, 7, c * P:(c + 1) * P], LW["on"][:, u, c * P:(c + 1) * P], ident)
                        mm.then_inc(sem("oT_ps"), 1)

                    def project(u):
                        pe.wait_ge(sem("oT_ready"), nth(n, 2, u) + done("D", "oT_ready"))
                        for c in range(2):
                            mm = nc.tensor.matmul(ps[:, 0, 0:D], LW["oT"][:, u, c * P:(c + 1) * P],
                                                  w["wout"][:, (2 * u + c) * D:(2 * u + c + 1) * D],
                                                  start=u == 0 and c == 0, stop=u == 1 and c == 1)
                        return mm

                    turn_p(0)
                    weigh_v(0)
                    turn_o(0)
                    turn_p(1)
                    weigh_v(1)
                    turn_o(1)
                    project(0)
                    project(1).then_inc(sem("y_ps"), 1)
                    pe.wait_ge(sem("D_x_light"), nth(n, 1, 0))

        ROUNDS = 50

        def route_dve(dve):
            link, ve = chain_dve.link, nc.vector
            s, u, y, e = RT["s"], RT["u"], RT["y"], RT["e"]
            for r, k in enumerate((NQ, NKV)):
                logk = float(np.log(np.float32(min(k * FETCH, SEQ_CAP))))
                link(ve.memset(RT["logk"][:, r * B:(r + 1) * B], logk))
                link(ve.memset(RT["k"][:, r * B:(r + 1) * B], float(k)))
                link(ve.memset(RT["a"][:, r * B:(r + 1) * B], float(np.float32(logk) - np.log(np.float32(S)))))
            ve.tensor_reduce(RT["pmax"], s, AX.X, ALU.max).then_inc(sem("D_pmax"), 1)
            dve.wait_ge(sem("D_smax"), 1)
            with dve.Fori(0, ROUNDS - 1) as i:
                chain_dve.begin(i, 5)
                link(ve.tensor_tensor(u, s, over_t(RT["a"]), ALU.add))
                link(ve.tensor_tensor(RT["um"], RT["m"], RT["a"], ALU.add))
                link(ve.scalar_tensor_tensor(out=flat32(y), in0=flat32(u), scalar=0.0, in1=flat32(s), op0=ALU.max, op1=ALU.subtract))
                link(ve.scalar_tensor_tensor(out=RT["ym"], in0=RT["um"], scalar=0.0, in1=RT["m"], op0=ALU.max, op1=ALU.subtract))
                ve.tensor_tensor(y, y, over_t(RT["ym"]), ALU.subtract).then_inc(sem("D_y_shift"), 1)
                dve.wait_ge(sem("D_e_sum"), nth(i, 1, 0))
                ve.tensor_reduce(RT["tot"], ps[:, 0, 0:NG * HT].rearrange("p (g t) -> p g t", g=NG), AX.X, ALU.add
                                 ).then_inc(sem("D_tot"), 1)
                dve.wait_ge(sem("D_ln"), nth(i, 1, 0))
                link(ve.tensor_tensor(RT["ym"], RT["ym"], RT["ln"], ALU.subtract))
                ve.tensor_tensor(RT["a"], RT["ym"], RT["logk"], ALU.add).then_inc(sem("D_a"), 1)
                dve.wait_ge(sem("D_a"), nth(i, 1, 0))
            chain_dve.end(ROUNDS - 1)
            link(ve.tensor_tensor(u, s, over_t(RT["a"]), ALU.add))
            ve.tensor_scalar(y, u, 0.0, None, ALU.min).then_inc(sem("D_fin"), 1)
            dve.wait_ge(sem("D_sc"), 1)
            dve.wait_ge(sem("D_scT_ps"), 1)
            ve.tensor_copy(HWK["scT"][0:NG * HT, :], ps[0:NG * HT, 0, 0:P]).then_inc(sem("D_scT"), 1)
            dve.wait_ge(sem("D_row"), 16)
            for g in range(NG):
                for t in range(HT):
                    k = g * HT + t
                    link(ve.tensor_scalar(HWK["selT"][:, 0, :], RB["row"][:, g, :], RT["sc"][:, g, t:t + 1], 0.0,
                                          ALU.is_gt, ALU.add, accum_out=RT["n"][:, g, t:t + 1]))
            k_t = over_t(RT["k"])
            link(ve.tensor_tensor(RT["tie"], RT["n"], k_t, ALU.is_lt))
            link(ve.tensor_tensor(RT["tie"], RT["tie"], RT["n"], ALU.mult))
            ve.tensor_reduce(RT["gm"], RT["tie"], AX.X, ALU.max).then_inc(sem("D_gm"), 1)
            dve.wait_ge(sem("D_gstar"), 1)
            link(ve.tensor_tensor(RT["sure"], RT["n"], over_t(RT["gstar"]), ALU.is_lt))
            ve.tensor_tensor(RT["tie"], RT["n"], over_t(RT["gstar"]), ALU.is_equal).then_inc(sem("D_tie"), 1)
            dve.wait_ge(sem("D_prefix"), 1)
            pre = ps[:, 1, 0:NG * HT].rearrange("p (g t) -> p g t", g=NG)
            link(ve.tensor_tensor(RT["u"], pre, over_t(RT["gstar"]), ALU.add))
            link(ve.tensor_tensor(RT["u"], RT["u"], k_t, ALU.is_lt))
            link(ve.tensor_tensor(RT["u"], RT["u"], RT["tie"], ALU.mult))
            ve.tensor_tensor(RT["sel"], RT["u"], RT["sure"], ALU.add).then_inc(sem("D_sel"), 1)
            dve.wait_ge(sem("D_prefix"), 2)
            link(ve.scalar_tensor_tensor(out=flat32(RT["pos"]), in0=ps[:, 2, 0:NG * HT], scalar=1.0, in1=flat32(RT["sel"]),
                                         op0=ALU.add, op1=ALU.mult))
            link(ve.tensor_scalar(RT["pos"], RT["pos"], -1.0, None, ALU.add))
            link(ve.tensor_scalar(RT["one"], RT["sc"], -1.0, 1.0, ALU.mult, ALU.add))
            link(ve.tensor_tensor(RT["one"], RT["one"], RT["sc"], ALU.add))
            aux = RT["aux"]
            dve.wait_ge(sem("D_norm"), 1)
            link(ve.tensor_scalar(RT["ssq"], RT["ssq"], 1e-12, None, ALU.max))
            link(ve.reciprocal(RT["ssq"], RT["ssq"]))
            link(ve.tensor_scalar(aux[:, :, 0], RT["ssq"][:, :, 0], float(D) ** 0.5, None, ALU.mult))
            link(ve.tensor_copy(aux[:, :, 1], flat32(RT["one"])[:, NT:2 * NT]))
            link(ve.tensor_copy(aux[:, :, 2], flat32(RT["one"])[:, 0:NT]))
            link(ve.tensor_scalar(RT["unsel"][:, :, 0], flat32(RT["sel"])[:, 0:NT], -1.0, 1.0, ALU.mult, ALU.add))

        def route_act(act):
            with act.Fori(0, ROUNDS - 1) as i:
                act.wait_ge(sem("D_y_shift"), nth(i, 1, 0))
                nc.scalar.activation(RT["e"], RT["y"], ACT.Exp, scale=-1.0).then_inc(sem("D_e"), 1)
                act.wait_ge(sem("D_tot"), nth(i, 1, 0))
                nc.scalar.activation(RT["ln"], RT["tot"], ACT.Ln).then_inc(sem("D_ln"), 1)
            act.wait_ge(sem("D_fin"), 1)
            nc.scalar.activation(RT["sc"], RT["y"], ACT.Exp).then_inc(sem("D_sc"), 1)
            nc.scalar.activation(RT["ssq"], RT["ssq"], ACT.Sqrt).then_inc(sem("D_norm"), 1)

        def route_pool(pool):
            mx = bass.bass_isa.ReduceOp.max
            pool.wait_ge(sem("D_pmax"), 1)
            nc.gpsimd.partition_all_reduce(RT["m"], RT["pmax"], P, mx).then_inc(sem("D_smax"), 1)
            pool.wait_ge(sem("D_gm"), 1)
            nc.gpsimd.partition_all_reduce(RT["gstar"], RT["gm"], P, mx).then_inc(sem("D_gstar"), 1)

        def route_pe(pe):
            with pe.Fori(0, ROUNDS - 1) as i:
                pe.wait_ge(sem("D_e"), nth(i, 1, 0))
                nc.tensor.matmul(ps[:, 0, 0:NG * HT], ones, flat32(RT["e"]), start=True, stop=True).then_inc(sem("D_e_sum"), 1)
            pe.wait_ge(sem("D_sc"), 1)
            nc.tensor.transpose(ps[0:NG * HT, 0, 0:P], flat32(RT["sc"]), ident).then_inc(sem("D_scT_ps"), 1)

            def prefix(v, bank):
                out_ = ps[:, bank, 0:NG * HT].rearrange("p (g t) -> p g t", g=NG)
                nc.tensor.matmul(out_, pk["const"]["before"], v, start=True, stop=False, skip_group_check=True)
                for d in range(1, HT):
                    mm = nc.tensor.matmul(out_[:, :, d:HT], ones, v[:, :, 0:HT - d], start=False, stop=d == HT - 1,
                                          skip_group_check=True)
                mm.then_inc(sem("D_prefix"), 1)

            pe.wait_ge(sem("D_tie"), 1)
            prefix(RT["tie"], 1)
            pe.wait_ge(sem("D_sel"), 1)
            prefix(RT["sel"], 2)

        def route_sp(sp):
            sp.wait_ge(sem("D_scT"), 1)
            sp.dma_start(score_rows, HWK["scT"][0:NG * HT, :]).then_inc(sem("D_score_rows"), 16)
            sp.wait_ge(sem("D_score_rows"), 16)
            sp.dma_start(RB["row"].rearrange("p g n -> p (g n)"),
                         score_rows.rearrange("r n -> (r n)").partition_broadcast(P)).then_inc(sem("D_row"), 16)

        QC, KC = NQ // P, NKV // P

        def heavy_dve(dve):
            link, ve = chain_dve.link, nc.vector
            w, r = pk["D"], rw["D"]
            link(ve.tensor_copy(RT["rmsg"], w["rmsg"]))
            slots = pk["const"]["slots"]
            with dve.Fori(0, B) as b:
                chain_dve.begin(b, HEAVY_LINKS)
                for t in range(HT):
                    n = b * HT + t
                    link(ve.tensor_scalar(HB["selq"][:, t, :], slots[:, 0:NQ], pos_cols[:, n, :], None, ALU.is_equal))
                    link(ve.tensor_scalar(HB["selk"][:, t, :], slots, pos_cols[:, n + NT, :], None, ALU.is_equal))
                dve.sem_inc(sem("D_onehot"), 1)
                for m in range(QC + KC):
                    dve.wait_ge(sem("D_gather_ps"), nth(b, QC + KC, m))
                    link(ve.tensor_copy(HWK["aux"][:, m, :], ps[:, m, D:D + 3]))
                    if m >= 2:
                        dve.wait_ge(sem("D_gT_ps"), nth(b, QC + KC, m - 2))
                    ve.tensor_scalar(HWK["xg"][:, m % 2, :], ps[:, m, 0:D], HWK["aux"][:, m, 0:1], None,
                                     ALU.mult).then_inc(sem("D_xg"), 1)
                for c in range(HC):
                    dve.wait_ge(sem("D_kh_ps"), nth(b, HC, c))
                    ve.tensor_copy(HB["kT"][:, c, :], ps[:, c % 4, :]).then_inc(sem("D_kh"), 1)
                for k in range(KC):
                    dve.wait_ge(sem("D_vh_ps"), nth(b, KC, k))
                    ve.tensor_scalar(HB["v"][:, k, :], ps[:, k, :], HWK["aux"][:, QC + k, 1:2], None,
                                     ALU.mult).then_inc(sem("D_vh"), 1)
                for qc in range(QC):
                    n = b * QC + qc
                    dve.wait_ge(sem("D_sn_ps"), nth(n, 1, 0))
                    link(ve.tensor_copy(HWK["sn"], ps[:, 7, 0:H8]))

                    def shift(h):
                        dve.wait_ge(sem("D_sh_ps"), nth(n, H8, h))
                        link(ve.tensor_reduce(HWK["m"][:, h:h + 1], ps[:, h % 2, :], AX.X, ALU.max))
                        link(ve.tensor_tensor(HWK["m"][:, h:h + 1], HWK["m"][:, h:h + 1], HWK["sn"][:, h:h + 1], ALU.max))
                        ve.tensor_scalar(HWK["nm"][:, h:h + 1], HWK["m"][:, h:h + 1], -1.0, None, ALU.mult
                                         ).then_inc(sem("D_nmh"), 1)

                    def take_pT(h):
                        dve.wait_ge(sem("D_phT_ps"), nth(n, H8, h))
                        if h >= 2:
                            dve.wait_ge(sem("D_oh_ps"), nth(n, H8, h - 2))
                        ve.tensor_copy(HWK["pT"][:, h % 2, :], ps[:, 2 + h % 2, :]).then_inc(sem("D_phT"), 1)

                    shift(0)
                    for h in range(H8):
                        if h + 1 < H8:
                            shift(h + 1)
                        if h == H8 - 1:
                            link(ve.tensor_tensor(HWK["sn"], HWK["sn"], HWK["m"], ALU.subtract))
                            dve.sem_inc(sem("D_sn_sub"), 1)
                        take_pT(h)
                    dve.wait_ge(sem("D_oh_ps"), nth(n, H8, H8 - 1))
                    dve.wait_ge(sem("D_pn"), nth(n, 1, 0))
                    head = lambda v: v.rearrange("p (h e) -> p h e", h=H8)
                    wide = lambda v: v.rearrange("p (h o) -> p h o", o=1).to_broadcast([P, H8, DH])
                    link(ve.tensor_tensor(head(HWK["pv"]), head(r["nv"]), wide(HWK["pn"]), ALU.mult))
                    link(ve.tensor_tensor(HWK["pv"], HWK["pv"], ps[:, 4, :], ALU.add))
                    link(ve.tensor_tensor(HWK["rs"], HWK["sum"][:, :, 0], HWK["pn"], ALU.add))
                    link(ve.reciprocal(HWK["rs"], HWK["rs"]))
                    ve.tensor_tensor(head(HWK["o"]), head(HWK["pv"]), wide(HWK["rs"]), ALU.mult).then_inc(sem("D_oh"), 1)
                    dve.wait_ge(sem("D_yh_ps"), nth(n, 1, 0))
                    ve.tensor_copy(HWK["routed"][:, qc, :], ps[:, 6, 0:D]).then_inc(sem("D_routed"), 1)
                for t in range(HT):
                    n = b * HT + t
                    tmp = HWK["t"][:, t % 2, :]
                    link(ve.tensor_scalar(tmp, r["nullq"], RT["unsel"][:, n, :], None, ALU.mult))
                    dve.wait_ge(sem("D_scat_ps"), nth(b, HT, t))
                    link(ve.scalar_tensor_tensor(out=tmp, in0=ps[:, t % 2, 0:D], scalar=RT["aux"][:, n, 2:3], in1=tmp,
                                                 op0=ALU.mult, op1=ALU.add))
                    finish(n, tmp, None, 5, None, sem("x_new"))
            chain_dve.end(B)

        HEAVY_LINKS = 2 * HT + (QC + KC) + QC * (1 + 2 * H8 + 1 + 4) + HT * 3

        def heavy_act(act):
            with act.Fori(0, B) as b:
                for m in range(QC + KC):
                    act.wait_ge(sem("D_gT_ps"), nth(b, QC + KC, m))
                    dst, at = (HB["xqT"], m) if m < QC else (HB["xkT"], m - QC)
                    for c in range(DC):
                        a = nc.scalar.activation(dst[:, c, at * P:(at + 1) * P], ps[:, 6 + m % 2, c * P:(c + 1) * P], ACT.Copy,
                                                 scale=RT["rmsg"][:, c:c + 1])
                    a.then_inc(sem("D_gT"), 1)
                for c in range(HC):
                    act.wait_ge(sem("D_qh_ps"), nth(b, HC, c))
                    nc.scalar.activation(HWK["qT"][:, c, :], ps[:, 4 + c % 4, 0:NQ], ACT.Copy, scale=DH ** -0.5
                                         ).then_inc(sem("D_qh"), 1)
                for m in range(4):
                    act.wait_ge(sem("D_selT_ps"), nth(b, 4, m))
                    nc.scalar.copy(HWK["selT"][:, m // 2, m % 2 * 512:(m % 2 + 1) * 512], ps[:, 4 + m, :]
                                   ).then_inc(sem("D_selT"), 1)
                for qc in range(QC):
                    n = b * QC + qc
                    for h in range(H8):
                        act.wait_ge(sem("D_nmh"), nth(n, H8, h))
                        if h >= 2:
                            act.wait_ge(sem("D_phT_ps"), nth(n, H8, h - 2))
                        nc.scalar.activation(HWK["p"][:, h % 2, :], ps[:, h % 2, :], ACT.Exp, bias=HWK["nm"][:, h:h + 1],
                                             accum_out=HWK["sum"][:, h, :]).then_inc(sem("D_ph"), 1)
                    act.wait_ge(sem("D_sn_sub"), nth(n, 1, 0))
                    nc.scalar.activation(HWK["pn"], HWK["sn"], ACT.Exp).then_inc(sem("D_pn"), 1)
                    act.wait_ge(sem("D_ohT_ps"), nth(n, 1, 0))
                    nc.scalar.copy(HWK["oT"], ps[:, 5, :].rearrange("p (c n) -> p c n", c=HC)).then_inc(sem("D_ohT"), 1)

        def heavy_pe(pe):
            w = pk["D"]
            with pe.Fori(0, B) as b:
                pe.wait_ge(sem("D_onehot"), nth(b, 1, 0))
                for m in range(QC + KC):
                    sel = HB["selq"][:, :, m * P:(m + 1) * P] if m < QC else HB["selk"][:, :, (m - QC) * P:(m - QC + 1) * P]
                    for t in range(HT):
                        nc.tensor.matmul(ps[:, m, 0:D], sel[:, t, :], hall[:, b * HT + t, :], start=t == 0,
                                         stop=t == HT - 1, skip_group_check=True)
                    for t in range(HT):
                        mm = nc.tensor.matmul(ps[:, m, D:D + 3], sel[:, t, :], RT["aux"][:, b * HT + t, :], start=t == 0,
                                              stop=t == HT - 1, skip_group_check=True)
                    mm.then_inc(sem("D_gather_ps"), 1)
                for m in range(QC + KC):
                    pe.wait_ge(sem("D_xg"), nth(b, QC + KC, m))
                    if m >= 2:
                        pe.wait_ge(sem("D_gT"), nth(b, QC + KC, m - 2))
                    for c in range(DC):
                        mm = nc.tensor.transpose(ps[:, 6 + m % 2, c * P:(c + 1) * P], HWK["xg"][:, m % 2, c * P:(c + 1) * P], ident)
                    mm.then_inc(sem("D_gT_ps"), 1)
                pe.wait_ge(sem("D_gT"), nth(b, QC + KC, QC + KC - 1))
                for c in range(HC):
                    for ci in range(DC):
                        mm = nc.tensor.matmul(ps[:, c, :], w["wkh"][:, ci * HDH + c * P:ci * HDH + (c + 1) * P],
                                              HB["xkT"][:, ci, :], start=ci == 0, stop=ci == DC - 1)
                    mm.then_inc(sem("D_kh_ps"), 1)
                for c in range(HC):
                    for ci in range(DC):
                        mm = nc.tensor.matmul(ps[:, 4 + c, 0:NQ], w["wqh"][:, ci * HDH + c * P:ci * HDH + (c + 1) * P],
                                              HB["xqT"][:, ci, :], start=ci == 0, stop=ci == DC - 1)
                    mm.then_inc(sem("D_qh_ps"), 1)
                for k in range(KC):
                    pe.wait_ge(sem("D_kh"), nth(b, HC, k))
                    for ci in range(DC):
                        mm = nc.tensor.matmul(ps[:, k, :], HB["xkT"][:, ci, k * P:(k + 1) * P],
                                              w["wvh"][:, ci * HDH:(ci + 1) * HDH], start=ci == 0, stop=ci == DC - 1)
                    mm.then_inc(sem("D_vh_ps"), 1)
                for m in range(4):
                    pe.wait_ge(sem("D_qh"), nth(b, HC, m))
                    for t in range(4):
                        mm = nc.tensor.transpose(ps[:, 4 + m, t * P:(t + 1) * P],
                                                 HB["selq"][:, m % 2 * 4 + t, m // 2 * P:(m // 2 + 1) * P], ident)
                    mm.then_inc(sem("D_selT_ps"), 1)
                pe.wait_ge(sem("D_selT"), nth(b, 4, 3))
                pe.wait_ge(sem("D_vh"), nth(b, KC, KC - 1))
                for qc in range(QC):
                    n = b * QC + qc
                    for c in range(HC):
                        mm = nc.tensor.matmul(ps[:, 7, 0:H8], HWK["qT"][:, c, qc * P:(qc + 1) * P],
                                              w["nk"][:, c * H8:(c + 1) * H8], start=c == 0, stop=c == HC - 1)
                    mm.then_inc(sem("D_sn_ps"), 1)

                    def scores(h):
                        hp = slice(h % 2 * DH, (h % 2 + 1) * DH)
                        if h >= 2:
                            pe.wait_ge(sem("D_ph"), nth(n, H8, h - 2))
                        nc.tensor.matmul(ps[:, h % 2, :], HWK["qT"][hp, h // 2, qc * P:(qc + 1) * P], HB["kT"][hp, h // 2, :],
                                         start=True, stop=True).then_inc(sem("D_sh_ps"), 1)

                    def turn_p(h):
                        pe.wait_ge(sem("D_ph"), nth(n, H8, h))
                        if h >= 2:
                            pe.wait_ge(sem("D_phT"), nth(n, H8, h - 2))
                        for k in range(KC):
                            mm = nc.tensor.transpose(ps[:, 2 + h % 2, k * P:(k + 1) * P], HWK["p"][:, h % 2, k * P:(k + 1) * P], ident)
                        mm.then_inc(sem("D_phT_ps"), 1)

                    def weigh_v(h):
                        pe.wait_ge(sem("D_phT"), nth(n, H8, h))
                        for k in range(KC):
                            mm = nc.tensor.matmul(ps[:, 4, h * DH:(h + 1) * DH], HWK["pT"][:, h % 2, k * P:(k + 1) * P],
                                                  HB["v"][:, k, h * DH:(h + 1) * DH], start=k == 0, stop=k == KC - 1)
                        mm.then_inc(sem("D_oh_ps"), 1)

                    scores(0)
                    scores(1)
                    for h in range(H8):
                        turn_p(h)
                        if h + 2 < H8:
                            scores(h + 2)
                        if h >= 1:
                            weigh_v(h - 1)
                    weigh_v(H8 - 1)
                    pe.wait_ge(sem("D_oh"), nth(n, 1, 0))
                    for c in range(HC):
                        mm = nc.tensor.transpose(ps[:, 5, c * P:(c + 1) * P], HWK["o"][:, c * P:(c + 1) * P], ident)
                    mm.then_inc(sem("D_ohT_ps"), 1)
                    pe.wait_ge(sem("D_ohT"), nth(n, 1, 0))
                    for c in range(HC):
                        mm = nc.tensor.matmul(ps[:, 6, 0:D], HWK["oT"][:, c, :], w["wouth"][:, c * D:(c + 1) * D],
                                              start=c == 0, stop=c == HC - 1)
                    mm.then_inc(sem("D_yh_ps"), 1)
                pe.wait_ge(sem("D_routed"), nth(b, QC, QC - 1))
                for t in range(HT):
                    if t >= 2:
                        pe.wait_ge(sem("x_new"), nth(b, HT, t - 2) + done("D", "x_new"))
                    for j in range(QC):
                        mm = nc.tensor.matmul(ps[:, t % 2, 0:D], HWK["selT"][:, j, t * P:(t + 1) * P], HWK["routed"][:, j, :],
                                              start=j == 0, stop=j == QC - 1)
                    mm.then_inc(sem("D_scat_ps"), 1)

        MW = carve([("xn", (B, D)), ("xnT", (DC, B * P)), ("pr", (NT, NE)), ("gt", (NT, NE)), ("eq", (NT, NE)), ("cum", (NT, NE)),
                    ("top", (NT, 8)), ("c16", (4, NT)), ("scT", (NT * P,)), ("sg", (2, 512)), ("act", (2, 512)), ("accT", (DC, 512)),
                    ("start", (NT * NE,))])
        MB = carve([("w1", (NE, DC, INTER)), ("w3", (NE, DC, INTER)), ("w2", (NE, D))], big)
        xnT_all = hflat.rearrange("p (c b n) -> p c b n", c=DC, b=B)
        xnT_tok = hflat.rearrange("p (c n) -> p c n", c=DC)
        BLK = 512
        NBLK = B * S // BLK

        def moe_pe(pe):
            w = pk["H"]
            pe.wait_ge(sem("H_in"), LOADS["H"])
            with pe.Fori(0, HT) as i:
                for b in range(B):
                    pe.wait_ge(sem("xn_ready"), nth(i, B, b) + done("H", "xn_ready"))
                    for c in range(DC):
                        mm = nc.tensor.transpose(ps[:, 0, c * D + b * P:c * D + (b + 1) * P],
                                                 MW["xn"][:, b, c * P:(c + 1) * P], ident)
                mm.then_inc(sem("xT_ps"), 1)
                pe.wait_ge(sem("xT_ready"), nth(i, 1, 0) + done("H", "xT_ready"))
                for b in range(B):
                    for c in range(DC):
                        mm = nc.tensor.matmul(ps[:, 1, b * NE:(b + 1) * NE], MW["xnT"][:, c, b * P:(b + 1) * P],
                                              w["gate"][:, c * NE:(c + 1) * NE], start=c == 0, stop=c == DC - 1)
                mm.then_inc(sem("H_logit_ps"), 1)
            pe.wait_ge(sem("H_score"), 1)
            for t in range(NT):
                mm = nc.tensor.transpose(ps[0:NE, 2 + t // 4, t % 4 * P:(t % 4 + 1) * P], MW["gt"][:, t, :], ident)
            mm.then_inc(sem("H_scT_ps"), 1)
            pe.wait_ge(sem("H_scT"), 1)
            with pe.Fori(0, NBLK) as i:
                def hidden(e):
                    if e >= 2:
                        pe.wait_ge(sem("H_act"), nth(i, NE, e - 2))
                    for bank, name in ((0, "w1"), (2, "w3")):
                        for c in range(DC):
                            mm = nc.tensor.matmul(ps[:, bank + e % 2, :], MB[name][:, e, c, :],
                                                  xnT_tok[:, c, bass.ds(i * BLK, BLK)], start=c == 0, stop=c == DC - 1)
                    mm = nc.tensor.matmul(ps[:, 4 + e % 2, :], esel[:, e, :], MW["scT"][0:NE, bass.ds(i * BLK, BLK)],
                                          start=True, stop=True)
                    mm.then_inc(sem("H_gu_ps"), 1)

                def down(e):
                    pe.wait_ge(sem("H_act"), nth(i, NE, e))
                    for c in range(DC):
                        mm = nc.tensor.matmul(ps[:, 6 + c, :], MB["w2"][:, e, c * P:(c + 1) * P], MW["act"][:, e % 2, :],
                                              start=e == 0, stop=e == NE - 1)
                    mm.then_inc(sem("H_down"), 1)

                hidden(0)
                for e in range(NE):
                    if e + 1 < NE:
                        hidden(e + 1)
                    down(e)
                pe.wait_ge(sem("H_accT"), nth(i, DC, DC - 1))
                for t in range(4):
                    for c in range(DC):
                        mm = nc.tensor.transpose(ps[:, t, c * P:(c + 1) * P], MW["accT"][:, c, t * P:(t + 1) * P], ident)
                    mm.then_inc(sem("y_ps"), 1)
                pe.wait_ge(sem("x_new"), nth(i, 4, 3) + done("H", "x_new"))

        def moe_act(act):
            with act.Fori(0, HT) as i:
                act.wait_ge(sem("xT_ps"), nth(i, 1, 0) + done("H", "xT_ps"))
                nc.scalar.copy(xnT_all[:, :, :, bass.ds(i * P, P)],
                               ps[:, 0, :].rearrange("p (c b n) -> p c b n", c=DC, b=B)).then_inc(sem("H_xT_all"), 1)
                nc.scalar.copy(MW["xnT"], ps[:, 0, :].rearrange("p (c n) -> p c n", c=DC)).then_inc(sem("xT_ready"), 1)
            act.wait_ge(sem("H_lsub"), 1)
            nc.scalar.activation(MW["pr"], MW["pr"], ACT.Exp).then_inc(sem("H_exp"), 1)
            with act.Fori(0, NBLK) as i:
                for e in range(NE):
                    act.wait_ge(sem("H_gu_ps"), nth(i, NE, e))
                    nc.scalar.activation(MW["sg"][:, e % 2, :], ps[:, e % 2, :], ACT.Silu).then_inc(sem("H_silu"), 1)
                act.wait_ge(sem("H_down"), nth(i, NE, NE - 1))
                for c in range(DC):
                    nc.scalar.copy(MW["accT"][:, c, :], ps[:, 6 + c, :]).then_inc(sem("H_accT"), 1)

        def moe_dve(dve):
            link, ve = chain_dve.link, nc.vector
            with dve.Fori(0, HT) as i:
                for b in range(B):
                    t = i + b * HT
                    ve.tensor_scalar(MW["xn"][:, b, :], x[:, t, :], mean[:, t, :], rstd[:, t, :],
                                     ALU.subtract, ALU.mult).then_inc(sem("xn_ready"), 1)
                dve.wait_ge(sem("H_logit_ps"), nth(i, 1, 0))
                for b in range(B):
                    t = i + b * HT
                    ve.tensor_copy(MW["pr"][:, t, :], ps[:, 1, b * NE:(b + 1) * NE]).then_inc(sem("H_logit"), 1)
            dve.wait_ge(sem("H_logit"), NT)
            pr, gt, eq, cum, c16 = MW["pr"], MW["gt"], MW["eq"], MW["cum"], MW["c16"]
            per_t = lambda v: v.rearrange("p (t o) -> p t o", o=1).to_broadcast([P, NT, NE])
            link(ve.tensor_reduce(c16[:, 0, :], pr, AX.X, ALU.max))
            ve.tensor_tensor(pr, pr, per_t(c16[:, 0, :]), ALU.subtract).then_inc(sem("H_lsub"), 1)
            dve.wait_ge(sem("H_exp"), 1)
            link(ve.tensor_reduce(c16[:, 0, :], pr, AX.X, ALU.add))
            link(ve.reciprocal(c16[:, 0, :], c16[:, 0, :]))
            link(ve.tensor_tensor(pr, pr, per_t(c16[:, 0, :]), ALU.mult))
            for t in range(NT):
                link(ve.max(MW["top"][:, t, :], pr[:, t, :]))
            link(ve.tensor_copy(c16[:, 1, :], MW["top"][:, :, TOP - 1]))
            link(ve.tensor_tensor(gt, pr, per_t(c16[:, 1, :]), ALU.is_gt))
            link(ve.tensor_tensor(eq, pr, per_t(c16[:, 1, :]), ALU.is_equal))
            link(ve.tensor_reduce(c16[:, 2, :], gt, AX.X, ALU.add))
            link(ve.memset(MW["start"], 1.0))
            link(ve.memset(MW["start"].rearrange("p (t e) -> p t e", t=NT)[:, :, 0:1], 0.0))
            link(ve.tensor_tensor_scan(cum.rearrange("p t e -> p (t e)"), MW["start"], eq.rearrange("p t e -> p (t e)"), 0.0,
                                       ALU.mult, ALU.add))
            link(ve.tensor_tensor(cum, cum, per_t(c16[:, 2, :]), ALU.add))
            link(ve.tensor_scalar(cum, cum, float(TOP), None, ALU.is_le))
            link(ve.tensor_tensor(eq, eq, cum, ALU.mult))
            link(ve.tensor_tensor(gt, gt, eq, ALU.add))
            link(ve.tensor_reduce(c16[:, 3, :], MW["top"][:, :, 0:TOP], AX.X, ALU.add))
            link(ve.reciprocal(c16[:, 3, :], c16[:, 3, :]))
            link(ve.tensor_tensor(gt, gt, pr, ALU.mult))
            ve.tensor_tensor(gt, gt, per_t(c16[:, 3, :]), ALU.mult).then_inc(sem("H_score"), 1)
            dve.wait_ge(sem("H_scT_ps"), 1)
            ve.tensor_copy(MW["scT"][0:NE, :].rearrange("p (k n) -> p k n", k=4), ps[0:NE, 2:6, :]).then_inc(sem("H_scT"), 1)
            with dve.Fori(0, NBLK) as i:
                chain_dve.begin(i, NE)
                for e in range(NE):
                    dve.wait_ge(sem("H_silu"), nth(i, NE, e))
                    if e >= 2:
                        dve.wait_ge(sem("H_down"), nth(i, NE, e - 2))
                    a = MW["act"][:, e % 2, :]
                    link(ve.tensor_tensor(a, MW["sg"][:, e % 2, :], ps[:, 2 + e % 2, :], ALU.mult))
                    ve.tensor_tensor(a, a, ps[:, 4 + e % 2, :], ALU.mult).then_inc(sem("H_act"), 1)
                for t in range(4):
                    dve.wait_ge(sem("y_ps"), nth(i, 4, t) + done("H", "y_ps"))
                    n = i * 4 + t
                    ve.scalar_tensor_tensor(out=x[:, n, :], in0=ps[:, t, 0:D], scalar=gates[:, 7:8], in1=x[:, n, :],
                                            op0=ALU.mult, op1=ALU.add).then_inc(sem("x_new"), 1)
            chain_dve.end(NBLK)

        def moe_sp(sp):
            out_v = out.rearrange("b (t p) d -> p (b t) d", p=P)
            with sp.Fori(0, NBLK) as i:
                sp.wait_ge(sem("x_new"), nth(i, 4, 3) + done("H", "x_new"))
                sp.dma_start(out_v[:, bass.ds(i * 4, 4), :], x[:, bass.ds(i * 4, 4), :]).then_inc(sem("out_done"), 16)
            sp.wait_ge(sem("out_done"), 16 * NBLK)

        chain_dve = None

        @block.sync
        def _(sp):
            x_tiles = "b (t p) d -> p (b t) d"
            sp.dma_start(x[:, :, :], ins["x"].rearrange(x_tiles, p=P)).then_inc(sem("x_in"), 16)
            sp.dma_start(packs["const"][:, :], ins["const"]).then_inc(sem("const_in"), 16)
            sp.dma_start(gates[:, :], ins["gates"].partition_broadcast(P)).then_inc(sem("const_in"), 16)
            sp.dma_start(ctxT[:, :, :], ins["ctxT"]).then_inc(sem("const_in"), 16)
            sp.dma_start(ctxN[:, :, :], ins["ctx"].rearrange("b s d -> s b d")).then_inc(sem("const_in"), 16)
            sp.dma_start(mask8[:, :], ins["maskT"]).then_inc(sem("const_in"), 16)
            sp.dma_start(maskrow8[:, :, :], ins["mask"].rearrange("(o b) s -> o b s", o=1)).then_inc(sem("const_in"), 16)
            def load(name):
                key = "B" if name == "lora" else name
                sp.dma_start(packs[name][:, :], ins["pack_" + name]).then_inc(sem(f"{key}_in"), 16)
                if name in ROWS:
                    sp.dma_start(rows[name][:, :], ins["rows_" + name].partition_broadcast(P)).then_inc(sem(f"{key}_in"), 16)

            for name in ("A", "B", "lora", "C", "D", "E", "F"):
                load(name)
            sp.dma_start(maskR[:, :, :], ins["maskR"]).then_inc(sem("D_in"), 16)
            sp.dma_start(maskL[:, :], ins["maskL"]).then_inc(sem("D_in"), 16)
            if stop >= 4:
                route_sp(sp)
                sp.wait_ge(sem("x_new"), NT + done("D", "x_new"))
                load("G")
                if stop >= 8:
                    load("H")
                    sp.dma_start(esel, ins["esel"]).then_inc(sem("H_in"), 16)
                    for k in ("w1", "w3", "w2"):
                        sp.dma_start(MB[k], ins[k]).then_inc(sem("H_in"), 16)
                if stop >= 7:
                    load_bias(sp)
            if stop >= 8:
                moe_sp(sp)
            else:
                sp.wait_ge(sem("x_done"), 1)
                for name in "ABCDEF" + ("G" if stop >= 4 else ""):
                    sp.wait_ge(sem(f"{name}_in"), LOADS[name])
                sp.dma_start(out.rearrange(x_tiles, p=P), x[:, :, :]).then_inc(sem("out_done"), 16)
                sp.wait_ge(sem("out_done"), 16)

        @block.gpsimd
        def _(pool):
            if stop >= 2:
                ffn_setup_pool(pool)
            if stop >= 4:
                route_pool(pool)
            if stop >= 5:
                sim_pool(pool)

        @block.scalar
        def _(act):
            act.wait_ge(sem("const_in"), 96)
            nc.scalar.activation(gates[:, :], gates[:, :], ACT.Tanh).then_inc(sem("gates_ready"), 1)
            norm_act(act, "A")
            heads16_act(act, "A")
            if stop >= 2:
                norm_act(act, "B")
                ffn_act(act)
            if stop >= 3:
                norm_act(act, "C")
                local_act(act)
            if stop >= 4:
                norm_act(act, "Dx")
                norm_act(act, "Dh")
                light_act(act)
                route_act(act)
                heavy_act(act)
            if stop >= 5:
                norm_act(act, "E")
                sim_act(act)
            if stop >= 6:
                norm_act(act, "F")
                rnn_act(act)
            if stop >= 7:
                norm_act(act, "G")
                heads16_act(act, "G")
            if stop >= 8:
                norm_act(act, "H")
                moe_act(act)

        @block.tensor
        def _(pe):
            heads16_pe(pe, "A")
            if stop >= 2:
                ffn_pe(pe)
            if stop >= 3:
                local_pe(pe)
            if stop >= 4:
                light_pe(pe)
                route_pe(pe)
                heavy_pe(pe)
            if stop >= 5:
                sim_pe(pe)
            if stop >= 6:
                rnn_pe(pe)
            if stop >= 7:
                pe.wait_ge(sem("x_new"), NT + done("F", "x_new"))
                heads16_pe(pe, "G")
            if stop >= 8:
                moe_pe(pe)

        @block.vector
        def _(dve):
            nonlocal chain_dve
            chain_dve = Chain(dve, sem("dve_chain"))
            dve.wait_ge(sem("x_in"), 16)
            with dve.Fori(0, NT) as t:
                nc.vector.bn_stats(stats[:, t, :], x[:, t, :]).then_inc(sem("x_stats"), 1)
            dve.wait_ge(sem("x_stats"), NT)
            dve.wait_ge(sem("gates_ready"), 1)
            norm_dve(dve, "A")
            heads16_dve(dve, "A")
            last = "A"
            if stop >= 2:
                dve.wait_ge(sem("x_new"), NT + done(last, "x_new"))
                ffn_setup_dve(dve)
                norm_dve(dve, "B")
                ffn_dve(dve)
                last = "B"
            if stop >= 3:
                dve.wait_ge(sem("x_new"), NT + done(last, "x_new"))
                norm_dve(dve, "C")
                local_dve(dve)
                last = "C"
            if stop >= 4:
                dve.wait_ge(sem("x_new"), NT + done(last, "x_new"))
                norm_dve(dve, "Dx")
                light_dve(dve)
                dve.wait_ge(sem("D_x_light"), NT)
                route_dve(dve)
                heavy_dve(dve)
                last = "D"
            if stop >= 5:
                dve.wait_ge(sem("x_new"), NT + done(last, "x_new"))
                sim_dve(dve)
                last = "E"
            if stop >= 6:
                dve.wait_ge(sem("x_new"), NT + done(last, "x_new"))
                rnn_dve(dve)
                last = "F"
            if stop >= 7:
                dve.wait_ge(sem("x_new"), NT + done(last, "x_new"))
                norm_dve(dve, "G")
                heads16_dve(dve, "G")
                last = "G"
            if stop >= 8:
                dve.wait_ge(sem("x_new"), NT + done(last, "x_new"))
                norm_dve(dve, "H")
                moe_dve(dve)
            else:
                dve.wait_ge(sem("x_new"), NT + done(last, "x_new"))
                dve.sem_inc(sem("x_done"), 1)


def chunked(w):
    k = w.shape[0] // P
    return w.reshape(k, P, -1).transpose(1, 0, 2).reshape(P, -1)


def kernel(**inputs):
    import ml_dtypes

    import concourse.bacc as bacc
    from concourse.bass_utils import run_bass_kernel_spmd

    v = {k: np.asarray(a) for k, a in inputs.items()}
    a, f = "L0_xattn_", "L0_ffn_"
    packs = {
        "const": [np.eye(P, dtype=np.float32), np.kron(np.eye(HPC), np.ones((HD16, 1))).astype(np.float32),
                  np.ones((P, P), np.float32), np.triu(np.ones((P, P), np.float32), 1),
                  np.broadcast_to(np.arange(NKV, dtype=np.float32), (P, NKV))],
        "pack_A": [chunked(v[a + "Wq"].T), chunked(v[a + "Wk"].T), chunked(v[a + "Wv"].T), chunked(v[a + "Wp"].T),
                   chunked(v[a + "bq"][:, None]), chunked(v[a + "bk"][:, None])],
        "pack_B": [chunked(v[f + "W_fc"].T), chunked(v[f + "W_proj"].T), chunked(v[f + "b_fc"][:, None])],
        "pack_lora": [v[f + "A_fc"], v[f + "B_fc"].T, v[f + "A_proj"], v[f + "B_proj"].T],
        "pack_G": [chunked(v["L3_xattn_" + n + "_w"].T) for n in "qkvo"]
                  + [chunked(v["L3_xattn_" + n + "_b"][:, None]) for n in "qk"],
    }
    wkv = v["L1_ffn_w_kv_h"]
    null_k = np.zeros((HDH, H8), np.float32)
    for h in range(H8):
        null_k[h * DH:(h + 1) * DH, h] = v["L1_ffn_null_kv"][0, h]
    packs |= {
        "pack_C": [chunked(v["L1_xattn_W_p"].T), chunked(v["L1_xattn_W_a"]),
                   np.concatenate([v["L1_xattn_V_p"][0], np.zeros(P - PSZ, np.float32)])[:, None],
                   np.broadcast_to(np.arange(SC, dtype=np.float32), (P, SC)),
                   np.broadcast_to(np.arange(WIN, dtype=np.float32) - 2, (P, WIN))],
        "pack_D": [chunked(v["L1_ffn_w_qkv_l"]), chunked(v["L1_ffn_w_out_l"]), chunked(v["L1_ffn_w_q_h"]),
                   chunked(wkv[:, :, :DH].reshape(D, HDH)), chunked(wkv[:, :, DH:].reshape(D, HDH)),
                   chunked(v["L1_ffn_w_out_h"]), chunked(v["L1_ffn_ln_g"][:, None]), chunked(v["L1_ffn_ln_b"][:, None]),
                   chunked(v["L1_ffn_rms_g"][:, None]), chunked(null_k)],
        "pack_E": [chunked(v["L2_xattn_W_qv"])] + [chunked(w[:, None]) for w in np.split(v["L2_xattn_w_sim"], 3)],
        "pack_F": [chunked(v["L2_ffn_" + n].T) for n in ("wf", "wi", "wc", "wo", "uf", "ui", "uc", "uo")]
                  + [chunked(v["L2_ffn_" + n][:, None]) for n in ("bf", "bi", "bc", "in_c")],
        "pack_H": [chunked(v["L3_ffn_gate_w"].T)],
    }
    rows = {
        "rows_D": [v["L1_ffn_rt_q"][0], v["L1_ffn_rt_kv"][0], v["L1_ffn_null_q"], v["L1_ffn_null_kv"][1].reshape(-1)],
        "rows_E": [v["L2_xattn_b_qv"], v["L2_xattn_b_sim"]],
        "rows_F": [v["L2_ffn_bo"]],
        "rows_A": [v[a + "bv"], v[a + "bp"]],
        "rows_B": [v[f + "b_proj"]],
        "rows_G": [v["L3_xattn_v_b"], v["L3_xattn_o_b"]],
    }
    arrays = {k: np.concatenate(p, axis=1) for k, p in packs.items()}
    arrays |= {k: np.concatenate(p) for k, p in rows.items()}
    ctx = v["ctx_1024"]
    masked = np.zeros((B, HT, 2 * P), bool)
    masked[0, :, 3 * WINDOW:] = masked[1, :, :WINDOW] = masked[:, 0, :WINDOW] = masked[:, -1, 3 * WINDOW:] = True
    experts = lambda w: w.reshape(NE, DC, P, INTER).transpose(2, 0, 1, 3)
    arrays |= {
        "x": v["x"], "gates": np.concatenate([v["g_xattn"], v["g_ffn"]]), "ctx": ctx,
        "ctxT": ctx.transpose(2, 0, 1).reshape(DC, P, B * SC).transpose(1, 0, 2),
        "mask": v["mask_BxS2_bk0"], "maskT": v["mask_BxS2_bk0"].T,
        "fside": v["fside_1x16xSxS2_0"],
        "maskR": np.where(masked, NEG, 0.0).astype(ml_dtypes.bfloat16),
        "maskL": np.kron(np.eye(B), np.ones((1, WINDOW))).astype(ml_dtypes.bfloat16),
        "esel": np.kron(np.eye(NE), np.ones((1, P))).astype(np.float32).reshape(NE, NE, P),
        "w1": experts(v["L3_ffn_w1"]), "w3": experts(v["L3_ffn_w3"]), "w2": v["L3_ffn_w2"].transpose(1, 0, 2),
    }
    nc = bacc.Bacc("TRN2", target_bir_lowering=False, num_devices=1)
    arrays = {f"in_{k}": np.ascontiguousarray(a) for k, a in arrays.items()}
    ins = {k[3:]: nc.dram_tensor(k, a.shape, mybir.dt.from_np(a.dtype), kind="ExternalInput").ap()
           for k, a in arrays.items()}
    out = nc.dram_tensor("out", (B, S, D), F32, kind="ExternalOutput").ap()
    build(nc, ins, out, STOP)
    return run_bass_kernel_spmd(nc, [arrays], core_ids=[0]).results[0]["out"]


STOP = 8
```

```python
from contextlib import ExitStack

import numpy as np

import concourse.bass as bass
from concourse import mybir

F32 = mybir.dt.float32
BF16 = mybir.dt.bfloat16
U8 = mybir.dt.uint8
ALU = mybir.AluOpType
ACT = mybir.ActivationFunctionType
AX = mybir.AxisListType

P = 128
B, S, D = 2, 1024, 256
NT = B * S // P
HT = S // P
DC = D // P
SC = 77
H16, HD16 = 16, 16
HPC = P // HD16
F0 = 1024
FC = F0 // P
RANK = 16
WIN, PSZ = 4, 100
H8, DH = 8, 64
HDH = H8 * DH
WINDOW = 64
HC = HDH // P
NQ, NKV = 256, 512
FETCH, SEQ_CAP = 9.0 / 8.0, 2048
NE, TOP, INTER = 16, 4, 128
EPS = 1e-5
NEG = -1e30
MAGIC = 12582912.0

PACKS = {
    "const": [("ident", P), ("headmask", HPC), ("ones", P), ("before", P), ("slots", NKV)],
    "A": [("wq", DC * D), ("wk", DC * D), ("wv", DC * D), ("wp", DC * D), ("bq", DC), ("bk", DC)],
    "B": [("fc", DC * F0), ("proj", FC * D), ("bfc", FC)],
    "lora": [("afc", D), ("bfcT", F0), ("aproj", F0), ("bprojT", D)],
    "C": [("wp", DC * PSZ), ("wa", DC * D), ("vp", 1), ("iota", SC), ("woff", WIN)],
    "D": [("wqkv", DC * 3 * HDH), ("wout", HC * D), ("wqh", DC * HDH), ("wkh", DC * HDH), ("wvh", DC * HDH),
          ("wouth", HC * D), ("lng", DC), ("lnb", DC), ("rmsg", DC), ("nk", HC * H8)],
    "E": [("wqv", 4 * DC * D), ("w1", DC), ("w2", DC), ("w3", DC)],
    "F": [(n, DC * D) for n in ("wf", "wi", "wc", "wo", "uf", "ui", "uc", "uo")] + [("bias", 3 * DC), ("c0", DC)],
    "G": [("wq", DC * D), ("wk", DC * D), ("wv", DC * D), ("wp", DC * D), ("bq", DC), ("bk", DC)],
    "H": [("gate", DC * NE)],
}
ROWS = {"A": [("bv", D), ("bp", D)], "B": [("bproj", D)], "D": [("rtq", D), ("rtkv", D), ("nullq", D), ("nv", HDH)],
        "E": [("bqv", D), ("bsim", 1)], "F": [("bo", D)], "G": [("bv", D), ("bp", D)]}
LOADS = {"A": 32, "B": 48, "C": 16, "D": 64, "E": 32, "F": 32, "G": 32, "H": 80}


def columns(pack):
    at, out = 0, {}
    for name, n in pack:
        out[name] = (at, at + n)
        at += n
    return out, at


class Chain:

    def __init__(self, eng, sem):
        self.eng, self.sem, self.base, self.k, self.i, self.per = eng, sem, 0, 0, None, 0

    def link(self, ins):
        ins.then_inc(self.sem, 1)
        self.k += 1
        if self.i is None:
            self.eng.wait_ge(self.sem, self.base + self.k)
        else:
            self.eng.wait_ge(self.sem, self.i * self.per + (self.base + self.k))

    def follow(self, ins):
        ins.then_inc(self.sem, 1)
        self.k += 1
        self.eng.wait_ge(self.sem, self.base + self.k - 1)

    def settle(self):
        self.eng.wait_ge(self.sem, self.base + self.k)

    def begin(self, i, per):
        self.base += self.k
        self.i, self.per, self.k = i, per, 0

    def end(self, trips):
        assert self.k == self.per, (self.k, self.per)
        self.base, self.i, self.k = self.base + trips * self.per, None, 0


def nth(i, per, k):
    return i * per + (k + 1)


TOTALS = {
    "xn_ready": {"A": 16, "B": 16, "C": 16, "D": 16, "E": 16, "F": 16, "G": 16, "H": 16},
    "xT_ps": {"A": 8, "B": 8, "C": 8, "D": 16, "E": 8, "F": 8, "G": 8, "H": 8},
    "xT_ready": {"A": 8, "B": 8, "C": 8, "D": 16, "E": 8, "F": 8, "G": 8, "H": 8},
    "x_new": {"A": 16, "B": 16, "C": 16, "D": 16, "E": 16, "F": 16, "G": 16, "H": 16},
    "y_ps": {"A": 16, "B": 16, "C": 16, "D": 16, "E": 16, "F": 8, "G": 16, "H": 16},
    "var": {"A": 1, "B": 1, "C": 1, "Dx": 1, "Dh": 1, "E": 1, "F": 1, "G": 1, "H": 1},
    "std": {"A": 1, "B": 1, "C": 1, "Dx": 1, "Dh": 1, "E": 1, "F": 1, "G": 1, "H": 1},
    "q_ps": {"A": 8, "D": 16, "G": 8},
    "q_ready": {"A": 8, "D": 16, "G": 8},
    "s_ps": {"A": 32, "C": 8, "D": 32, "E": 16, "G": 32},
    "p_ready": {"A": 32, "D": 32, "E": 16, "G": 32},
    "pT_ps": {"A": 32, "D": 32, "G": 32},
    "pT_ready": {"A": 32, "D": 32, "G": 32},
    "o_ps": {"A": 32, "D": 32, "G": 32},
    "on_ready": {"A": 32, "D": 32, "G": 32},
    "oT_ps": {"A": 16, "D": 32, "G": 16},
    "oT_ready": {"A": 16, "D": 32, "G": 16},
    "a_ready": {"C": 8, "E": 8},
    "aT_ps": {"C": 8, "E": 8},
    "aT_ready": {"C": 8, "E": 8},
    "kv_ps": {"A": 1, "G": 1},
    "kv_ready": {"A": 1, "G": 1},
    "sub_ready": {"A": 32, "G": 32},
}


def done(layer, name):
    total = 0
    for each, count in TOTALS[name].items():
        if each == layer:
            return total
        total += count


def build(nc, ins, out):
    ctx = ExitStack()
    with ctx:
        def sb(name, shape, dt=F32):
            return ctx.enter_context(nc.sbuf_tensor(name, shape, dt))

        sems = {}

        def sem(name):
            if name not in sems:
                sems[name] = ctx.enter_context(nc.semaphore(name))
            return sems[name]

        x = sb("x", [P, NT, D])
        hall = sb("hall", [P, NT, D])
        work = sb("work", [P, 9216])
        stats = sb("stats", [P, NT, 6])
        mean = sb("mean", [P, NT, 1])
        rstd = sb("rstd", [P, NT, 1])
        small = sb("small", [P, 512])
        gates = sb("gates", [P, 8])
        ctxT = sb("ctxT", [P, DC, B * SC])
        ctxN = sb("ctxN", [SC, B, D])
        maskR = sb("maskR", [B, HT, 2 * P], BF16)
        maskL = sb("maskL", [B, P], BF16)
        route = sb("route", [P, 640])
        mask8 = sb("mask8", [SC, B], U8)
        maskrow8 = sb("maskrow8", [1, B, SC], U8)
        big = sb("big", [P, 12288])
        dpack = sb("dpack", [P, columns(PACKS["D"])[1]])
        place, at_big, at_d = {"D": dpack}, 0, 0
        for name in ("A", "B", "lora"):
            n = columns(PACKS[name])[1]
            place[name] = big[0:RANK if name == "lora" else P, at_big:at_big + n]
            at_big += n
        for name in ("G", "H"):
            n = columns(PACKS[name])[1]
            place[name] = dpack[:, at_d:at_d + n]
            at_d += n
        bias_sb = dpack[:, at_d:at_d + 2 * H16 * SC].rearrange("p (j n) -> p j n", j=2)
        at_d += 2 * H16 * SC
        esel = dpack[0:3 * NE, at_d:at_d + NE * P // 2].bitcast(BF16).rearrange("p (e n) -> p e n", e=NE)
        packs, pk = {}, {}
        for name, pack in PACKS.items():
            cols, n = columns(pack)
            packs[name] = place[name] if name in place else sb(f"pack_{name}", [P, n])
            pk[name] = {k: packs[name][:, a:b] for k, (a, b) in cols.items()}
        rows, rw = {}, {}
        for name, pack in ROWS.items():
            cols, n = columns(pack)
            rows[name] = sb(f"rows_{name}", [P, n])
            rw[name] = {k: rows[name][:, a:b] for k, (a, b) in cols.items()}
        ps = ctx.enter_context(nc.psum_tensor("ps", [P, 8, 512], F32))
        ident = pk["const"]["ident"]
        ones = pk["const"]["ones"]

        def carve(specs, base=work, at=0):
            views = {}
            for name, dims in specs:
                n = int(np.prod(dims))
                assert at + n <= base.shape[1], name
                v = base[:, at:at + n]
                at += n
                if len(dims) == 2:
                    v = v.rearrange("p (a b) -> p a b", a=dims[0])
                elif len(dims) == 3:
                    v = v.rearrange("p (a b c) -> p a b c", a=dims[0], b=dims[1])
                elif len(dims) == 4:
                    v = v.rearrange("p (a b c d) -> p a b c d", a=dims[0], b=dims[1], c=dims[2])
                views[name] = v
            return views

        score_rows = nc.dram_tensor("score_rows", (2 * B * HT, P), F32, kind="Internal").ap()
        hflat = hall[:, :, :].rearrange("p t d -> p (t d)")
        KV = carve([("kbd", (DC, B, HPC * SC)), ("vaug", (B, H16, HD16 + 1)), ("kmask", (512,))], hflat)
        keep = small[0:SC, 0:B]
        maskrow = sb("maskrow", [1, B, SC], BF16)
        onesb = sb("onesb", [1, P], BF16)

        block = ctx.enter_context(nc.Block())

        UNITS = [(b, c) for b in range(B) for c in range(DC)]
        NU = len(UNITS)
        A = carve([("xn", (B, D)), ("xnT", (DC, B * P)), ("qT", (DC, B * P)), ("sub", (2, HPC * SC)),
                   ("p", (2, HPC * SC)), ("pT", (2, HPC * P)), ("on", (2, P)), ("oT", (B, D)), ("tmp", (B, D)),
                   ("mx", (2, HPC)), ("den", (2, HPC)), ("em", (NU, HPC)), ("rden", (2, HPC))])
        S_BANK = [0, 2]
        XT_BANK, Q_BANK, PT_BANK = 0, 1, 6
        O_REG = ps[:, 4, 0:HPC * (HD16 + 1)]
        OT_REG, Y_REG = ps[:, 5, 0:D], ps[:, 5, D:2 * D]

        def s_psum(u):
            return ps[:, S_BANK[u % 2]:S_BANK[u % 2] + 2, 0:4 * SC].rearrange("p k (h s) -> p k h s", h=4)

        def quad(ap):
            return ap.rearrange("p (k h s) -> p k h s", k=2, h=4)

        def load_bias(sp):
            def load(n, j):
                sp.dma_start(bias_sb[:, j, :].rearrange("p (h s) -> p h s", h=H16),
                             ins["fside"][:, :, bass.ds(n * P, P), :].rearrange("o h p s -> p (o h) s")
                             ).then_inc(sem(f"G_bias_in{j}"), 16)

            load(0, 0)
            load(1, 1)
            with sp.Fori(1, HT // 2) as i:
                for j in range(2):
                    sp.wait_ge(sem("G_bias_free"), i * 2 + (j - 1))
                    load(i * 2 + j, j)

        def heads16_pe(pe, L):
            w = pk[L]
            s = lambda n: sem(n if n in TOTALS else f"{L}_{n}")
            pe.wait_ge(sem("const_in"), 96)
            pe.wait_ge(sem(f"{L}_in"), LOADS[L])
            for c in range(DC):
                for ci in range(DC):
                    mm = nc.tensor.matmul(ps[:, c, 0:B * SC], w["wk"][:, ci * D + c * P:ci * D + (c + 1) * P],
                                          ctxT[:, ci, :], start=ci == 0, stop=ci == DC - 1)
            for b in range(B):
                for ci in range(DC):
                    mm = nc.tensor.matmul(ps[0:SC, 2 + b, 0:D], ctxT[:, ci, b * SC:(b + 1) * SC],
                                          w["wv"][:, ci * D:(ci + 1) * D], start=ci == 0, stop=ci == DC - 1)
            mm.then_inc(s("kv_ps"), 1)
            pe.wait_ge(s("kv_ready"), 1 + done(L, "kv_ready"))

            def turn_x(n):
                for b in range(B):
                    pe.wait_ge(s("xn_ready"), nth(n, B, b) + done(L, "xn_ready"))
                    for c in range(DC):
                        mm = nc.tensor.transpose(ps[:, XT_BANK, c * D + b * P:c * D + (b + 1) * P],
                                                 A["xn"][:, b, c * P:(c + 1) * P], ident)
                mm.then_inc(s("xT_ps"), 1)

            def queries(n):
                pe.wait_ge(s("xT_ready"), nth(n, 1, 0) + done(L, "xT_ready"))
                for co in range(DC):
                    for ci in range(DC):
                        mm = nc.tensor.matmul(ps[:, Q_BANK, co * D:(co + 1) * D],
                                              w["wq"][:, ci * D + co * P:ci * D + (co + 1) * P],
                                              A["xnT"][:, ci, :], start=ci == 0, stop=ci == DC - 1)
                mm.then_inc(s("q_ps"), 1)

            def scores(i, u):
                b, c = UNITS[u]
                if u == 0:
                    pe.wait_ge(s("q_ready"), nth(i, 1, 0) + done(L, "q_ready"))
                if u >= 2:
                    pe.wait_ge(s("sub_ready"), nth(i, NU, u - 2) + done(L, "sub_ready"))
                for k in range(2):
                    o = ps[:, S_BANK[u % 2] + k, 0:4 * SC]
                    mm = nc.tensor.matmul(o, A["qT"][:, c, b * P:(b + 1) * P],
                                          KV["kbd"][:, c, b, k * 4 * SC:(k + 1) * 4 * SC], start=True, stop=L == "A")
                    if L == "G":
                        for h in range(4):
                            mm = nc.tensor.matmul(ps[:, S_BANK[u % 2] + k, h * SC:(h + 1) * SC], onesb[:, :],
                                                  maskrow[:, b, :], start=False, stop=h == 3)
                mm.then_inc(s("s_ps"), 1)

            def pair(i, more):
                def turn_p(u):
                    pe.wait_ge(s("p_ready"), nth(i, NU, u) + done(L, "p_ready"))
                    if u >= 1:
                        pe.wait_ge(s("pT_ready"), nth(i, NU, u - 1) + done(L, "pT_ready"))
                    for h in range(HPC):
                        mm = nc.tensor.transpose(ps[0:SC, PT_BANK + h // 4, h % 4 * P:(h % 4 + 1) * P],
                                                 A["p"][:, u % 2, h * SC:(h + 1) * SC], ident)
                    mm.then_inc(s("pT_ps"), 1)

                def weigh_v(u):
                    b, c = UNITS[u]
                    pe.wait_ge(s("pT_ready"), nth(i, NU, u) + done(L, "pT_ready"))
                    if u >= 1:
                        pe.wait_ge(s("on_ready"), nth(i, NU, u - 1) + done(L, "on_ready"))
                    for h in range(HPC):
                        mm = nc.tensor.matmul(O_REG[:, h * 17:h * 17 + 17],
                                              A["pT"][0:SC, u % 2, h * P:(h + 1) * P],
                                              KV["vaug"][0:SC, b, c * HPC + h, :], start=True, stop=True)
                    mm.then_inc(s("o_ps"), 1)

                def turn_o(b):
                    pe.wait_ge(s("on_ready"), nth(i, NU, 2 * b + 1) + done(L, "on_ready"))
                    if b == 1:
                        pe.wait_ge(s("x_new"), nth(i, B, 0) + done(L, "x_new"))
                    for c in range(DC):
                        mm = nc.tensor.transpose(OT_REG[:, c * P:(c + 1) * P], A["on"][:, (2 * b + c) % 2, :], ident)
                    mm.then_inc(s("oT_ps"), 1)

                def project(b):
                    pe.wait_ge(s("oT_ready"), nth(i, B, b) + done(L, "oT_ready"))
                    for c in range(DC):
                        mm = nc.tensor.matmul(Y_REG, A["oT"][:, b, c * P:(c + 1) * P], w["wp"][:, c * D:(c + 1) * D],
                                              start=c == 0, stop=c == DC - 1)
                    mm.then_inc(s("y_ps"), 1)

                scores(i, 1)
                turn_p(0)
                scores(i, 2)
                weigh_v(0)
                turn_p(1)
                scores(i, 3)
                weigh_v(1)
                turn_p(2)
                if more:
                    turn_x(i + 1)
                turn_o(0)
                weigh_v(2)
                turn_p(3)
                if more:
                    queries(i + 1)
                project(0)
                weigh_v(3)
                if more:
                    scores(i + 1, 0)
                turn_o(1)
                project(1)

            turn_x(0)
            queries(0)
            scores(0, 0)
            with pe.Fori(0, HT - 1) as i:
                pair(i, True)
            pair(HT - 1, False)

        def heads16_act(act, L):
            s = lambda n: sem(n if n in TOTALS else f"{L}_{n}")
            def take_x(n):
                act.wait_ge(s("xT_ps"), nth(n, 1, 0) + done(L, "xT_ps"))
                nc.scalar.copy(A["xnT"], ps[:, XT_BANK, :].rearrange("p (c n) -> p c n", c=DC)).then_inc(s("xT_ready"), 1)

            def exps(i, u):
                act.wait_ge(s("sub_ready"), nth(i, NU, u) + done(L, "sub_ready"))
                if u >= 2:
                    act.wait_ge(s("pT_ps"), nth(i, NU, u - 2) + done(L, "pT_ps"))
                if L == "A":
                    nc.scalar.activation(A["em"][:, u, :], A["mx"][:, u % 2, :], ACT.Exp,
                                         scale=-1.0).then_inc(s("em_ready"), 1)
                nc.scalar.activation(A["p"][:, u % 2, :], A["sub"][:, u % 2, :], ACT.Exp).then_inc(s("p_ready"), 1)

            def pair(i, more):
                def take_pT(u):
                    act.wait_ge(s("pT_ps"), nth(i, NU, u) + done(L, "pT_ps"))
                    if u >= 2:
                        act.wait_ge(s("o_ps"), nth(i, NU, u - 2) + done(L, "o_ps"))
                    nc.scalar.copy(A["pT"][0:SC, u % 2, :].rearrange("p (k n) -> p k n", k=2),
                                   ps[0:SC, PT_BANK:PT_BANK + 2, :]).then_inc(s("pT_ready"), 1)

                def take_oT(b):
                    act.wait_ge(s("oT_ps"), nth(i, B, b) + done(L, "oT_ps"))
                    nc.scalar.copy(A["oT"][:, b, :], OT_REG).then_inc(s("oT_ready"), 1)

                take_pT(0)
                exps(i, 1)
                take_pT(1)
                exps(i, 2)
                exps(i, 3)
                take_pT(2)
                if more:
                    take_x(i + 1)
                take_oT(0)
                take_pT(3)
                take_oT(1)
                if more:
                    exps(i + 1, 0)

            take_x(0)
            exps(0, 0)
            with act.Fori(0, HT - 1) as i:
                pair(i, True)
            pair(HT - 1, False)

        def finish(t, y, bias, gate, tmp, done):
            if bias is not None:
                chain_dve.link(nc.vector.tensor_tensor(tmp, y, bias, ALU.add))
                y = tmp
            chain_dve.link(nc.vector.scalar_tensor_tensor(out=x[:, t, :], in0=y, scalar=gates[:, gate:gate + 1], in1=x[:, t, :],
                                         op0=ALU.mult, op1=ALU.add))
            nc.vector.bn_stats(stats[:, t, :], x[:, t, :]).then_inc(done, 1)

        def heads16_dve(dve, L):
            link = chain_dve.link
            w = pk[L]
            s = lambda n: sem(n if n in TOTALS else f"{L}_{n}")
            ve = nc.vector
            dve.wait_ge(sem("const_in"), 96)
            dve.wait_ge(sem(f"{L}_in"), LOADS[L])
            dve.wait_ge(s("kv_ps"), 1 + done(L, "kv_ps"))
            hm = pk["const"]["headmask"]
            for c in range(DC):
                for b in range(B):
                    link(ve.scalar_tensor_tensor(
                        out=KV["kbd"][:, c, b, :].rearrange("p (h s) -> p h s", h=HPC),
                        in0=ps[:, c, b * SC:(b + 1) * SC].rearrange("p (o s) -> p o s", o=1).to_broadcast([P, HPC, SC]),
                        scalar=w["bk"][:, c:c + 1], in1=hm.rearrange("p (h o) -> p h o", o=1).to_broadcast([P, HPC, SC]),
                        op0=ALU.add, op1=ALU.mult))
            if L == "G":
                link(ve.tensor_copy(keep, mask8[:, :]))
                link(ve.tensor_scalar(keep, keep, -1.0, 1.0, ALU.mult, ALU.add))
                link(ve.tensor_copy(small[0:1, 8:8 + B * SC], maskrow8[:, :, :].rearrange("p b s -> p (b s)")))
                link(ve.tensor_scalar(maskrow[:, :, :].rearrange("p b s -> p (b s)"), small[0:1, 8:8 + B * SC], NEG, None, ALU.mult))
                link(ve.memset(onesb[:, :], 1.0))
            link(ve.memset(KV["vaug"][0:SC], 1.0))
            for b in range(B):
                link(ve.tensor_tensor(KV["vaug"][0:SC, b, :, 0:HD16],
                                      ps[0:SC, 2 + b, 0:D].rearrange("p (h e) -> p h e", h=H16),
                                      rw[L]["bv"][0:SC, :].rearrange("p (h e) -> p h e", h=H16), ALU.add))
                if L == "G":
                    link(ve.tensor_scalar(KV["vaug"][0:SC, b], KV["vaug"][0:SC, b], keep[:, b:b + 1], None, ALU.mult))
            link(ve.memset(small[:, 511:512], 0.0))
            dve.sem_inc(s("kv_ready"), 1)

            def normed(n):
                for b in range(B):
                    t = n + b * HT
                    ve.tensor_scalar(A["xn"][:, b, :], x[:, t, :], mean[:, t, :], rstd[:, t, :],
                                     ALU.subtract, ALU.mult).then_inc(s("xn_ready"), 1)

            def take_q(n):
                dve.wait_ge(s("q_ps"), nth(n, 1, 0) + done(L, "q_ps"))
                for c in range(DC):
                    q = ve.tensor_scalar(A["qT"][:, c, :], ps[:, Q_BANK, c * D:(c + 1) * D], w["bq"][:, c:c + 1],
                                         HD16 ** -0.5, ALU.add, ALU.mult)
                    if c == 0:
                        link(q)
                    else:
                        q.then_inc(s("q_ready"), 1)

            def shift(i, j, u):
                n = i if j is None else i * 2 + j
                b, c = UNITS[u]
                m = A["mx"][:, u % 2, :]
                dve.wait_ge(s("s_ps"), nth(n, NU, u) + done(L, "s_ps"))
                if u >= 2:
                    dve.wait_ge(s("p_ready"), nth(n, NU, u - 2) + done(L, "p_ready"))
                src = s_psum(u)
                if L == "G":
                    if u == 0:
                        dve.wait_ge(sem(f"G_bias_in{j}"), nth(i, 1, 0) * 16)
                    ins_ = ve.tensor_tensor(quad(A["sub"][:, u % 2, :]), src,
                                            quad(bias_sb[:, j, c * HPC * SC:(c + 1) * HPC * SC]), ALU.add)
                    if u == NU - 1:
                        ins_.then_inc(s("bias_free"), 1)
                        dve.wait_ge(s("bias_free"), nth(n, 1, 0))
                    else:
                        link(ins_)
                    src = quad(A["sub"][:, u % 2, :])
                link(ve.tensor_reduce(m.rearrange("p (k h) -> p k h", k=2), src, AX.X, ALU.max))
                ve.tensor_tensor(quad(A["sub"][:, u % 2, :]), src,
                                 m.rearrange("p (k h o) -> p k h o", k=2, o=1).to_broadcast([P, 2, 4, SC]),
                                 ALU.subtract).then_inc(s("sub_ready"), 1)

            def pair(i, j=None, more=True):
                n = i if j is None else i * 2 + j

                def normalise(u):
                    o = O_REG.rearrange("p (h e) -> p h e", h=HPC)
                    den = A["den"][:, u % 2, :]
                    dve.wait_ge(s("o_ps"), nth(n, NU, u) + done(L, "o_ps"))
                    if L == "A":
                        dve.wait_ge(s("em_ready"), nth(n, NU, u))
                        link(ve.tensor_scalar(A["em"][:, u, :], A["em"][:, u, :], 0.0, 1.0, ALU.mult, ALU.add))
                        link(ve.tensor_tensor(den, A["em"][:, u, :], o[:, :, HD16], ALU.add))
                    else:
                        link(ve.tensor_scalar(den, o[:, :, HD16], 1e-6, None, ALU.max))
                    link(ve.reciprocal(A["rden"][:, u % 2, :], den))
                    if u >= 2:
                        dve.wait_ge(s("oT_ps"), nth(n, B, u // 2 - 1) + done(L, "oT_ps"))
                    ve.tensor_tensor(A["on"][:, u % 2, :].rearrange("p (h e) -> p h e", h=HPC), o[:, :, 0:HD16],
                                     A["rden"][:, u % 2, :].rearrange("p (h o) -> p h o", o=1).to_broadcast([P, HPC, HD16]),
                                     ALU.mult).then_inc(s("on_ready"), 1)

                def update(b):
                    dve.wait_ge(s("y_ps"), nth(n, B, b) + done(L, "y_ps"))
                    finish(n + b * HT, Y_REG, rw[L]["bp"], {"A": 0, "G": 3}[L], A["tmp"][:, b, :], s("x_new"))

                shift(i, j, 1)
                shift(i, j, 2)
                normalise(0)
                if more:
                    normed(n + 1)
                shift(i, j, 3)
                normalise(1)
                normalise(2)
                if more:
                    take_q(n + 1)
                update(0)
                normalise(3)
                if more:
                    shift(*((i + 1, None) if j is None else (i, 1) if j == 0 else (i + 1, 0)), 0)
                update(1)

            normed(0)
            if L == "A":
                ffn_max_dve(dve)
            take_q(0)
            if L == "A":
                ffn_inv_dve(dve)
            shift(0, None if L == "A" else 0, 0)
            if L == "A":
                per = 1 + 4 * 1 + 4 * 3 + 2 * 2
                with dve.Fori(0, HT - 1) as i:
                    chain_dve.begin(i, per)
                    pair(i)
                chain_dve.end(HT - 1)
                pair(HT - 1, more=False)
            else:
                per = 2 * (1 + 3 * 2 + 1 + 4 * 2 + 2 * 2)
                with dve.Fori(0, HT // 2 - 1) as i:
                    chain_dve.begin(i, per)
                    for j in range(2):
                        pair(i, j)
                chain_dve.end(HT // 2 - 1)
                pair(HT // 2 - 1, 0)
                pair(HT // 2 - 1, 1, more=False)

        def norm_dve(dve, L):
            link, ve = chain_dve.link, nc.vector
            m0, m1, v0, v1 = (stats[:, :, k] for k in (1, 4, 2, 5))
            half, t1 = small[:, 256:256 + NT], small[:, 272:272 + NT]
            link(ve.tensor_tensor(t1, m0, m1, ALU.add))
            link(ve.tensor_scalar(mean[:, :, 0], t1, 0.5, None, ALU.mult))
            link(ve.tensor_tensor(half, m0, m1, ALU.subtract))
            link(ve.scalar_tensor_tensor(out=half, in0=half, scalar=0.25, in1=half, op0=ALU.mult, op1=ALU.mult))
            link(ve.tensor_tensor(t1, v0, v1, ALU.add))
            link(ve.scalar_tensor_tensor(out=t1, in0=t1, scalar=1.0 / D, in1=half, op0=ALU.mult, op1=ALU.add))
            ve.tensor_scalar(rstd[:, :, 0], t1, EPS, None, ALU.add).then_inc(sem("var"), 1)
            dve.wait_ge(sem("std"), 1 + done(L, "std"))
            link(ve.reciprocal(rstd[:, :, 0], rstd[:, :, 0]))

        def norm_act(act, L):
            act.wait_ge(sem("var"), 1 + done(L, "var"))
            nc.scalar.activation(rstd[:, :, 0], rstd[:, :, 0], ACT.Sqrt).then_inc(sem("std"), 1)

        BW = carve([("xn", (B, D)), ("xnT", (DC, B * P)), ("hT", (FC, B * P)), ("tmp", (B, D))])

        quant = big[:, at_big:at_big + DC * F0]
        assert at_big + DC * F0 <= big.shape[1]

        def ffn_max_dve(dve):
            dve.wait_ge(sem("B_in"), LOADS["B"])
            for k, name in enumerate(("fc", "proj")):
                nc.vector.tensor_reduce(small[:, 300 + k:301 + k], pk["B"][name], AX.X, ALU.max,
                                        apply_absolute_value=True).then_inc(sem("B_absmax"), 1)

        def ffn_setup_pool(pool):
            gp = nc.gpsimd
            chain = Chain(pool, sem("B_quant"))
            pool.wait_ge(sem("B_in"), LOADS["B"])
            for k in range(2):
                mxa, scale = (small[:, c + k:c + k + 1] for c in (304, 302))
                pool.wait_ge(sem("B_absmax"), k + 1)
                chain.link(gp.partition_all_reduce(mxa, small[:, 300 + k:301 + k], P, bass.bass_isa.ReduceOp.max))
                gp.tensor_scalar(scale, mxa, 1.0 / 127.0, 0.0, ALU.mult, ALU.add).then_inc(sem("B_scale"), 1)
                pool.wait_ge(sem("B_scale"), k + 1)
            for k, name in enumerate(("fc", "proj")):
                w, q = pk["B"][name], quant
                scale, inv = (small[:, c + k:c + k + 1] for c in (302, 306))
                pool.wait_ge(sem("B_inv"), k + 1)
                chain.link(gp.tensor_scalar(q, w, inv, MAGIC, ALU.mult, ALU.add))
                chain.link(gp.tensor_scalar(q, q, -MAGIC, 1.0, ALU.add, ALU.mult))
                chain.link(gp.tensor_scalar(q, q, 127.0, -128.0, ALU.min, ALU.max))
                chain.link(gp.tensor_scalar(q, q, scale, 0.0, ALU.mult, ALU.add))
                chain.link(gp.tensor_tensor(q, q, w, ALU.subtract))
                gp.tensor_tensor(w, w, q, ALU.add).then_inc(sem("B_quantised"), 1)
                pool.wait_ge(sem("B_quantised"), k + 1)

        def ffn_inv_dve(dve):
            for k in range(2):
                dve.wait_ge(sem("B_scale"), k + 1)
                nc.vector.reciprocal(small[:, 306 + k:307 + k], small[:, 302 + k:303 + k]).then_inc(sem("B_inv"), 1)

        def ffn_setup_dve(dve):
            dve.wait_ge(sem("B_quantised"), 2)
            dve.wait_ge(sem("B_lora"), 1)
            for k, name in enumerate(("fc", "proj")):
                w = pk["B"][name]
                src = ps[:, 4 * k:4 * k + 4, :].rearrange("p k n -> p (k n)")
                chain_dve.link(nc.vector.scalar_tensor_tensor(out=w, in0=src, scalar=2.0, in1=w, op0=ALU.mult, op1=ALU.add))
            dve.sem_inc(sem("B_weights"), 1)

        def ffn_pe(pe):
            w, lo = pk["B"], pk["lora"]
            pe.wait_ge(sem("B_in"), LOADS["B"])
            pe.wait_ge(sem("x_new"), NT + done("A", "x_new"))
            for c in range(DC):
                for n in range(F0 // 512):
                    nc.tensor.matmul(ps[:, c * 2 + n, :], lo["afc"][:, c * P:(c + 1) * P],
                                     lo["bfcT"][:, n * 512:(n + 1) * 512], start=True, stop=True)
            for f in range(FC):
                mm = nc.tensor.matmul(ps[:, 4 + f // 2, f % 2 * D:(f % 2 + 1) * D], lo["aproj"][:, f * P:(f + 1) * P],
                                      lo["bprojT"], start=True, stop=True)
            mm.then_inc(sem("B_lora"), 1)
            pe.wait_ge(sem("B_weights"), 1)

            def turn_x(n):
                for b in range(B):
                    pe.wait_ge(sem("xn_ready"), nth(n, B, b) + done("B", "xn_ready"))
                    for c in range(DC):
                        mm = nc.tensor.transpose(ps[:, 0, c * D + b * P:c * D + (b + 1) * P],
                                                 BW["xn"][:, b, c * P:(c + 1) * P], ident)
                mm.then_inc(sem("xT_ps"), 1)

            def pair(n, more):
                pe.wait_ge(sem("xT_ready"), nth(n, 1, 0) + done("B", "xT_ready"))
                for f in range(FC):
                    for c in range(DC):
                        mm = nc.tensor.matmul(ps[:, 1 + f // 2, f % 2 * D:(f % 2 + 1) * D],
                                              w["fc"][:, c * F0 + f * P:c * F0 + (f + 1) * P], BW["xnT"][:, c, :],
                                              start=c == 0, stop=c == DC - 1)
                    if f % 2:
                        mm.then_inc(sem("B_h_ps"), 1)
                if more:
                    turn_x(n + 1)
                for b in range(B):
                    pe.wait_ge(sem("x_new"), nth(n, B, b) - B + done("B", "x_new"))
                    for f in range(FC):
                        if b == 0:
                            pe.wait_ge(sem("B_h_ready"), nth(n, FC, f))
                        mm = nc.tensor.matmul(ps[:, 5 + b, 0:D], BW["hT"][:, f, b * P:(b + 1) * P],
                                              w["proj"][:, f * D:(f + 1) * D], start=f == 0, stop=f == FC - 1)
                    mm.then_inc(sem("y_ps"), 1)

            turn_x(0)
            with pe.Fori(0, HT - 1) as i:
                pair(i, True)
            pair(HT - 1, False)

        def ffn_act(act):
            def take_x(n):
                act.wait_ge(sem("xT_ps"), nth(n, 1, 0) + done("B", "xT_ps"))
                nc.scalar.copy(BW["xnT"], ps[:, 0, :].rearrange("p (c n) -> p c n", c=DC)).then_inc(sem("xT_ready"), 1)

            def pair(n, more):
                for f in range(FC):
                    act.wait_ge(sem("B_h_ps"), nth(n, FC // 2, f // 2))
                    nc.scalar.activation(BW["hT"][:, f, :], ps[:, 1 + f // 2, f % 2 * D:(f % 2 + 1) * D], ACT.Gelu,
                                         bias=pk["B"]["bfc"][:, f:f + 1]).then_inc(sem("B_h_ready"), 1)
                if more:
                    take_x(n + 1)

            take_x(0)
            with act.Fori(0, HT - 1) as i:
                pair(i, True)
            pair(HT - 1, False)

        def ffn_dve(dve):
            def normed(n):
                for b in range(B):
                    t = n + b * HT
                    nc.vector.tensor_scalar(BW["xn"][:, b, :], x[:, t, :], mean[:, t, :], rstd[:, t, :],
                                            ALU.subtract, ALU.mult).then_inc(sem("xn_ready"), 1)

            def pair(n, more):
                if more:
                    dve.wait_ge(sem("B_h_ps"), nth(n, FC // 2, 0))
                    normed(n + 1)
                for b in range(B):
                    dve.wait_ge(sem("y_ps"), nth(n, B, b) + done("B", "y_ps"))
                    finish(n + b * HT, ps[:, 5 + b, 0:D], rw["B"]["bproj"], 4, BW["tmp"][:, b, :], sem("x_new"))

            normed(0)
            with dve.Fori(0, HT - 1) as i:
                chain_dve.begin(i, 4)
                pair(i, True)
            chain_dve.end(HT - 1)
            pair(HT - 1, False)

        CW = carve([("xn", (B, D)), ("xnT", (DC, B * P)), ("hidT", (B * P,)), ("RT", (DC, B * P)), ("hot", (B, WIN, SC)),
                    ("prod", (B, WIN, SC)), ("a", (B, SC)), ("aT", (B * P,)), ("pos", (6, B)), ("w4", (6, B, WIN))])

        def local_pe(pe):
            w = pk["C"]
            pe.wait_ge(sem("C_in"), LOADS["C"])

            def project_x(n):
                for b in range(B):
                    pe.wait_ge(sem("xn_ready"), nth(n, B, b) + done("C", "xn_ready"))
                    for c in range(DC):
                        mm = nc.tensor.transpose(ps[:, 0, c * D + b * P:c * D + (b + 1) * P],
                                                 CW["xn"][:, b, c * P:(c + 1) * P], ident)
                mm.then_inc(sem("xT_ps"), 1)
                pe.wait_ge(sem("xT_ready"), nth(n, 1, 0) + done("C", "xT_ready"))
                for c in range(DC):
                    mm = nc.tensor.matmul(ps[0:PSZ, 1, 0:B * P], w["wp"][:, c * PSZ:(c + 1) * PSZ], CW["xnT"][:, c, :],
                                          start=c == 0, stop=c == DC - 1)
                mm.then_inc(sem("C_hid_ps"), 1)
                for co in range(DC):
                    for ci in range(DC):
                        mm = nc.tensor.matmul(ps[:, 2, co * D:(co + 1) * D],
                                              w["wa"][:, ci * D + co * P:ci * D + (co + 1) * P], CW["xnT"][:, ci, :],
                                              start=ci == 0, stop=ci == DC - 1)
                mm.then_inc(sem("C_R_ps"), 1)
                pe.wait_ge(sem("C_hid_ready"), nth(n, 1, 0))
                for b in range(B):
                    mm = nc.tensor.matmul(ps[:, 4, b:b + 1], CW["hidT"][0:PSZ, b * P:(b + 1) * P], w["vp"][0:PSZ, :],
                                          start=True, stop=True)
                mm.then_inc(sem("C_z_ps"), 1)

            def scores(n):
                pe.wait_ge(sem("C_R_ready"), nth(n, 1, 0))
                for b in range(B):
                    for c in range(DC):
                        mm = nc.tensor.matmul(ps[:, 3, b * SC:(b + 1) * SC], CW["RT"][:, c, b * P:(b + 1) * P],
                                              ctxT[:, c, b * SC:(b + 1) * SC], start=c == 0, stop=c == DC - 1)
                mm.then_inc(sem("s_ps"), 1)

            def pair(i, more):
                if more:
                    project_x(i + 1)
                pe.wait_ge(sem("a_ready"), nth(i, 1, 0) + done("C", "a_ready"))
                for b in range(B):
                    mm = nc.tensor.transpose(ps[0:SC, 5, b * P:(b + 1) * P], CW["a"][:, b, :], ident)
                mm.then_inc(sem("aT_ps"), 1)
                if more:
                    scores(i + 1)
                pe.wait_ge(sem("aT_ready"), nth(i, 1, 0) + done("C", "aT_ready"))
                for b in range(B):
                    nc.tensor.matmul(ps[:, 6 + b, 0:D], CW["aT"][0:SC, b * P:(b + 1) * P], ctxN[:, b, :],
                                     start=True, stop=True).then_inc(sem("y_ps"), 1)

            project_x(0)
            scores(0)
            with pe.Fori(0, HT - 1) as i:
                pair(i, True)
            pair(HT - 1, False)

        def local_act(act):
            pos, w4 = CW["pos"], CW["w4"]
            def take_x(n):
                act.wait_ge(sem("xT_ps"), nth(n, 1, 0) + done("C", "xT_ps"))
                nc.scalar.copy(CW["xnT"], ps[:, 0, :].rearrange("p (c n) -> p c n", c=DC)).then_inc(sem("xT_ready"), 1)

            def take_hidden(n):
                act.wait_ge(sem("C_hid_ps"), nth(n, 1, 0))
                nc.scalar.activation(CW["hidT"][0:PSZ, :], ps[0:PSZ, 1, 0:B * P], ACT.Tanh).then_inc(sem("C_hid_ready"), 1)

            def take_R(n):
                act.wait_ge(sem("C_R_ps"), nth(n, 1, 0))
                nc.scalar.copy(CW["RT"], ps[:, 2, :].rearrange("p (c n) -> p c n", c=DC)).then_inc(sem("C_R_ready"), 1)

            def take_z(n):
                act.wait_ge(sem("C_z_ps"), nth(n, 1, 0))
                nc.scalar.activation(pos[:, 0, :], ps[:, 4, 0:B], ACT.Exp, scale=-1.0).then_inc(sem("C_ez_ready"), 1)

            def pair(i, more):
                if more:
                    take_x(i + 1)
                act.wait_ge(sem("C_d2_ready"), nth(i, 1, 0))
                nc.scalar.activation(w4[:, 2], w4[:, 1], ACT.Exp, scale=-0.5).then_inc(sem("C_gauss_ready"), 1)
                if more:
                    take_hidden(i + 1)
                act.wait_ge(sem("C_sc_ready"), nth(i, 1, 0))
                nc.scalar.activation(w4[:, 4], w4[:, 3], ACT.Exp).then_inc(sem("C_e_ready"), 1)
                if more:
                    take_R(i + 1)
                    take_z(i + 1)
                act.wait_ge(sem("aT_ps"), nth(i, 1, 0) + done("C", "aT_ps"))
                nc.scalar.copy(CW["aT"][0:SC, :], ps[0:SC, 5, 0:B * P]).then_inc(sem("aT_ready"), 1)

            take_x(0)
            take_hidden(0)
            take_R(0)
            take_z(0)
            with act.Fori(0, HT - 1) as i:
                pair(i, True)
            pair(HT - 1, False)

        def local_dve(dve):
            link, ve = chain_dve.link, nc.vector
            pos, w4 = CW["pos"], CW["w4"]
            hot, prod = CW["hot"], CW["prod"]
            iota = pk["C"]["iota"].rearrange("p (o s) -> p o s", o=1)
            woff = pk["C"]["woff"].rearrange("p (o w) -> p o w", o=1)

            def per_tok(v):
                return v.rearrange("p (b o) -> p b o", o=1).to_broadcast([P, B, WIN])

            def over_s(v):
                return v.rearrange("p b (w o) -> p (b w) o", o=1).to_broadcast([P, B * WIN, SC])

            flat = lambda v: v.rearrange("p b w s -> p (b w) s")
            dve.wait_ge(sem("C_in"), LOADS["C"])

            def normed(n):
                for b in range(B):
                    t = n + b * HT
                    ve.tensor_scalar(CW["xn"][:, b, :], x[:, t, :], mean[:, t, :], rstd[:, t, :],
                                     ALU.subtract, ALU.mult).then_inc(sem("xn_ready"), 1)

            def pair(i, more):
                if more:
                    dve.wait_ge(sem("xT_ps"), nth(i, 1, 0) + done("C", "xT_ps"))
                    normed(i + 1)
                dve.wait_ge(sem("C_ez_ready"), nth(i, 1, 0))
                link(ve.tensor_scalar(pos[:, 0, :], pos[:, 0, :], 1.0, None, ALU.add))
                link(ve.reciprocal(pos[:, 0, :], pos[:, 0, :]))
                link(ve.tensor_scalar(pos[:, 1, :], pos[:, 0, :], float(SC), None, ALU.mult))
                link(ve.tensor_scalar(pos[:, 2, :], pos[:, 1, :], MAGIC, None, ALU.add))
                link(ve.tensor_scalar(pos[:, 2, :], pos[:, 2, :], MAGIC, None, ALU.subtract))
                link(ve.tensor_tensor(pos[:, 3, :], pos[:, 2, :], pos[:, 1, :], ALU.is_gt))
                link(ve.tensor_tensor(pos[:, 2, :], pos[:, 2, :], pos[:, 3, :], ALU.subtract))
                link(ve.tensor_tensor(w4[:, 0], per_tok(pos[:, 2, :]), woff.to_broadcast([P, B, WIN]), ALU.add))
                link(ve.tensor_scalar(w4[:, 0], w4[:, 0], 0.0, float(SC - 1), ALU.max, ALU.min))
                link(ve.tensor_tensor(w4[:, 1], w4[:, 0], per_tok(pos[:, 1, :]), ALU.subtract))
                ve.tensor_tensor(w4[:, 1], w4[:, 1], w4[:, 1], ALU.mult).then_inc(sem("C_d2_ready"), 1)
                link(ve.tensor_tensor(flat(hot), iota.to_broadcast([P, B * WIN, SC]), over_s(w4[:, 0]), ALU.is_equal))
                dve.wait_ge(sem("s_ps"), nth(i, 1, 0) + done("C", "s_ps"))
                for b in range(B):
                    s_b = ps[:, 3, b * SC:(b + 1) * SC].rearrange("p (o s) -> p o s", o=1)
                    link(ve.tensor_tensor(prod[:, b], hot[:, b], s_b.to_broadcast([P, WIN, SC]), ALU.mult))
                link(ve.tensor_reduce(w4[:, 3].rearrange("p b w -> p (b w)"), flat(prod), AX.X, ALU.add))
                link(ve.tensor_reduce(pos[:, 4, :], w4[:, 3], AX.X, ALU.max))
                ve.tensor_tensor(w4[:, 3], w4[:, 3], per_tok(pos[:, 4, :]), ALU.subtract).then_inc(sem("C_sc_ready"), 1)
                dve.wait_ge(sem("C_e_ready"), nth(i, 1, 0))
                link(ve.tensor_reduce(pos[:, 5, :], w4[:, 4], AX.X, ALU.add))
                link(ve.reciprocal(pos[:, 5, :], pos[:, 5, :]))
                dve.wait_ge(sem("C_gauss_ready"), nth(i, 1, 0))
                link(ve.tensor_tensor(w4[:, 5], w4[:, 4], w4[:, 2], ALU.mult))
                link(ve.tensor_tensor(w4[:, 5], w4[:, 5], per_tok(pos[:, 5, :]), ALU.mult))
                link(ve.tensor_tensor(flat(prod), flat(hot), over_s(w4[:, 5]), ALU.mult))
                ve.tensor_reduce(CW["a"], prod.rearrange("p b w s -> p b s w"), AX.X, ALU.add).then_inc(sem("a_ready"), 1)
                for b in range(B):
                    dve.wait_ge(sem("y_ps"), nth(i, B, b) + done("C", "y_ps"))
                    finish(i + b * HT, ps[:, 6 + b, 0:D], None, 1, None, sem("x_new"))

            normed(0)
            with dve.Fori(0, HT - 1) as i:
                chain_dve.begin(i, 20 + 2)
                pair(i, True)
            chain_dve.end(HT - 1)
            pair(HT - 1, False)

        EW = carve([("xn", (B, D)), ("xnT", (DC, B * P)), ("hqT", (DC, B * P)), ("ehT", (DC, B * P)), ("p", (B, SC)),
                    ("aT", (B * P,)), ("RT", (DC, B * SC)), ("simrow", (B * SC,)), ("sim", (NT, SC)), ("mx", (NT, 1)),
                    ("wgt", (NT,)), ("m", (2, B)), ("hc", (DC, B)), ("sum", (2, B, 1)), ("w14", (B, DC, D)), ("tmp", (B, D))])

        def sim_pe(pe):
            w = pk["E"]
            pe.wait_ge(sem("E_in"), LOADS["E"])
            pe.wait_ge(sem("E_setup"), 1)
            for c in range(DC):
                mm = nc.tensor.matmul(ps[0:1, 7, 0:B * SC], w["w2"][:, c:c + 1], ctxT[:, c, :], start=c == 0, stop=c == DC - 1)
            mm.then_inc(sem("E_row_ps"), 1)
            pe.wait_ge(sem("E_row_ready"), 1)

            def turn_x(n):
                for b in range(B):
                    pe.wait_ge(sem("xn_ready"), nth(n, B, b) + done("E", "xn_ready"))
                    for c in range(DC):
                        mm = nc.tensor.transpose(ps[:, 0, c * D + b * P:c * D + (b + 1) * P],
                                                 EW["xn"][:, b, c * P:(c + 1) * P], ident)
                mm.then_inc(sem("xT_ps"), 1)

            def similarity(n):
                pe.wait_ge(sem("xT_ready"), nth(n, 1, 0) + done("E", "xT_ready"))
                for b in range(B):
                    for c in range(DC):
                        nc.tensor.matmul(ps[:, 1 + b, 0:SC], EW["xnT"][:, c, b * P:(b + 1) * P],
                                         EW["RT"][:, c, b * SC:(b + 1) * SC], start=c == 0, stop=False)
                    nc.tensor.matmul(ps[:, 1 + b, 0:SC], ones[0:1, :], EW["simrow"][0:1, b * SC:(b + 1) * SC],
                                     start=False, stop=True).then_inc(sem("s_ps"), 1)

            turn_x(0)
            with pe.Fori(0, HT - 1) as i:
                similarity(i)
                turn_x(i + 1)
                pe.wait_ge(sem("E_sim_ready"), nth(i, B, B - 1))
            similarity(HT - 1)
            pe.wait_ge(sem("E_wgt_ready"), 1)
            pe.wait_ge(sem("E_wsum_ready"), 1)
            pe.wait_ge(sem("E_h_kept"), NT)
            for b in range(B):
                for c in range(DC):
                    for t in range(HT):
                        nc.tensor.matmul(ps[:, 3, c * B + b:c * B + b + 1], hall[:, b * HT + t, c * P:(c + 1) * P],
                                         EW["wgt"][:, b * HT + t:b * HT + t + 1], start=t == 0, stop=t == HT - 1)
            mm = nc.tensor.matmul(ps[:, 4, 0:B], ones, EW["m"][:, 0, :], start=True, stop=True)
            mm.then_inc(sem("E_hc_ps"), 1)
            pe.wait_ge(sem("E_w14_ready"), 1)
            with pe.Fori(0, HT) as i:
                for b in range(B):
                    pe.wait_ge(sem("E_h_back"), nth(i, B, b))
                    for c in range(DC):
                        mm = nc.tensor.transpose(ps[:, 0, c * D + b * P:c * D + (b + 1) * P],
                                                 EW["xn"][:, b, c * P:(c + 1) * P], ident)
                mm.then_inc(sem("E_xT2_ps"), 1)
                pe.wait_ge(sem("a_ready"), nth(i, 1, 0) + done("E", "a_ready"))
                for b in range(B):
                    mm = nc.tensor.transpose(ps[0:SC, 1, b * P:(b + 1) * P], EW["p"][:, b, :], ident)
                mm.then_inc(sem("aT_ps"), 1)
                pe.wait_ge(sem("aT_ready"), nth(i, 1, 0) + done("E", "aT_ready"))
                for c in range(DC):
                    for b in range(B):
                        mm = nc.tensor.matmul(ps[:, 2, c * D + b * P:c * D + (b + 1) * P], ctxN[:, b, c * P:(c + 1) * P],
                                              EW["aT"][0:SC, b * P:(b + 1) * P], start=True, stop=True)
                mm.then_inc(sem("E_hq_ps"), 1)
                pe.wait_ge(sem("E_xT2_ready"), nth(i, 1, 0))
                pe.wait_ge(sem("x_new"), nth(i, B, B - 1) - B + done("E", "x_new"))
                for b in range(B):
                    for c in range(DC):
                        nc.tensor.matmul(ps[:, 5 + b, 0:D], EW["xnT"][:, c, b * P:(b + 1) * P], EW["w14"][:, b, c, :],
                                         start=c == 0, stop=False)
                pe.wait_ge(sem("E_hq_ready"), nth(i, 1, 0))
                for b in range(B):
                    for c in range(DC):
                        nc.tensor.matmul(ps[:, 5 + b, 0:D], EW["hqT"][:, c, b * P:(b + 1) * P],
                                         w["wqv"][:, (DC + c) * D:(DC + c + 1) * D], start=False, stop=False)
                pe.wait_ge(sem("E_eh_ready"), nth(i, 1, 0))
                for b in range(B):
                    for c in range(DC):
                        mm = nc.tensor.matmul(ps[:, 5 + b, 0:D], EW["ehT"][:, c, b * P:(b + 1) * P],
                                              w["wqv"][:, (2 * DC + c) * D:(2 * DC + c + 1) * D],
                                              start=False, stop=c == DC - 1)
                    mm.then_inc(sem("y_ps"), 1)

        def sim_pool(pool):
            with pool.Fori(0, HT) as i:
                for b in range(B):
                    pool.wait_ge(sem("xn_ready"), nth(i, B, b) + done("E", "xn_ready"))
                    nc.gpsimd.tensor_copy(hall[:, i + b * HT, :], EW["xn"][:, b, :]).then_inc(sem("E_h_kept"), 1)
            pool.wait_ge(sem("E_m_ready"), 1)
            nc.gpsimd.partition_all_reduce(EW["m"][:, 1, :], EW["m"][:, 0, :], P,
                                           bass.bass_isa.ReduceOp.max).then_inc(sem("E_mall_ready"), 1)
            pool.wait_ge(sem("E_h_kept"), NT)
            pool.wait_ge(sem("E_hc_ps"), 1)
            for i in (0,):
                for b in range(B):
                    nc.gpsimd.tensor_copy(EW["xn"][:, b, :], hall[:, i + b * HT, :]).then_inc(sem("E_h_back"), 1)
            with pool.Fori(1, HT) as i:
                for b in range(B):
                    pool.wait_ge(sem("E_xT2_ps"), i)
                    nc.gpsimd.tensor_copy(EW["xn"][:, b, :], hall[:, i + b * HT, :]).then_inc(sem("E_h_back"), 1)

        def sim_act(act):
            with act.Fori(0, HT) as i:
                act.wait_ge(sem("xT_ps"), nth(i, 1, 0) + done("E", "xT_ps"))
                nc.scalar.copy(EW["xnT"], ps[:, 0, :].rearrange("p (c n) -> p c n", c=DC)).then_inc(sem("xT_ready"), 1)
            act.wait_ge(sem("E_wsub_ready"), 1)
            nc.scalar.activation(EW["wgt"], EW["wgt"], ACT.Exp).then_inc(sem("E_wgt_ready"), 1)
            act.wait_ge(sem("E_sim_ready"), NT)
            with act.Fori(0, HT) as i:
                for b in range(B):
                    t = i + b * HT
                    nc.scalar.activation(EW["p"][:, b, :], EW["sim"][:, t, :], ACT.Exp,
                                         accum_out=EW["sum"][:, 0, b, :]).then_inc(sem("p_ready"), 1)
                act.wait_ge(sem("E_xT2_ps"), nth(i, 1, 0))
                nc.scalar.copy(EW["xnT"], ps[:, 0, :].rearrange("p (c n) -> p c n", c=DC)).then_inc(sem("E_xT2_ready"), 1)
                act.wait_ge(sem("aT_ps"), nth(i, 1, 0) + done("E", "aT_ps"))
                nc.scalar.copy(EW["aT"][0:SC, :], ps[0:SC, 1, 0:B * P]).then_inc(sem("aT_ready"), 1)
                act.wait_ge(sem("E_hq_ps"), nth(i, 1, 0))
                nc.scalar.copy(EW["hqT"], ps[:, 2, :].rearrange("p (c n) -> p c n", c=DC)).then_inc(sem("E_hq_ready"), 1)

        def sim_dve(dve):
            link, ve = chain_dve.link, nc.vector
            w = pk["E"]
            dve.wait_ge(sem("E_in"), LOADS["E"])
            for c in range(DC):
                link(ve.tensor_scalar(EW["RT"][:, c, :], ctxT[:, c, :], w["w3"][:, c:c + 1], w["w1"][:, c:c + 1],
                                      ALU.mult, ALU.add))
            dve.sem_inc(sem("E_setup"), 1)
            dve.wait_ge(sem("E_row_ps"), 1)
            ve.tensor_scalar(EW["simrow"][0:1, :], ps[0:1, 7, 0:B * SC], rw["E"]["bsim"][0:1, :], None,
                             ALU.add).then_inc(sem("E_row_ready"), 1)
            norm_dve(dve, "E")

            def normed(n):
                for b in range(B):
                    t = n + b * HT
                    ve.tensor_scalar(EW["xn"][:, b, :], x[:, t, :], mean[:, t, :], rstd[:, t, :],
                                     ALU.subtract, ALU.mult).then_inc(sem("xn_ready"), 1)

            def pair(i, more):
                if more:
                    dve.wait_ge(sem("xT_ps"), nth(i, 1, 0) + done("E", "xT_ps"))
                    dve.wait_ge(sem("E_h_kept"), nth(i, B, B - 1))
                    normed(i + 1)
                for b in range(B):
                    t = i + b * HT
                    dve.wait_ge(sem("s_ps"), nth(i, B, b) + done("E", "s_ps"))
                    link(ve.tensor_reduce(EW["mx"][:, t, :], ps[:, 1 + b, 0:SC], AX.X, ALU.max))
                    ve.tensor_scalar(EW["sim"][:, t, :], ps[:, 1 + b, 0:SC], EW["mx"][:, t, :], None,
                                     ALU.subtract).then_inc(sem("E_sim_ready"), 1)

            normed(0)
            with dve.Fori(0, HT - 1) as i:
                chain_dve.begin(i, 2)
                pair(i, True)
            chain_dve.end(HT - 1)
            pair(HT - 1, False)
            mx = EW["mx"].rearrange("p (b t) o -> p b (t o)", b=B)
            wgt = EW["wgt"].rearrange("p (b t) -> p b t", b=B)
            ve.tensor_reduce(EW["m"][:, 0, :], mx, AX.X, ALU.max).then_inc(sem("E_m_ready"), 1)
            dve.wait_ge(sem("E_mall_ready"), 1)
            ve.tensor_tensor(wgt, mx, EW["m"][:, 1, :].rearrange("p (b o) -> p b o", o=1).to_broadcast([P, B, HT]),
                             ALU.subtract).then_inc(sem("E_wsub_ready"), 1)
            dve.wait_ge(sem("E_wgt_ready"), 1)
            ve.tensor_reduce(EW["m"][:, 0, :], wgt, AX.X, ALU.add).then_inc(sem("E_wsum_ready"), 1)
            dve.wait_ge(sem("E_hc_ps"), 1)
            link(ve.reciprocal(EW["m"][:, 0, :], ps[:, 4, 0:B]))
            link(ve.tensor_tensor(EW["hc"], ps[:, 3, 0:DC * B].rearrange("p (c b) -> p c b", c=DC),
                                  EW["m"][:, 0, :].rearrange("p (o b) -> p o b", o=1).to_broadcast([P, DC, B]), ALU.mult))
            for b in range(B):
                for c in range(DC):
                    link(ve.scalar_tensor_tensor(out=EW["w14"][:, b, c, :], in0=w["wqv"][:, (3 * DC + c) * D:(3 * DC + c + 1) * D],
                                                 scalar=EW["hc"][:, c, b:b + 1], in1=w["wqv"][:, c * D:(c + 1) * D],
                                                 op0=ALU.mult, op1=ALU.add))
            dve.sem_inc(sem("E_w14_ready"), 1)

            def weights(n):
                for b in range(B):
                    dve.wait_ge(sem("p_ready"), nth(n, B, b) + done("E", "p_ready"))
                    link(ve.reciprocal(EW["sum"][:, 1, b, :], EW["sum"][:, 0, b, :]))
                    a = ve.tensor_scalar(EW["p"][:, b, :], EW["p"][:, b, :], EW["sum"][:, 1, b, :], None, ALU.mult)
                    if b == B - 1:
                        a.then_inc(sem("a_ready"), 1)

            def update(i, more):
                dve.wait_ge(sem("E_hq_ready"), nth(i, 1, 0))
                ve.tensor_tensor(EW["ehT"], EW["xnT"], EW["hqT"], ALU.mult).then_inc(sem("E_eh_ready"), 1)
                if more:
                    weights(i + 1)
                for b in range(B):
                    dve.wait_ge(sem("y_ps"), nth(i, B, b) + done("E", "y_ps"))
                    finish(i + b * HT, ps[:, 5 + b, 0:D], rw["E"]["bqv"], 2, EW["tmp"][:, b, :], sem("x_new"))

            weights(0)
            with dve.Fori(0, HT - 1) as i:
                chain_dve.begin(i, 2 + 2 * 2)
                update(i, True)
            chain_dve.end(HT - 1)
            update(HT - 1, False)

        GW = carve([("xn", (B, D)), ("xnT", (DC, B * P)), ("f", (DC, P)), ("i", (DC, P)), ("g", (DC, P)), ("c1", (DC, P)),
                    ("c2", (DC, P)), ("y", (B, D)), ("bias", (2, 3 * DC)), ("c0", (DC,))])
        GATES = ("f", "i", "g")

        def rnn_pe(pe):
            w = pk["F"]
            pe.wait_ge(sem("F_in"), LOADS["F"])
            pe.wait_ge(sem("x_new"), NT + done("E", "x_new"))
            for g in range(3):
                for co in range(DC):
                    for ci in range(DC):
                        mm = nc.tensor.matmul(ps[:, 7, g * DC + co:g * DC + co + 1],
                                              w["u" + "fic"[g]][:, ci * D + co * P:ci * D + (co + 1) * P],
                                              w["c0"][:, ci:ci + 1], start=ci == 0, stop=ci == DC - 1)
            mm.then_inc(sem("F_u0_ps"), 1)

            def turn_x(n):
                for b in range(B):
                    pe.wait_ge(sem("xn_ready"), nth(n, B, b) + done("F", "xn_ready"))
                    for c in range(DC):
                        mm = nc.tensor.transpose(ps[:, 0, c * D + b * P:c * D + (b + 1) * P],
                                                 GW["xn"][:, b, c * P:(c + 1) * P], ident)
                mm.then_inc(sem("xT_ps"), 1)

            def gate_part(b, g, kind, v):
                for co in range(DC):
                    for ci in range(DC):
                        mm = nc.tensor.matmul(ps[:, 1 + 3 * b + g, co * P:(co + 1) * P],
                                              w[kind + "fic"[g]][:, ci * D + co * P:ci * D + (co + 1) * P], v[:, ci, :],
                                              start=kind == "w" and co == 0 and ci == 0,
                                              stop=(kind == "u" or b == 0) and ci == DC - 1, skip_group_check=True)
                return mm

            def pair(i, more):
                pe.wait_ge(sem("xT_ready"), nth(i, 1, 0) + done("F", "xT_ready"))
                for g in range(3):
                    gate_part(0, g, "w", GW["xnT"][:, :, 0:P]).then_inc(sem("F_z_ps"), 1)
                for g in range(3):
                    gate_part(1, g, "w", GW["xnT"][:, :, P:2 * P])
                pe.wait_ge(sem("F_c1_ready"), nth(i, 1, 0))
                for g in range(3):
                    gate_part(1, g, "u", GW["c1"]).then_inc(sem("F_z_ps"), 1)
                for b in range(B):
                    for ci in range(DC):
                        nc.tensor.matmul(ps[:, 7, b * D:(b + 1) * D], GW["xnT"][:, ci, b * P:(b + 1) * P],
                                         w["wo"][:, ci * D:(ci + 1) * D], start=b == 0 and ci == 0, stop=False, skip_group_check=True)
                if more:
                    turn_x(i + 1)
                pe.wait_ge(sem("F_c2_ready"), nth(i, 1, 0))
                for b in range(B):
                    for ci in range(DC):
                        mm = nc.tensor.matmul(ps[:, 7, b * D:(b + 1) * D], GW["c2"][:, ci, :], w["uo"][:, ci * D:(ci + 1) * D],
                                              start=False, stop=ci == DC - 1, skip_group_check=True)
                mm.then_inc(sem("y_ps"), 1)

            turn_x(0)
            with pe.Fori(0, HT - 1) as i:
                pair(i, True)
            pair(HT - 1, False)

        def rnn_act(act):
            def take_x(n):
                act.wait_ge(sem("xT_ps"), nth(n, 1, 0) + done("F", "xT_ps"))
                nc.scalar.copy(GW["xnT"], ps[:, 0, :].rearrange("p (c n) -> p c n", c=DC)).then_inc(sem("xT_ready"), 1)

            def pair(i, more):
                for b in range(B):
                    for g in range(3):
                        act.wait_ge(sem("F_z_ps"), nth(i, B * 3, b * 3 + g))
                        for co in range(DC):
                            a = nc.scalar.activation(GW[GATES[g]][:, co, :], ps[:, 1 + 3 * b + g, co * P:(co + 1) * P],
                                                     ACT.Tanh, bias=GW["bias"][:, b, g * DC + co:g * DC + co + 1],
                                                     scale=0.5 if g < 2 else 1.0)
                        a.then_inc(sem("F_gate_ready"), 1)
                if more:
                    act.wait_ge(sem("y_ps"), nth(i, 1, 0) + done("F", "y_ps"))
                    take_x(i + 1)
                act.wait_ge(sem("F_ysum_ready"), nth(i, 1, 0))
                nc.scalar.activation(GW["y"], GW["y"], ACT.Tanh).then_inc(sem("F_h_ready"), 1)

            take_x(0)
            with act.Fori(0, HT - 1) as i:
                pair(i, True)
            pair(HT - 1, False)

        def rnn_dve(dve):
            link, ve = chain_dve.link, nc.vector
            w = pk["F"]
            dve.wait_ge(sem("F_in"), LOADS["F"])
            dve.wait_ge(sem("F_u0_ps"), 1)
            b0, b1 = GW["bias"][:, 0, :], GW["bias"][:, 1, :]
            link(ve.tensor_tensor(b0, ps[:, 7, 0:3 * DC], w["bias"], ALU.add))
            link(ve.tensor_scalar(GW["bias"][:, 0, 0:2 * DC], GW["bias"][:, 0, 0:2 * DC], 0.5, None, ALU.mult))
            link(ve.tensor_scalar(GW["bias"][:, 1, 0:2 * DC], w["bias"][:, 0:2 * DC], 0.5, None, ALU.mult))
            link(ve.tensor_copy(GW["bias"][:, 1, 2 * DC:3 * DC], w["bias"][:, 2 * DC:3 * DC]))
            norm_dve(dve, "F")

            def normed(n):
                for b in range(B):
                    t = n + b * HT
                    ve.tensor_scalar(GW["xn"][:, b, :], x[:, t, :], mean[:, t, :], rstd[:, t, :],
                                     ALU.subtract, ALU.mult).then_inc(sem("xn_ready"), 1)

            def pair(i, more):
                if more:
                    dve.wait_ge(sem("xT_ps"), nth(i, 1, 0) + done("F", "xT_ps"))
                    normed(i + 1)
                for b in range(B):
                    dve.wait_ge(sem("F_gate_ready"), nth(i, B * 3, b * 3 + 2))
                    fi = GW["f"].rearrange("p c n -> p (c n)"), GW["i"].rearrange("p c n -> p (c n)")
                    both = work[:, FI_AT:FI_AT + 4 * P]
                    link(ve.tensor_scalar(both, both, 0.5, 0.5, ALU.mult, ALU.add))
                    link(ve.tensor_tensor(GW["i"], GW["i"], GW["g"], ALU.mult))
                    if b == 0:
                        for c in range(DC):
                            last = ve.scalar_tensor_tensor(out=GW["c1"][:, c, :], in0=GW["f"][:, c, :], scalar=w["c0"][:, c:c + 1],
                                                           in1=GW["i"][:, c, :], op0=ALU.mult, op1=ALU.add)
                            if c < DC - 1:
                                link(last)
                        last.then_inc(sem("F_c1_ready"), 1)
                    else:
                        link(ve.tensor_tensor(GW["c2"], GW["f"], GW["c1"], ALU.mult))
                        ve.tensor_tensor(GW["c2"], GW["c2"], GW["i"], ALU.add).then_inc(sem("F_c2_ready"), 1)
                dve.wait_ge(sem("y_ps"), nth(i, 1, 0) + done("F", "y_ps"))
                ve.tensor_tensor(GW["y"], ps[:, 7, :].rearrange("p (b d) -> p b d", b=B),
                                 rw["F"]["bo"].rearrange("p (o d) -> p o d", o=1).to_broadcast([P, B, D]),
                                 ALU.add).then_inc(sem("F_ysum_ready"), 1)
                dve.wait_ge(sem("F_h_ready"), nth(i, 1, 0))
                for b in range(B):
                    finish(i + b * HT, GW["y"][:, b, :], None, 6, None, sem("x_new"))

            normed(0)
            with dve.Fori(0, HT - 1) as i:
                chain_dve.begin(i, 3 + 3 + 2)
                pair(i, True)
            chain_dve.end(HT - 1)
            pair(HT - 1, False)

        FI_AT = B * D + DC * B * P

        NG = 2 * B
        RT = carve([("s", (NG, HT)), ("u", (NG, HT)), ("y", (NG, HT + 1)), ("e", (NG, HT + 1)), ("sc", (NG, HT)), ("n", (NG, HT)),
                    ("tie", (NG, HT)), ("sure", (NG, HT)), ("sel", (NG, HT)), ("pos", (NG, HT)), ("one", (NG, HT)),
                    ("c", (NG,)), ("m", (NG,)), ("pmax", (NG,)), ("a", (NG,)), ("t", (NG,)), ("part", (NG,)), ("ln", (NG,)), ("gm", (NG,)), ("k", (NG,)), ("gstar", (NG,)),
                    ("ssq", (NT, 1)), ("aux", (NT, 3)), ("unsel", (NT, 1)), ("rmsg", (DC,))], route)
        s_cols = RT["s"].rearrange("p g (t o) -> p (g t) o", o=1)
        pos_cols = RT["pos"].rearrange("p g (t o) -> p (g t) o", o=1)
        flat32 = lambda v: v.rearrange("p g t -> p (g t)")

        def over_t(v):
            return v.rearrange("p (g o) -> p g o", o=1).to_broadcast([P, NG, HT])

        SPAN = S + P
        LB = carve([("xnT", (DC, SPAN)), ("kT", (HC, SPAN)), ("v", (HT + 1, HDH))], big)
        LW = carve([("xn", (2, D)), ("q", (H8, P)), ("p", (2, 4, 2 * P)), ("pT", (2, 8 * P)), ("on", (2, D)), ("oT", (2, D)),
                    ("nm", (2, 4)), ("sum", (2, 4, 1)), ("rs", (2, 4)), ("junk", (2, 2, D))])
        HB = carve([("selq", (HT, NQ)), ("selk", (HT, NKV)), ("xqT", (DC, NQ)), ("xkT", (DC, NKV)), ("kT", (HC, NKV)),
                    ("v", (NKV // P, HDH))], big)
        RB = carve([("row", (NG, S))], big)
        HWK = carve([("qT", (HC, NQ)), ("selT", (2, S)), ("xg", (2, D)), ("p", (2, NKV)), ("pT", (2, NKV)), ("o", (HDH,)),
                     ("oT", (HC, P)), ("nm", (H8,)), ("m", (H8,)), ("sum", (H8, 1)), ("pn", (H8,)), ("rs", (H8,)), ("sn", (H8,)),
                     ("routed", (2, D)), ("aux", (6, 3)), ("t", (2, D)), ("pv", (HDH,)), ("scT", (P,))])

        def light_dve(dve):
            link, ve = chain_dve.link, nc.vector
            w, r = pk["D"], rw["D"]
            dve.wait_ge(sem("D_in"), LOADS["D"])
            with dve.Fori(0, NT // 2) as i:
                for j in range(2):
                    t = i * 2 + j
                    ve.tensor_scalar(hall[:, t, :], x[:, t, :], mean[:, t, :], rstd[:, t, :],
                                     ALU.subtract, ALU.mult).then_inc(sem("D_h_ready"), 1)
                for j in range(2):
                    t = i * 2 + j
                    dve.wait_ge(sem("D_h_ready"), nth(i, 2, j))
                    ve.bn_stats(stats[:, t, :], hall[:, t, :]).then_inc(sem("D_h_read"), 1)
            dve.wait_ge(sem("D_h_read"), NT)
            ssq = RT["ssq"][:, :, 0]
            m0, m1, v0, v1 = (stats[:, :, k] for k in (1, 4, 2, 5))
            sq0, sq1 = small[:, 256:256 + NT], small[:, 272:272 + NT]
            link(ve.tensor_tensor(sq0, m0, m0, ALU.mult))
            link(ve.tensor_tensor(sq1, m1, m1, ALU.mult))
            link(ve.tensor_tensor(sq0, sq0, sq1, ALU.add))
            link(ve.tensor_tensor(ssq, v0, v1, ALU.add))
            link(ve.scalar_tensor_tensor(out=ssq, in0=sq0, scalar=D / 2.0, in1=ssq, op0=ALU.mult, op1=ALU.add))
            link(ve.memset(LB["xnT"][:, :, 0:P // 2], 0.0))
            link(ve.memset(LB["xnT"][:, :, SPAN - P // 2:SPAN], 0.0))
            link(ve.memset(LW["q"], 0.0))
            dve.sem_inc(sem("D_zeros"), 1)
            norm_dve(dve, "Dh")
            with dve.Fori(0, B) as b:
                with dve.Fori(0, HT // 2) as i2:
                    for j in range(2):
                        n = b * HT + i2 * 2 + j
                        ve.tensor_scalar(LW["xn"][:, j, :], hall[:, n, :], mean[:, n, :], rstd[:, n, :],
                                         ALU.subtract, ALU.mult).then_inc(sem("xn_ready"), 1)
                    dve.wait_ge(sem("xT_ps"), b * HT + i2 * 2 + 2 + done("D", "xT_ps"))
                with dve.Fori(0, HT // 2) as i2:
                    dve.wait_ge(sem("D_h_read"), b * (2 * HT) + i2 * 4 + NT)
                    for j in range(2):
                        t = b * HT + i2 * 2 + j
                        for k, rt in enumerate(("rtq", "rtkv")):
                            ve.scalar_tensor_tensor(out=LW["junk"][:, j, k, :], in0=hall[:, t, :], scalar=1.0, in1=r[rt],
                                                    op0=ALU.mult, op1=ALU.mult,
                                                    accum_out=s_cols[:, t + k * NT, :]).then_inc(sem("D_h_read"), 1)
                for j in range(HT + 1):
                    dve.wait_ge(sem("D_v_ps"), nth(b, HT + 1, j))
                    ve.tensor_copy(LB["v"][:, j, :], ps[:, 1 + j % 6, :]).then_inc(sem("D_v_ready"), 1)
                def row_max(n, u):
                    dve.wait_ge(sem("s_ps"), nth(n, 2, u) + done("D", "s_ps"))
                    ve.tensor_reduce(LW["nm"][:, u, :], ps[:, 1 + 2 * u:3 + 2 * u, :].rearrange("p k (h s) -> p (k h) s", h=2),
                                     AX.X, ALU.max, negate=True).then_inc(sem("D_nm_ready"), 1)

                def take_pT(n, u):
                    dve.wait_ge(sem("pT_ps"), nth(n, 2, u) + done("D", "pT_ps"))
                    ve.tensor_copy(LW["pT"][:, u, :].rearrange("p (k n) -> p k n", k=2),
                                   ps[:, 5:7, :]).then_inc(sem("pT_ready"), 1)

                def normalise(n, u):
                    dve.wait_ge(sem("o_ps"), nth(n, 2, u) + done("D", "o_ps"))
                    ve.reciprocal(LW["rs"][:, u, :], LW["sum"][:, u, :, 0]).then_inc(sem("D_rs"), 1)
                    dve.wait_ge(sem("D_rs"), nth(n, 2, u))
                    ve.tensor_tensor(LW["on"][:, u, :].rearrange("p (h e) -> p h e", h=4),
                                     ps[:, 7, 0:D].rearrange("p (h e) -> p h e", h=4),
                                     LW["rs"][:, u, :].rearrange("p (h o) -> p h o", o=1).to_broadcast([P, 4, DH]),
                                     ALU.mult).then_inc(sem("on_ready"), 1)

                def update(n):
                    dve.wait_ge(sem("y_ps"), nth(n, 1, 0) + done("D", "y_ps"))
                    ve.scalar_tensor_tensor(out=x[:, n, :], in0=ps[:, 7, D:2 * D], scalar=gates[:, 5:6], in1=x[:, n, :],
                                            op0=ALU.mult, op1=ALU.add).then_inc(sem("D_x_light"), 1)

                def tile(n, more):
                    take_pT(n, 0)
                    normalise(n, 0)
                    take_pT(n, 1)
                    if more:
                        row_max(n + 1, 0)
                    normalise(n, 1)
                    if more:
                        row_max(n + 1, 1)
                    update(n)

                row_max(b * HT, 0)
                row_max(b * HT, 1)
                with dve.Fori(0, HT - 1) as i:
                    tile(b * HT + i, True)
                tile(b * HT + (HT - 1), False)

        def light_act(act):
            w = pk["D"]
            with act.Fori(0, B) as b:
                with act.Fori(0, HT // 2) as i2:
                    for j in range(2):
                        n = b * HT + i2 * 2 + j
                        if j == 0:
                            act.wait_ge(sem("D_zeros"), 1)
                        act.wait_ge(sem("xT_ps"), n + 1 + done("D", "xT_ps"))
                        for c in range(DC):
                            a = nc.scalar.activation(LB["xnT"][:, c, bass.ds(i2 * D + (j * P + P // 2), P)],
                                                     ps[:, j, c * P:(c + 1) * P], ACT.Identity,
                                                     scale=w["lng"][:, c:c + 1], bias=w["lnb"][:, c:c + 1])
                        a.then_inc(sem("xT_ready"), 1)
                for m in range(HC * 3):
                    act.wait_ge(sem("D_k_ps"), nth(b, HC * 3, m))
                    nc.scalar.copy(LB["kT"][:, m // 3, m % 3 * (SPAN // 3):(m % 3 + 1) * (SPAN // 3)],
                                   ps[:, 1 + m % 6, 0:SPAN // 3]).then_inc(sem("D_k_ready"), 1)
                def take_q(n):
                    act.wait_ge(sem("q_ps"), nth(n, 1, 0) + done("D", "q_ps"))
                    for hh in range(2):
                        half = slice(hh * DH, (hh + 1) * DH)
                        a = nc.scalar.activation(LW["q"][half].rearrange("p (c h) n -> p c h n", h=2)[:, :, hh, :],
                                                 ps[half, 0, :].rearrange("p (c n) -> p c n", c=HC), ACT.Copy,
                                                 scale=DH ** -0.5)
                    a.then_inc(sem("q_ready"), 1)

                def exps(n, u):
                    act.wait_ge(sem("D_nm_ready"), nth(n, 2, u))
                    for h in range(4):
                        a = nc.scalar.activation(LW["p"][:, u, h, :], ps[:, 1 + 2 * u + h // 2, h % 2 * D:(h % 2 + 1) * D],
                                                 ACT.Exp, bias=LW["nm"][:, u, h:h + 1], accum_out=LW["sum"][:, u, h, :])
                    a.then_inc(sem("p_ready"), 1)

                def take_oT(n, u):
                    act.wait_ge(sem("oT_ps"), nth(n, 2, u) + done("D", "oT_ps"))
                    nc.scalar.copy(LW["oT"][:, u, :], ps[:, 7, 0:D]).then_inc(sem("oT_ready"), 1)

                def tile(n, more):
                    if more:
                        take_q(n + 1)
                    take_oT(n, 0)
                    if more:
                        exps(n + 1, 0)
                    take_oT(n, 1)
                    if more:
                        exps(n + 1, 1)

                take_q(b * HT)
                exps(b * HT, 0)
                exps(b * HT, 1)
                with act.Fori(0, HT - 1) as i:
                    tile(b * HT + i, True)
                tile(b * HT + (HT - 1), False)

        def light_pe(pe):
            w = pk["D"]
            pe.wait_ge(sem("D_in"), LOADS["D"])
            pe.wait_ge(sem("D_zeros"), 1)
            with pe.Fori(0, B) as b:
                with pe.Fori(0, HT // 2) as i2:
                    for j in range(2):
                        n = b * HT + i2 * 2 + j
                        pe.wait_ge(sem("xn_ready"), n + 1 + done("D", "xn_ready"))
                        for c in range(DC):
                            mm = nc.tensor.transpose(ps[:, j, c * P:(c + 1) * P], LW["xn"][:, j, c * P:(c + 1) * P], ident)
                        mm.then_inc(sem("xT_ps"), 1)
                    pe.wait_ge(sem("xT_ready"), b * HT + i2 * 2 + 2 + done("D", "xT_ready"))
                for m in range(HC * 3):
                    if m >= 6:
                        pe.wait_ge(sem("D_k_ready"), nth(b, HC * 3, m - 6))
                    at = m % 3 * (SPAN // 3)
                    for ci in range(DC):
                        mm = nc.tensor.matmul(ps[:, 1 + m % 6, 0:SPAN // 3],
                                              w["wqkv"][:, ci * 3 * HDH + HDH + m // 3 * P:ci * 3 * HDH + HDH + (m // 3 + 1) * P],
                                              LB["xnT"][:, ci, at:at + SPAN // 3], start=ci == 0, stop=ci == DC - 1)
                    mm.then_inc(sem("D_k_ps"), 1)
                for j in range(HT + 1):
                    if j < 6:
                        pe.wait_ge(sem("D_k_ready"), nth(b, HC * 3, 6 + j))
                    else:
                        pe.wait_ge(sem("D_v_ready"), nth(b, HT + 1, j - 6))
                    for ci in range(DC):
                        mm = nc.tensor.matmul(ps[:, 1 + j % 6, :], LB["xnT"][:, ci, j * P:(j + 1) * P],
                                              w["wqkv"][:, ci * 3 * HDH + 2 * HDH:(ci + 1) * 3 * HDH], start=ci == 0, stop=ci == DC - 1)
                    mm.then_inc(sem("D_v_ps"), 1)

                def project_q(n, i):
                    for c in range(HC):
                        for ci in range(DC):
                            mm = nc.tensor.matmul(ps[:, 0, c * P:(c + 1) * P],
                                                  w["wqkv"][:, ci * 3 * HDH + c * P:ci * 3 * HDH + (c + 1) * P],
                                                  LB["xnT"][:, ci, bass.ds(i * P + P // 2, P)], start=ci == 0, stop=ci == DC - 1)
                    mm.then_inc(sem("q_ps"), 1)

                def scores(n, i, u):
                    if u == 0:
                        pe.wait_ge(sem("q_ready"), nth(n, 1, 0) + done("D", "q_ready"))
                    for k in range(2):
                        bank = ps[:, 1 + 2 * u + k, :]
                        for h in range(2):
                            nc.tensor.matmul(bank[:, h * D:(h + 1) * D], maskL[:, :], maskR[:, i, :],
                                             start=h == 0, stop=False, skip_group_check=True)
                        for h in range(2):
                            hd = 4 * u + 2 * k + h
                            mm = nc.tensor.matmul(bank[:, h * D:(h + 1) * D], LW["q"][:, hd, :],
                                                  LB["kT"][:, hd // 2, bass.ds(i * P, 2 * P)], start=False, stop=h == 1,
                                                  skip_group_check=True)
                    mm.then_inc(sem("s_ps"), 1)

                def turn_p(n, u):
                    pe.wait_ge(sem("p_ready"), nth(n, 2, u) + done("D", "p_ready"))
                    if u == 1:
                        pe.wait_ge(sem("pT_ready"), nth(n, 2, 0) + done("D", "pT_ready"))
                    for h in range(4):
                        for k in range(2):
                            m = 2 * h + k
                            mm = nc.tensor.transpose(ps[:, 5 + m // 4, m % 4 * P:(m % 4 + 1) * P],
                                                     LW["p"][:, u, h, k * P:(k + 1) * P], ident)
                    mm.then_inc(sem("pT_ps"), 1)

                def weigh_v(n, i, u):
                    pe.wait_ge(sem("pT_ready"), nth(n, 2, u) + done("D", "pT_ready"))
                    if u == 1:
                        pe.wait_ge(sem("oT_ready"), nth(n, 2, 0) + done("D", "oT_ready"))
                    for h in range(4):
                        hd = 4 * u + h
                        for k in range(2):
                            mm = nc.tensor.matmul(ps[:, 7, h * DH:(h + 1) * DH],
                                                  LW["pT"][:, u, (2 * h + k) * P:(2 * h + k + 1) * P],
                                                  LB["v"][:, i + k, hd * DH:(hd + 1) * DH], start=k == 0, stop=k == 1)
                    mm.then_inc(sem("o_ps"), 1)

                def turn_o(n, u):
                    pe.wait_ge(sem("on_ready"), nth(n, 2, u) + done("D", "on_ready"))
                    for c in range(2):
                        mm = nc.tensor.transpose(ps[:, 7, c * P:(c + 1) * P], LW["on"][:, u, c * P:(c + 1) * P], ident)
                    mm.then_inc(sem("oT_ps"), 1)

                def project(n):
                    pe.wait_ge(sem("oT_ready"), nth(n, 2, 1) + done("D", "oT_ready"))
                    for u in range(2):
                        for c in range(2):
                            mm = nc.tensor.matmul(ps[:, 7, D:2 * D], LW["oT"][:, u, c * P:(c + 1) * P],
                                                  w["wout"][:, (2 * u + c) * D:(2 * u + c + 1) * D],
                                                  start=u == 0 and c == 0, stop=u == 1 and c == 1)
                    mm.then_inc(sem("y_ps"), 1)

                def tile(n, i, more):
                    turn_p(n, 0)
                    if more:
                        project_q(n + 1, i + 1)
                    weigh_v(n, i, 0)
                    turn_p(n, 1)
                    if more:
                        scores(n + 1, i + 1, 0)
                    turn_o(n, 0)
                    weigh_v(n, i, 1)
                    if more:
                        scores(n + 1, i + 1, 1)
                    turn_o(n, 1)
                    project(n)
                    pe.wait_ge(sem("D_x_light"), nth(n, 1, 0))

                pe.wait_ge(sem("D_v_ready"), nth(b, HT + 1, HT))
                project_q(b * HT, 0)
                scores(b * HT, 0, 0)
                scores(b * HT, 0, 1)
                with pe.Fori(0, HT - 1) as i:
                    tile(b * HT + i, i, True)
                tile(b * HT + (HT - 1), HT - 1, False)

        ROUNDS, SPELL, CAP = 50, 7, 60.0
        SPELLS = (ROUNDS - 1) // SPELL

        def route_dve(dve):
            link, ve = chain_dve.link, nc.vector
            s, u, y, e = RT["s"], RT["u"], RT["y"], RT["e"]
            for r, k in enumerate((NQ, NKV)):
                logk = float(np.log(np.float32(min(k * FETCH, SEQ_CAP))))
                link(ve.memset(RT["k"][:, r * B:(r + 1) * B], float(k)))
                link(ve.memset(RT["a"][:, r * B:(r + 1) * B], float(np.log(np.float32(S)) - np.float32(logk))))
            dve.wait_ge(sem("D_h_read"), 3 * NT)
            ve.tensor_reduce(RT["pmax"], s, AX.X, ALU.max).then_inc(sem("D_pmax"), 1)
            dve.wait_ge(sem("D_smax"), 1)
            with dve.Fori(0, SPELLS) as i:
                chain_dve.begin(i, 3 + 1 + 2 * (SPELL - 1))
                link(ve.tensor_tensor(RT["c"], RT["m"], RT["a"], ALU.min))
                link(ve.tensor_tensor(y[:, :, 0:HT], s, over_t(RT["c"]), ALU.subtract))
                link(ve.tensor_tensor(y[:, :, HT], RT["a"], RT["c"], ALU.subtract))
                ve.tensor_scalar(y, y, CAP, None, ALU.min).then_inc(sem("D_y_shift"), 1)
                dve.wait_ge(sem("D_e"), nth(i, 1, 0))
                for k in range(SPELL):
                    if k == 0:
                        link(ve.tensor_tensor(u, e[:, :, 0:HT], over_t(e[:, :, HT]), ALU.min))
                    else:
                        for r in range(2):
                            g = slice(r * B, (r + 1) * B)
                            link(ve.scalar_tensor_tensor(
                                out=u[:, g], in0=ps[:, 0, g].rearrange("p (g o) -> p g o", o=1).to_broadcast([P, B, HT]),
                                scalar=1.0 / min((NQ, NKV)[r] * FETCH, SEQ_CAP), in1=e[:, g, 0:HT], op0=ALU.mult, op1=ALU.min))
                    ve.tensor_reduce(RT["part"], u, AX.X, ALU.add).then_inc(sem("D_part"), 1)
                    dve.wait_ge(sem("D_t_ps"), nth(i, SPELL, k))
                for r in range(2):
                    g = slice(r * B, (r + 1) * B)
                    ve.tensor_scalar(RT["t"][:, g], ps[:, 0, g], 1.0 / min((NQ, NKV)[r] * FETCH, SEQ_CAP), None,
                                     ALU.mult).then_inc(sem("D_t"), 1)
                dve.wait_ge(sem("D_ln"), nth(i, 1, 0))
                ve.tensor_tensor(RT["a"], RT["c"], RT["ln"], ALU.add).then_inc(sem("D_c"), 1)
                dve.wait_ge(sem("D_c"), nth(i, 1, 0))
            chain_dve.end(SPELLS)
            link(ve.tensor_tensor(u, s, over_t(RT["a"]), ALU.subtract))
            ve.tensor_scalar(y[:, :, 0:HT], u, 0.0, None, ALU.min).then_inc(sem("D_fin"), 1)
            dve.wait_ge(sem("D_sc"), 1)
            dve.wait_ge(sem("D_scT_ps"), 1)
            ve.tensor_copy(HWK["scT"][0:NG * HT, :], ps[0:NG * HT, 0, 0:P]).then_inc(sem("D_scT"), 1)
            dve.wait_ge(sem("D_row"), 16)
            for g in range(NG):
                for t in range(HT):
                    k = g * HT + t
                    chain_dve.follow(ve.tensor_scalar(HWK["selT"][:, k % 2, :], RB["row"][:, g, :], RT["sc"][:, g, t:t + 1], 0.0,
                                     ALU.is_gt, ALU.add, accum_out=RT["n"][:, g, t:t + 1]))
            chain_dve.settle()
            k_t = over_t(RT["k"])
            link(ve.tensor_tensor(RT["tie"], RT["n"], k_t, ALU.is_lt))
            link(ve.tensor_tensor(RT["tie"], RT["tie"], RT["n"], ALU.mult))
            ve.tensor_reduce(RT["gm"], RT["tie"], AX.X, ALU.max).then_inc(sem("D_gm"), 1)
            dve.wait_ge(sem("D_gstar"), 1)
            link(ve.tensor_tensor(RT["sure"], RT["n"], over_t(RT["gstar"]), ALU.is_lt))
            ve.tensor_tensor(RT["tie"], RT["n"], over_t(RT["gstar"]), ALU.is_equal).then_inc(sem("D_tie"), 1)
            dve.wait_ge(sem("D_prefix"), 1)
            pre = ps[:, 1, 0:NG * HT].rearrange("p (g t) -> p g t", g=NG)
            link(ve.tensor_tensor(RT["u"], pre, over_t(RT["gstar"]), ALU.add))
            link(ve.tensor_tensor(RT["u"], RT["u"], k_t, ALU.is_lt))
            link(ve.tensor_tensor(RT["u"], RT["u"], RT["tie"], ALU.mult))
            ve.tensor_tensor(RT["sel"], RT["u"], RT["sure"], ALU.add).then_inc(sem("D_sel"), 1)
            dve.wait_ge(sem("D_prefix"), 2)
            link(ve.scalar_tensor_tensor(out=flat32(RT["pos"]), in0=ps[:, 2, 0:NG * HT], scalar=1.0, in1=flat32(RT["sel"]),
                                         op0=ALU.add, op1=ALU.mult))
            link(ve.tensor_scalar(RT["pos"], RT["pos"], -1.0, None, ALU.add))
            link(ve.tensor_scalar(RT["one"], RT["sc"], -1.0, 1.0, ALU.mult, ALU.add))
            link(ve.tensor_tensor(RT["one"], RT["one"], RT["sc"], ALU.add))
            aux = RT["aux"]
            dve.wait_ge(sem("D_norm"), 1)
            link(ve.tensor_scalar(RT["ssq"], RT["ssq"], 1e-12, None, ALU.max))
            link(ve.reciprocal(RT["ssq"], RT["ssq"]))
            link(ve.tensor_scalar(aux[:, :, 0], RT["ssq"][:, :, 0], float(D) ** 0.5, None, ALU.mult))
            link(ve.tensor_copy(aux[:, :, 1], flat32(RT["one"])[:, NT:2 * NT]))
            link(ve.tensor_copy(aux[:, :, 2], flat32(RT["one"])[:, 0:NT]))
            link(ve.tensor_scalar(RT["unsel"][:, :, 0], flat32(RT["sel"])[:, 0:NT], -1.0, 1.0, ALU.mult, ALU.add))

        def route_act(act):
            with act.Fori(0, SPELLS) as i:
                act.wait_ge(sem("D_y_shift"), nth(i, 1, 0))
                nc.scalar.activation(RT["e"], RT["y"], ACT.Exp).then_inc(sem("D_e"), 1)
                act.wait_ge(sem("D_t"), nth(i, 2, 1))
                nc.scalar.activation(RT["ln"], RT["t"], ACT.Ln).then_inc(sem("D_ln"), 1)
            act.wait_ge(sem("D_fin"), 1)
            nc.scalar.activation(RT["sc"], RT["y"][:, :, 0:HT], ACT.Exp).then_inc(sem("D_sc"), 1)
            nc.scalar.activation(RT["ssq"], RT["ssq"], ACT.Sqrt).then_inc(sem("D_norm"), 1)

        def route_pool(pool):
            mx = bass.bass_isa.ReduceOp.max
            pool.wait_ge(sem("D_pmax"), 1)
            nc.gpsimd.partition_all_reduce(RT["m"], RT["pmax"], P, mx).then_inc(sem("D_smax"), 1)
            pool.wait_ge(sem("D_gm"), 1)
            nc.gpsimd.partition_all_reduce(RT["gstar"], RT["gm"], P, mx).then_inc(sem("D_gstar"), 1)

        def route_pe(pe):
            with pe.Fori(0, SPELLS) as i:
                for k in range(SPELL):
                    pe.wait_ge(sem("D_part"), nth(i, SPELL, k))
                    nc.tensor.matmul(ps[:, 0, 0:NG], ones, RT["part"], start=True, stop=True).then_inc(sem("D_t_ps"), 1)
            pe.wait_ge(sem("D_sc"), 1)
            nc.tensor.transpose(ps[0:NG * HT, 0, 0:P], flat32(RT["sc"]), ident).then_inc(sem("D_scT_ps"), 1)

            def prefix(v, bank):
                out_ = ps[:, bank, 0:NG * HT].rearrange("p (g t) -> p g t", g=NG)
                nc.tensor.matmul(out_, pk["const"]["before"], v, start=True, stop=False, skip_group_check=True)
                for d in range(1, HT):
                    mm = nc.tensor.matmul(out_[:, :, d:HT], ones, v[:, :, 0:HT - d], start=False, stop=d == HT - 1,
                                          skip_group_check=True)
                mm.then_inc(sem("D_prefix"), 1)

            pe.wait_ge(sem("D_tie"), 1)
            prefix(RT["tie"], 1)
            pe.wait_ge(sem("D_sel"), 1)
            prefix(RT["sel"], 2)

        def route_sp(sp):
            sp.wait_ge(sem("D_scT"), 1)
            sp.dma_start(score_rows, HWK["scT"][0:NG * HT, :]).then_inc(sem("D_score_rows"), 16)
            sp.wait_ge(sem("D_score_rows"), 16)
            sp.dma_start(RB["row"].rearrange("p g n -> p (g n)"),
                         score_rows.rearrange("r n -> (r n)").partition_broadcast(P)).then_inc(sem("D_row"), 16)

        QC, KC = NQ // P, NKV // P

        def heavy_dve(dve):
            link, ve = chain_dve.link, nc.vector
            w, r = pk["D"], rw["D"]
            link(ve.tensor_copy(RT["rmsg"], w["rmsg"]))
            slots = pk["const"]["slots"]
            with dve.Fori(0, B) as b:
                chain_dve.begin(b, HEAVY_LINKS)
                for t in range(HT):
                    ve.tensor_scalar(HB["selq"][:, t, :], slots[:, 0:NQ], pos_cols[:, b * HT + t, :], None,
                                     ALU.is_equal).then_inc(sem("D_onehot"), 1)
                for t in range(HT):
                    ve.tensor_scalar(HB["selk"][:, t, :], slots, pos_cols[:, b * HT + t + NT, :], None,
                                     ALU.is_equal).then_inc(sem("D_onehot"), 1)
                for m in range(QC + KC):
                    dve.wait_ge(sem("D_gather_ps"), nth(b, QC + KC, m))
                    link(ve.tensor_copy(HWK["aux"][:, m, :], ps[:, m, D:D + 3]))
                    if m >= 2:
                        dve.wait_ge(sem("D_gT_ps"), nth(b, QC + KC, m - 2))
                    ve.tensor_scalar(HWK["xg"][:, m % 2, :], ps[:, m, 0:D], HWK["aux"][:, m, 0:1], None,
                                     ALU.mult).then_inc(sem("D_xg"), 1)
                for c in range(HC):
                    dve.wait_ge(sem("D_kh_ps"), nth(b, HC, c))
                    ve.tensor_copy(HB["kT"][:, c, :], ps[:, c % 4, :]).then_inc(sem("D_kh"), 1)
                for k in range(KC):
                    dve.wait_ge(sem("D_vh_ps"), nth(b, KC, k))
                    ve.tensor_scalar(HB["v"][:, k, :], ps[:, k, :], HWK["aux"][:, QC + k, 1:2], None,
                                     ALU.mult).then_inc(sem("D_vh"), 1)
                for qc in range(QC):
                    n = b * QC + qc
                    dve.wait_ge(sem("D_sn_ps"), nth(n, 1, 0))
                    link(ve.tensor_copy(HWK["sn"], ps[:, 7, 0:H8]))

                    def shift(h):
                        dve.wait_ge(sem("D_sh_ps"), nth(n, H8, h))
                        link(ve.tensor_reduce(HWK["m"][:, h:h + 1], ps[:, h % 2, :], AX.X, ALU.max))
                        link(ve.tensor_tensor(HWK["m"][:, h:h + 1], HWK["m"][:, h:h + 1], HWK["sn"][:, h:h + 1], ALU.max))
                        ve.tensor_scalar(HWK["nm"][:, h:h + 1], HWK["m"][:, h:h + 1], -1.0, None, ALU.mult
                                         ).then_inc(sem("D_nmh"), 1)

                    def take_pT(h):
                        dve.wait_ge(sem("D_phT_ps"), nth(n, H8, h))
                        if h >= 2:
                            dve.wait_ge(sem("D_oh_ps"), nth(n, H8, h - 2))
                        ve.tensor_copy(HWK["pT"][:, h % 2, :], ps[:, 2 + h % 2, :]).then_inc(sem("D_phT"), 1)

                    shift(0)
                    for h in range(H8):
                        if h + 1 < H8:
                            shift(h + 1)
                        if h == H8 - 1:
                            link(ve.tensor_tensor(HWK["sn"], HWK["sn"], HWK["m"], ALU.subtract))
                            dve.sem_inc(sem("D_sn_sub"), 1)
                        take_pT(h)
                    dve.wait_ge(sem("D_oh_ps"), nth(n, H8, H8 - 1))
                    dve.wait_ge(sem("D_pn"), nth(n, 1, 0))
                    head = lambda v: v.rearrange("p (h e) -> p h e", h=H8)
                    wide = lambda v: v.rearrange("p (h o) -> p h o", o=1).to_broadcast([P, H8, DH])
                    link(ve.tensor_tensor(head(HWK["pv"]), head(r["nv"]), wide(HWK["pn"]), ALU.mult))
                    link(ve.tensor_tensor(HWK["pv"], HWK["pv"], ps[:, 4, :], ALU.add))
                    link(ve.tensor_tensor(HWK["rs"], HWK["sum"][:, :, 0], HWK["pn"], ALU.add))
                    link(ve.reciprocal(HWK["rs"], HWK["rs"]))
                    ve.tensor_tensor(head(HWK["o"]), head(HWK["pv"]), wide(HWK["rs"]), ALU.mult).then_inc(sem("D_oh"), 1)
                    dve.wait_ge(sem("D_yh_ps"), nth(n, 1, 0))
                    ve.tensor_copy(HWK["routed"][:, qc, :], ps[:, 6, 0:D]).then_inc(sem("D_routed"), 1)
                for t in range(HT):
                    n = b * HT + t
                    tmp = HWK["t"][:, t % 2, :]
                    link(ve.tensor_scalar(tmp, r["nullq"], RT["unsel"][:, n, :], None, ALU.mult))
                    dve.wait_ge(sem("D_scat_ps"), nth(b, HT, t))
                    link(ve.scalar_tensor_tensor(out=tmp, in0=ps[:, t % 2, 0:D], scalar=RT["aux"][:, n, 2:3], in1=tmp,
                                                 op0=ALU.mult, op1=ALU.add))
                    finish(n, tmp, None, 5, None, sem("x_new"))
            chain_dve.end(B)

        HEAVY_LINKS = (QC + KC) + QC * (1 + 2 * H8 + 1 + 4) + HT * 3

        def heavy_act(act):
            with act.Fori(0, B) as b:
                for m in range(QC + KC):
                    act.wait_ge(sem("D_gT_ps"), nth(b, QC + KC, m))
                    dst, at = (HB["xqT"], m) if m < QC else (HB["xkT"], m - QC)
                    for c in range(DC):
                        a = nc.scalar.activation(dst[:, c, at * P:(at + 1) * P], ps[:, 6 + m % 2, c * P:(c + 1) * P], ACT.Copy,
                                                 scale=RT["rmsg"][:, c:c + 1])
                    a.then_inc(sem("D_gT"), 1)
                for c in range(HC):
                    act.wait_ge(sem("D_qh_ps"), nth(b, HC, c))
                    nc.scalar.activation(HWK["qT"][:, c, :], ps[:, 4 + c % 4, 0:NQ], ACT.Copy, scale=DH ** -0.5
                                         ).then_inc(sem("D_qh"), 1)
                for m in range(4):
                    act.wait_ge(sem("D_selT_ps"), nth(b, 4, m))
                    nc.scalar.copy(HWK["selT"][:, m // 2, m % 2 * 512:(m % 2 + 1) * 512], ps[:, 4 + m, :]
                                   ).then_inc(sem("D_selT"), 1)
                for qc in range(QC):
                    n = b * QC + qc
                    for h in range(H8):
                        act.wait_ge(sem("D_nmh"), nth(n, H8, h))
                        if h >= 2:
                            act.wait_ge(sem("D_phT_ps"), nth(n, H8, h - 2))
                        nc.scalar.activation(HWK["p"][:, h % 2, :], ps[:, h % 2, :], ACT.Exp, bias=HWK["nm"][:, h:h + 1],
                                             accum_out=HWK["sum"][:, h, :]).then_inc(sem("D_ph"), 1)
                    act.wait_ge(sem("D_sn_sub"), nth(n, 1, 0))
                    nc.scalar.activation(HWK["pn"], HWK["sn"], ACT.Exp).then_inc(sem("D_pn"), 1)
                    act.wait_ge(sem("D_ohT_ps"), nth(n, 1, 0))
                    nc.scalar.copy(HWK["oT"], ps[:, 5, :].rearrange("p (c n) -> p c n", c=HC)).then_inc(sem("D_ohT"), 1)

        def heavy_pe(pe):
            w = pk["D"]
            with pe.Fori(0, B) as b:
                for m in range(QC + KC):
                    if m == 0:
                        pe.wait_ge(sem("D_onehot"), nth(b, 2 * HT, HT - 1))
                    if m == QC:
                        pe.wait_ge(sem("D_onehot"), nth(b, 2 * HT, 2 * HT - 1))
                    sel = HB["selq"][:, :, m * P:(m + 1) * P] if m < QC else HB["selk"][:, :, (m - QC) * P:(m - QC + 1) * P]
                    for t in range(HT):
                        nc.tensor.matmul(ps[:, m, 0:D], sel[:, t, :], hall[:, b * HT + t, :], start=t == 0,
                                         stop=t == HT - 1, skip_group_check=True)
                    for t in range(HT):
                        mm = nc.tensor.matmul(ps[:, m, D:D + 3], sel[:, t, :], RT["aux"][:, b * HT + t, :], start=t == 0,
                                              stop=t == HT - 1, skip_group_check=True)
                    mm.then_inc(sem("D_gather_ps"), 1)
                for m in range(QC + KC):
                    pe.wait_ge(sem("D_xg"), nth(b, QC + KC, m))
                    if m >= 2:
                        pe.wait_ge(sem("D_gT"), nth(b, QC + KC, m - 2))
                    for c in range(DC):
                        mm = nc.tensor.transpose(ps[:, 6 + m % 2, c * P:(c + 1) * P], HWK["xg"][:, m % 2, c * P:(c + 1) * P], ident)
                    mm.then_inc(sem("D_gT_ps"), 1)
                pe.wait_ge(sem("D_gT"), nth(b, QC + KC, QC + KC - 1))
                for c in range(HC):
                    for ci in range(DC):
                        mm = nc.tensor.matmul(ps[:, c, :], w["wkh"][:, ci * HDH + c * P:ci * HDH + (c + 1) * P],
                                              HB["xkT"][:, ci, :], start=ci == 0, stop=ci == DC - 1)
                    mm.then_inc(sem("D_kh_ps"), 1)
                for c in range(HC):
                    for ci in range(DC):
                        mm = nc.tensor.matmul(ps[:, 4 + c, 0:NQ], w["wqh"][:, ci * HDH + c * P:ci * HDH + (c + 1) * P],
                                              HB["xqT"][:, ci, :], start=ci == 0, stop=ci == DC - 1)
                    mm.then_inc(sem("D_qh_ps"), 1)
                for k in range(KC):
                    pe.wait_ge(sem("D_kh"), nth(b, HC, k))
                    for ci in range(DC):
                        mm = nc.tensor.matmul(ps[:, k, :], HB["xkT"][:, ci, k * P:(k + 1) * P],
                                              w["wvh"][:, ci * HDH:(ci + 1) * HDH], start=ci == 0, stop=ci == DC - 1)
                    mm.then_inc(sem("D_vh_ps"), 1)
                for m in range(4):
                    pe.wait_ge(sem("D_qh"), nth(b, HC, m))
                    for t in range(4):
                        mm = nc.tensor.transpose(ps[:, 4 + m, t * P:(t + 1) * P],
                                                 HB["selq"][:, m % 2 * 4 + t, m // 2 * P:(m // 2 + 1) * P], ident)
                    mm.then_inc(sem("D_selT_ps"), 1)
                pe.wait_ge(sem("D_selT"), nth(b, 4, 3))
                pe.wait_ge(sem("D_vh"), nth(b, KC, KC - 1))
                for qc in range(QC):
                    n = b * QC + qc
                    for c in range(HC):
                        mm = nc.tensor.matmul(ps[:, 7, 0:H8], HWK["qT"][:, c, qc * P:(qc + 1) * P],
                                              w["nk"][:, c * H8:(c + 1) * H8], start=c == 0, stop=c == HC - 1)
                    mm.then_inc(sem("D_sn_ps"), 1)

                    def scores(h):
                        hp = slice(h % 2 * DH, (h % 2 + 1) * DH)
                        if h >= 2:
                            pe.wait_ge(sem("D_ph"), nth(n, H8, h - 2))
                        nc.tensor.matmul(ps[:, h % 2, :], HWK["qT"][hp, h // 2, qc * P:(qc + 1) * P], HB["kT"][hp, h // 2, :],
                                         start=True, stop=True).then_inc(sem("D_sh_ps"), 1)

                    def turn_p(h):
                        pe.wait_ge(sem("D_ph"), nth(n, H8, h))
                        if h >= 2:
                            pe.wait_ge(sem("D_phT"), nth(n, H8, h - 2))
                        for k in range(KC):
                            mm = nc.tensor.transpose(ps[:, 2 + h % 2, k * P:(k + 1) * P], HWK["p"][:, h % 2, k * P:(k + 1) * P], ident)
                        mm.then_inc(sem("D_phT_ps"), 1)

                    def weigh_v(h):
                        pe.wait_ge(sem("D_phT"), nth(n, H8, h))
                        for k in range(KC):
                            mm = nc.tensor.matmul(ps[:, 4, h * DH:(h + 1) * DH], HWK["pT"][:, h % 2, k * P:(k + 1) * P],
                                                  HB["v"][:, k, h * DH:(h + 1) * DH], start=k == 0, stop=k == KC - 1)
                        mm.then_inc(sem("D_oh_ps"), 1)

                    scores(0)
                    scores(1)
                    for h in range(H8):
                        turn_p(h)
                        if h + 2 < H8:
                            scores(h + 2)
                        if h >= 1:
                            weigh_v(h - 1)
                    weigh_v(H8 - 1)
                    pe.wait_ge(sem("D_oh"), nth(n, 1, 0))
                    for c in range(HC):
                        mm = nc.tensor.transpose(ps[:, 5, c * P:(c + 1) * P], HWK["o"][:, c * P:(c + 1) * P], ident)
                    mm.then_inc(sem("D_ohT_ps"), 1)
                    pe.wait_ge(sem("D_ohT"), nth(n, 1, 0))
                    for c in range(HC):
                        mm = nc.tensor.matmul(ps[:, 6, 0:D], HWK["oT"][:, c, :], w["wouth"][:, c * D:(c + 1) * D],
                                              start=c == 0, stop=c == HC - 1)
                    mm.then_inc(sem("D_yh_ps"), 1)
                pe.wait_ge(sem("D_routed"), nth(b, QC, QC - 1))
                for t in range(HT):
                    if t >= 2:
                        pe.wait_ge(sem("x_new"), nth(b, HT, t - 2) + done("D", "x_new"))
                    for j in range(QC):
                        mm = nc.tensor.matmul(ps[:, t % 2, 0:D], HWK["selT"][:, j, t * P:(t + 1) * P], HWK["routed"][:, j, :],
                                              start=j == 0, stop=j == QC - 1)
                    mm.then_inc(sem("D_scat_ps"), 1)

        MW = carve([("xn", (B, D)), ("xnT", (DC, B * P)), ("pr", (NT, NE)), ("gt", (NT, NE)), ("eq", (NT, NE)), ("cum", (NT, NE)),
                    ("top", (NT, 8)), ("c16", (4, NT)), ("scT", (NT * P // 2,)), ("gt3", (NT * 3 * NE // 2,)), ("idb", (P // 2,)), ("sg", (2, 512)), ("act", (2, 512)), ("accT", (DC, 512)),
                    ("start", (NT * NE,))])
        MB = carve([("w1", (NE, DC, INTER)), ("w3", (NE, DC, INTER)), ("w2", (NE, D))], big)
        gt3 = MW["gt3"].bitcast(BF16).rearrange("p (t k e) -> p t k e", t=NT, k=3)
        scT = MW["scT"].bitcast(BF16)[0:3 * NE, :]
        identb = MW["idb"].bitcast(BF16)
        xnT_all = hflat.rearrange("p (c b n) -> p c b n", c=DC, b=B)
        xnT_tok = hflat.rearrange("p (c n) -> p c n", c=DC)
        BLK = 512
        NBLK = B * S // BLK

        def moe_pe(pe):
            w = pk["H"]
            pe.wait_ge(sem("H_in"), LOADS["H"])
            with pe.Fori(0, HT) as i:
                for b in range(B):
                    pe.wait_ge(sem("xn_ready"), nth(i, B, b) + done("H", "xn_ready"))
                    for c in range(DC):
                        mm = nc.tensor.transpose(ps[:, 0, c * D + b * P:c * D + (b + 1) * P],
                                                 MW["xn"][:, b, c * P:(c + 1) * P], ident)
                mm.then_inc(sem("xT_ps"), 1)
                pe.wait_ge(sem("xT_ready"), nth(i, 1, 0) + done("H", "xT_ready"))
                for b in range(B):
                    for c in range(DC):
                        mm = nc.tensor.matmul(ps[:, 1, b * NE:(b + 1) * NE], MW["xnT"][:, c, b * P:(b + 1) * P],
                                              w["gate"][:, c * NE:(c + 1) * NE], start=c == 0, stop=c == DC - 1)
                mm.then_inc(sem("H_logit_ps"), 1)
            pe.wait_ge(sem("H_score"), 1)
            for t in range(NT):
                mm = nc.tensor.transpose(ps[0:3 * NE, 2 + t // 8, :].bitcast(BF16)[:, t % 8 * P:(t % 8 + 1) * P],
                                         gt3[:, t].rearrange("p k e -> p (k e)"), identb)
            mm.then_inc(sem("H_scT_ps"), 1)
            pe.wait_ge(sem("H_scT"), 2)
            with pe.Fori(0, NBLK) as i:
                def hidden(e):
                    if e >= 2:
                        pe.wait_ge(sem("H_act"), nth(i, NE, e - 2))
                    for bank, name in ((0, "w1"), (2, "w3")):
                        for c in range(DC):
                            mm = nc.tensor.matmul(ps[:, bank + e % 2, :], MB[name][:, e, c, :],
                                                  xnT_tok[:, c, bass.ds(i * BLK, BLK)], start=c == 0, stop=c == DC - 1)
                    mm = nc.tensor.matmul(ps[:, 4 + e % 2, :], esel[:, e, :], scT[:, bass.ds(i * BLK, BLK)],
                                          start=True, stop=True)
                    mm.then_inc(sem("H_gu_ps"), 1)

                def down(e):
                    pe.wait_ge(sem("H_act"), nth(i, NE, e))
                    for c in range(DC):
                        mm = nc.tensor.matmul(ps[:, 6 + c, :], MB["w2"][:, e, c * P:(c + 1) * P], MW["act"][:, e % 2, :],
                                              start=e == 0, stop=e == NE - 1)
                    mm.then_inc(sem("H_down"), 1)

                hidden(0)
                for e in range(NE):
                    if e + 1 < NE:
                        hidden(e + 1)
                    down(e)
                pe.wait_ge(sem("H_accT"), nth(i, DC, DC - 1))
                for t in range(4):
                    for c in range(DC):
                        mm = nc.tensor.transpose(ps[:, t, c * P:(c + 1) * P], MW["accT"][:, c, t * P:(t + 1) * P], ident)
                    mm.then_inc(sem("y_ps"), 1)
                pe.wait_ge(sem("x_new"), nth(i, 4, 3) + done("H", "x_new"))

        def moe_act(act):
            with act.Fori(0, HT) as i:
                act.wait_ge(sem("xT_ps"), nth(i, 1, 0) + done("H", "xT_ps"))
                nc.scalar.copy(xnT_all[:, :, :, bass.ds(i * P, P)],
                               ps[:, 0, :].rearrange("p (c b n) -> p c b n", c=DC, b=B)).then_inc(sem("H_xT_all"), 1)
                nc.scalar.copy(MW["xnT"], ps[:, 0, :].rearrange("p (c n) -> p c n", c=DC)).then_inc(sem("xT_ready"), 1)
            act.wait_ge(sem("H_lsub"), 1)
            nc.scalar.activation(MW["pr"], MW["pr"], ACT.Exp).then_inc(sem("H_exp"), 1)
            with act.Fori(0, NBLK) as i:
                for e in range(NE):
                    act.wait_ge(sem("H_gu_ps"), nth(i, NE, e))
                    nc.scalar.activation(MW["sg"][:, e % 2, :], ps[:, e % 2, :], ACT.Silu).then_inc(sem("H_silu"), 1)
                act.wait_ge(sem("H_down"), nth(i, NE, NE - 1))
                for c in range(DC):
                    nc.scalar.copy(MW["accT"][:, c, :], ps[:, 6 + c, :]).then_inc(sem("H_accT"), 1)

        def moe_dve(dve):
            link, ve = chain_dve.link, nc.vector
            with dve.Fori(0, HT) as i:
                for b in range(B):
                    t = i + b * HT
                    ve.tensor_scalar(MW["xn"][:, b, :], x[:, t, :], mean[:, t, :], rstd[:, t, :],
                                     ALU.subtract, ALU.mult).then_inc(sem("xn_ready"), 1)
                dve.wait_ge(sem("H_logit_ps"), nth(i, 1, 0))
                for b in range(B):
                    t = i + b * HT
                    ve.tensor_copy(MW["pr"][:, t, :], ps[:, 1, b * NE:(b + 1) * NE]).then_inc(sem("H_logit"), 1)
            dve.wait_ge(sem("H_logit"), NT)
            pr, gt, eq, cum, c16 = MW["pr"], MW["gt"], MW["eq"], MW["cum"], MW["c16"]
            per_t = lambda v: v.rearrange("p (t o) -> p t o", o=1).to_broadcast([P, NT, NE])
            link(ve.tensor_reduce(c16[:, 0, :], pr, AX.X, ALU.max))
            ve.tensor_tensor(pr, pr, per_t(c16[:, 0, :]), ALU.subtract).then_inc(sem("H_lsub"), 1)
            dve.wait_ge(sem("H_exp"), 1)
            link(ve.tensor_reduce(c16[:, 0, :], pr, AX.X, ALU.add))
            link(ve.reciprocal(c16[:, 0, :], c16[:, 0, :]))
            link(ve.tensor_tensor(pr, pr, per_t(c16[:, 0, :]), ALU.mult))
            for t in range(NT):
                link(ve.max(MW["top"][:, t, :], pr[:, t, :]))
            link(ve.tensor_copy(c16[:, 1, :], MW["top"][:, :, TOP - 1]))
            link(ve.tensor_tensor(gt, pr, per_t(c16[:, 1, :]), ALU.is_gt))
            link(ve.tensor_tensor(eq, pr, per_t(c16[:, 1, :]), ALU.is_equal))
            link(ve.tensor_reduce(c16[:, 2, :], gt, AX.X, ALU.add))
            link(ve.memset(MW["start"], 1.0))
            link(ve.memset(MW["start"].rearrange("p (t e) -> p t e", t=NT)[:, :, 0:1], 0.0))
            link(ve.tensor_tensor_scan(cum.rearrange("p t e -> p (t e)"), MW["start"], eq.rearrange("p t e -> p (t e)"), 0.0,
                                       ALU.mult, ALU.add))
            link(ve.tensor_tensor(cum, cum, per_t(c16[:, 2, :]), ALU.add))
            link(ve.tensor_scalar(cum, cum, float(TOP), None, ALU.is_le))
            link(ve.tensor_tensor(eq, eq, cum, ALU.mult))
            link(ve.tensor_tensor(gt, gt, eq, ALU.add))
            link(ve.tensor_reduce(c16[:, 3, :], MW["top"][:, :, 0:TOP], AX.X, ALU.add))
            link(ve.reciprocal(c16[:, 3, :], c16[:, 3, :]))
            link(ve.tensor_tensor(gt, gt, pr, ALU.mult))
            link(ve.tensor_tensor(gt, gt, per_t(c16[:, 3, :]), ALU.mult))
            link(ve.tensor_copy(identb, ident))
            for k in range(3):
                part = ve.tensor_copy(gt3[:, :, k, :], gt)
                if k < 2:
                    link(part)
                    link(ve.tensor_tensor(gt, gt, gt3[:, :, k, :], ALU.subtract))
            part.then_inc(sem("H_score"), 1)
            dve.wait_ge(sem("H_scT_ps"), 1)
            for k in range(2):
                ve.tensor_copy(scT[:, k * NT * P // 2:(k + 1) * NT * P // 2], ps[0:3 * NE, 2 + k, :].bitcast(BF16)
                               ).then_inc(sem("H_scT"), 1)
            with dve.Fori(0, NBLK) as i:
                chain_dve.begin(i, NE)
                for e in range(NE):
                    dve.wait_ge(sem("H_silu"), nth(i, NE, e))
                    if e >= 2:
                        dve.wait_ge(sem("H_down"), nth(i, NE, e - 2))
                    a = MW["act"][:, e % 2, :]
                    link(ve.tensor_tensor(a, MW["sg"][:, e % 2, :], ps[:, 2 + e % 2, :], ALU.mult))
                    ve.tensor_tensor(a, a, ps[:, 4 + e % 2, :], ALU.mult).then_inc(sem("H_act"), 1)
                for t in range(4):
                    dve.wait_ge(sem("y_ps"), nth(i, 4, t) + done("H", "y_ps"))
                    n = i * 4 + t
                    ve.scalar_tensor_tensor(out=x[:, n, :], in0=ps[:, t, 0:D], scalar=gates[:, 7:8], in1=x[:, n, :],
                                            op0=ALU.mult, op1=ALU.add).then_inc(sem("x_new"), 1)
            chain_dve.end(NBLK)

        def moe_sp(sp):
            out_v = out.rearrange("b (t p) d -> p (b t) d", p=P)
            with sp.Fori(0, NBLK) as i:
                sp.wait_ge(sem("x_new"), nth(i, 4, 3) + done("H", "x_new"))
                sp.dma_start(out_v[:, bass.ds(i * 4, 4), :], x[:, bass.ds(i * 4, 4), :]).then_inc(sem("out_done"), 16)
            sp.wait_ge(sem("out_done"), 16 * NBLK)

        chain_dve = None

        @block.sync
        def _(sp):
            x_tiles = "b (t p) d -> p (b t) d"
            sp.dma_start(x[:, :, :], ins["x"].rearrange(x_tiles, p=P)).then_inc(sem("x_in"), 16)
            sp.dma_start(packs["const"][:, :], ins["const"]).then_inc(sem("const_in"), 16)
            sp.dma_start(gates[:, :], ins["gates"].partition_broadcast(P)).then_inc(sem("const_in"), 16)
            sp.dma_start(ctxT[:, :, :], ins["ctxT"]).then_inc(sem("const_in"), 16)
            sp.dma_start(ctxN[:, :, :], ins["ctx"].rearrange("b s d -> s b d")).then_inc(sem("const_in"), 16)
            sp.dma_start(mask8[:, :], ins["maskT"]).then_inc(sem("const_in"), 16)
            sp.dma_start(maskrow8[:, :, :], ins["mask"].rearrange("(o b) s -> o b s", o=1)).then_inc(sem("const_in"), 16)
            def load(name):
                key = "B" if name == "lora" else name
                sp.dma_start(packs[name][:, :], ins["pack_" + name]).then_inc(sem(f"{key}_in"), 16)
                if name in ROWS:
                    sp.dma_start(rows[name][:, :], ins["rows_" + name].partition_broadcast(P)).then_inc(sem(f"{key}_in"), 16)

            for name in ("A", "B", "lora", "C", "D", "E", "F"):
                load(name)
            sp.dma_start(maskR[:, :, :], ins["maskR"]).then_inc(sem("D_in"), 16)
            sp.dma_start(maskL[:, :], ins["maskL"]).then_inc(sem("D_in"), 16)
            route_sp(sp)
            sp.wait_ge(sem("x_new"), NT + done("D", "x_new"))
            load("G")
            load("H")
            sp.dma_start(esel, ins["esel"]).then_inc(sem("H_in"), 16)
            for k in ("w1", "w3", "w2"):
                sp.dma_start(MB[k], ins[k]).then_inc(sem("H_in"), 16)
            load_bias(sp)
            moe_sp(sp)

        @block.gpsimd
        def _(pool):
            ffn_setup_pool(pool)
            route_pool(pool)
            sim_pool(pool)

        @block.scalar
        def _(act):
            act.wait_ge(sem("const_in"), 96)
            nc.scalar.activation(gates[:, :], gates[:, :], ACT.Tanh).then_inc(sem("gates_ready"), 1)
            norm_act(act, "A")
            heads16_act(act, "A")
            norm_act(act, "B")
            ffn_act(act)
            norm_act(act, "C")
            local_act(act)
            norm_act(act, "Dx")
            norm_act(act, "Dh")
            light_act(act)
            route_act(act)
            heavy_act(act)
            norm_act(act, "E")
            sim_act(act)
            norm_act(act, "F")
            rnn_act(act)
            norm_act(act, "G")
            heads16_act(act, "G")
            norm_act(act, "H")
            moe_act(act)

        @block.tensor
        def _(pe):
            heads16_pe(pe, "A")
            ffn_pe(pe)
            local_pe(pe)
            light_pe(pe)
            route_pe(pe)
            heavy_pe(pe)
            sim_pe(pe)
            rnn_pe(pe)
            pe.wait_ge(sem("x_new"), NT + done("F", "x_new"))
            heads16_pe(pe, "G")
            moe_pe(pe)

        @block.vector
        def _(dve):
            nonlocal chain_dve
            chain_dve = Chain(dve, sem("dve_chain"))
            dve.wait_ge(sem("x_in"), 16)
            with dve.Fori(0, NT // 4) as i:
                for j in range(4):
                    nc.vector.bn_stats(stats[:, i * 4 + j, :], x[:, i * 4 + j, :]).then_inc(sem("x_stats"), 1)
            dve.wait_ge(sem("x_stats"), NT)
            dve.wait_ge(sem("gates_ready"), 1)
            norm_dve(dve, "A")
            heads16_dve(dve, "A")
            dve.wait_ge(sem("x_new"), NT + done("A", "x_new"))
            ffn_setup_dve(dve)
            norm_dve(dve, "B")
            ffn_dve(dve)
            dve.wait_ge(sem("x_new"), NT + done("B", "x_new"))
            norm_dve(dve, "C")
            local_dve(dve)
            dve.wait_ge(sem("x_new"), NT + done("C", "x_new"))
            norm_dve(dve, "Dx")
            light_dve(dve)
            dve.wait_ge(sem("D_x_light"), NT)
            route_dve(dve)
            heavy_dve(dve)
            dve.wait_ge(sem("x_new"), NT + done("D", "x_new"))
            sim_dve(dve)
            dve.wait_ge(sem("x_new"), NT + done("E", "x_new"))
            rnn_dve(dve)
            dve.wait_ge(sem("x_new"), NT + done("F", "x_new"))
            norm_dve(dve, "G")
            heads16_dve(dve, "G")
            dve.wait_ge(sem("x_new"), NT + done("G", "x_new"))
            norm_dve(dve, "H")
            moe_dve(dve)


def chunked(w):
    k = w.shape[0] // P
    return w.reshape(k, P, -1).transpose(1, 0, 2).reshape(P, -1)


def kernel(**inputs):
    import ml_dtypes

    import concourse.bacc as bacc
    from concourse.bass_utils import run_bass_kernel_spmd

    v = {k: np.asarray(a) for k, a in inputs.items()}
    a, f = "L0_xattn_", "L0_ffn_"
    packs = {
        "const": [np.eye(P, dtype=np.float32), np.kron(np.eye(HPC), np.ones((HD16, 1))).astype(np.float32),
                  np.ones((P, P), np.float32), np.triu(np.ones((P, P), np.float32), 1),
                  np.broadcast_to(np.arange(NKV, dtype=np.float32), (P, NKV))],
        "pack_A": [chunked(v[a + "Wq"].T), chunked(v[a + "Wk"].T), chunked(v[a + "Wv"].T), chunked(v[a + "Wp"].T),
                   chunked(v[a + "bq"][:, None]), chunked(v[a + "bk"][:, None])],
        "pack_B": [chunked(v[f + "W_fc"].T), chunked(v[f + "W_proj"].T), chunked(v[f + "b_fc"][:, None])],
        "pack_lora": [v[f + "A_fc"], v[f + "B_fc"].T, v[f + "A_proj"], v[f + "B_proj"].T],
        "pack_G": [chunked(v["L3_xattn_" + n + "_w"].T) for n in "qkvo"]
                  + [chunked(v["L3_xattn_" + n + "_b"][:, None]) for n in "qk"],
    }
    wkv = v["L1_ffn_w_kv_h"]
    null_k = np.zeros((HDH, H8), np.float32)
    for h in range(H8):
        null_k[h * DH:(h + 1) * DH, h] = v["L1_ffn_null_kv"][0, h]
    packs |= {
        "pack_C": [chunked(v["L1_xattn_W_p"].T), chunked(v["L1_xattn_W_a"]),
                   np.concatenate([v["L1_xattn_V_p"][0], np.zeros(P - PSZ, np.float32)])[:, None],
                   np.broadcast_to(np.arange(SC, dtype=np.float32), (P, SC)),
                   np.broadcast_to(np.arange(WIN, dtype=np.float32) - 2, (P, WIN))],
        "pack_D": [chunked(v["L1_ffn_w_qkv_l"]), chunked(v["L1_ffn_w_out_l"]), chunked(v["L1_ffn_w_q_h"]),
                   chunked(wkv[:, :, :DH].reshape(D, HDH)), chunked(wkv[:, :, DH:].reshape(D, HDH)),
                   chunked(v["L1_ffn_w_out_h"]), chunked(v["L1_ffn_ln_g"][:, None]), chunked(v["L1_ffn_ln_b"][:, None]),
                   chunked(v["L1_ffn_rms_g"][:, None]), chunked(null_k)],
        "pack_E": [chunked(v["L2_xattn_W_qv"])] + [chunked(w[:, None]) for w in np.split(v["L2_xattn_w_sim"], 3)],
        "pack_F": [chunked(v["L2_ffn_" + n].T) for n in ("wf", "wi", "wc", "wo", "uf", "ui", "uc", "uo")]
                  + [chunked(v["L2_ffn_" + n][:, None]) for n in ("bf", "bi", "bc", "in_c")],
        "pack_H": [chunked(v["L3_ffn_gate_w"].T)],
    }
    rows = {
        "rows_D": [v["L1_ffn_rt_q"][0], v["L1_ffn_rt_kv"][0], v["L1_ffn_null_q"], v["L1_ffn_null_kv"][1].reshape(-1)],
        "rows_E": [v["L2_xattn_b_qv"], v["L2_xattn_b_sim"]],
        "rows_F": [v["L2_ffn_bo"]],
        "rows_A": [v[a + "bv"], v[a + "bp"]],
        "rows_B": [v[f + "b_proj"]],
        "rows_G": [v["L3_xattn_v_b"], v["L3_xattn_o_b"]],
    }
    arrays = {k: np.concatenate(p, axis=1) for k, p in packs.items()}
    arrays |= {k: np.concatenate(p) for k, p in rows.items()}
    ctx = v["ctx_1024"]
    masked = np.zeros((B, HT, 2 * P), bool)
    masked[0, :, 3 * WINDOW:] = masked[1, :, :WINDOW] = masked[:, 0, :WINDOW] = masked[:, -1, 3 * WINDOW:] = True
    experts = lambda w: w.reshape(NE, DC, P, INTER).transpose(2, 0, 1, 3)
    arrays |= {
        "x": v["x"], "gates": np.concatenate([v["g_xattn"], v["g_ffn"]]), "ctx": ctx,
        "ctxT": ctx.transpose(2, 0, 1).reshape(DC, P, B * SC).transpose(1, 0, 2),
        "mask": v["mask_BxS2_bk0"], "maskT": v["mask_BxS2_bk0"].T,
        "fside": v["fside_1x16xSxS2_0"],
        "maskR": np.where(masked, NEG, 0.0).astype(ml_dtypes.bfloat16),
        "maskL": np.kron(np.eye(B), np.ones((1, WINDOW))).astype(ml_dtypes.bfloat16),
        "esel": np.tile(np.kron(np.eye(NE), np.ones((1, P))), (3, 1)).astype(ml_dtypes.bfloat16).reshape(3 * NE, NE, P),
        "w1": experts(v["L3_ffn_w1"]), "w3": experts(v["L3_ffn_w3"]), "w2": v["L3_ffn_w2"].transpose(1, 0, 2),
    }
    nc = bacc.Bacc("TRN2", target_bir_lowering=False, num_devices=1)
    arrays = {f"in_{k}": np.ascontiguousarray(a) for k, a in arrays.items()}
    ins = {k[3:]: nc.dram_tensor(k, a.shape, mybir.dt.from_np(a.dtype), kind="ExternalInput").ap()
           for k, a in arrays.items()}
    out = nc.dram_tensor("out", (B, S, D), F32, kind="ExternalOutput").ap()
    build(nc, ins, out)
    return run_bass_kernel_spmd(nc, [arrays], core_ids=[0]).results[0]["out"]
```
